# Optimizing a Trainium2 kernel written in Bass

```python
import numpy as np
import jax
import jax.numpy as jnp

def _softmax(x, axis=-1):
    return jax.nn.softmax(x, axis=axis)

def _gelu(x):
    return jax.nn.gelu(x, approximate=True)

def _silu(x):
    return jax.nn.silu(x)

def _sigmoid(x):
    return jax.nn.sigmoid(x)

def _layernorm(x, axis=-1, eps=1e-05):
    m = jnp.mean(x, axis=axis, keepdims=True)
    v = jnp.var(x, axis=axis, keepdims=True)
    return (x - m) / jnp.sqrt(v + eps)

def _scatter_add(tgt, idx, src, axis=0):
    return tgt.at[idx].add(src)

def _segment_sum(src, seg, n):
    return jax.ops.segment_sum(src, seg, n)
kernel_name = 'mk_early_fusion_d1_tok_img768_r4_2a2ab4'

def setup_inputs(seed: int=0):
    np.random.seed(seed)
    _w = jnp.asarray

    def _rec_inputs():
        import jax
        import jax.numpy as jnp
        _rk = jax.random.key(seed)
        x = -0.00016672 + 0.999947 * jax.random.normal(jax.random.fold_in(_rk, 1), (32, 3, 96, 96), jnp.float32)
        txt = -0.0020558 + 1.41328 * jax.random.normal(jax.random.fold_in(_rk, 2), (32, 128, 192), jnp.float32)
        return (x, txt)
    x, txt = _rec_inputs()

    def _L0_tok_setup():
        import jax, jax.numpy as jnp
        import numpy as np
        B, C, H, W = (64, 3, 96, 96)
        P = 16
        NH, NW = (H // P, W // P)
        N = NH * NW
        PATCH_DIM = C * P * P
        DIM = 192

        def _layernorm(x, g, b, eps=1e-05):
            mu = jnp.mean(x, axis=-1, keepdims=True)
            var = jnp.var(x, axis=-1, keepdims=True)
            return (x - mu) * jax.lax.rsqrt(var + eps) * g + b
        key = jax.random.key(seed)
        ks = jax.random.split(key, 8)
        img = jax.random.normal(ks[0], (B, C, H, W), dtype=jnp.float32)
        ln1_g = jnp.ones((PATCH_DIM,), jnp.float32)
        ln1_b = jnp.zeros((PATCH_DIM,), jnp.float32)
        W_lin = jax.random.normal(ks[1], (PATCH_DIM, DIM), jnp.float32) / np.sqrt(PATCH_DIM)
        b_lin = jnp.zeros((DIM,), jnp.float32)
        ln2_g = jnp.ones((DIM,), jnp.float32)
        ln2_b = jnp.zeros((DIM,), jnp.float32)
        pos_embedding = jax.random.normal(ks[2], (1, N + 1, DIM), jnp.float32)
        cls_token = jax.random.normal(ks[3], (1, 1, DIM), jnp.float32)
        return {'img': img, 'ln1_g': ln1_g, 'ln1_b': ln1_b, 'W_lin': W_lin, 'b_lin': b_lin, 'ln2_g': ln2_g, 'ln2_b': ln2_b, 'pos_embedding': pos_embedding, 'cls_token': cls_token}
    _L0_tok_all = _L0_tok_setup()
    _L0_tok_in = {k: v for k, v in _L0_tok_all.items() if k in ('ln1_g', 'ln1_b', 'W_lin', 'b_lin', 'ln2_g', 'ln2_b', 'pos_embedding', 'cls_token')}
    del _L0_tok_all

    def _L0_attn_setup():
        import jax, jax.numpy as jnp
        import numpy as np
        import math
        B, S, D = (4, 1024, 192)
        key = jax.random.key(seed)
        ks = jax.random.split(key, 7)
        sc = 0.02
        return {'x': jax.random.normal(ks[0], (B, S, D), dtype=jnp.float32), 'Wq': jax.random.normal(ks[1], (D, D), dtype=jnp.float32) * sc, 'bq': jax.random.normal(ks[2], (D,), dtype=jnp.float32) * sc, 'Wk': jax.random.normal(ks[3], (D, D), dtype=jnp.float32) * sc, 'bk': jax.random.normal(ks[4], (D,), dtype=jnp.float32) * sc, 'Wv': jax.random.normal(ks[5], (D, D), dtype=jnp.float32) * sc, 'bv': jax.random.normal(ks[6], (D,), dtype=jnp.float32) * sc}
    _L0_attn_all = _L0_attn_setup()
    _L0_attn_in = {k: v for k, v in _L0_attn_all.items() if k in ('Wq', 'bq', 'Wk', 'bk', 'Wv', 'bv')}
    del _L0_attn_all

    def _L0_ffn_setup():
        import jax, jax.numpy as jnp
        import numpy as np
        E = 192
        H = 12
        D = E // H
        HID = 768
        NEXP = 4
        TOPK = 2
        EPS = 1e-05

        def _ln(x, g, b):
            m = jnp.mean(x, axis=-1, keepdims=True)
            v = jnp.mean(jnp.square(x - m), axis=-1, keepdims=True)
            return (x - m) * jax.lax.rsqrt(v + EPS) * g + b
        key = jax.random.key(seed)
        ks = jax.random.split(key, 10)
        s = 0.02
        return {'x': jax.random.normal(ks[0], (8, 256, E), jnp.float32), 'ln1_g': jnp.ones((E,), jnp.float32), 'ln1_b': jnp.zeros((E,), jnp.float32), 'in_w': jax.random.normal(ks[1], (3 * E, E), jnp.float32) * s, 'in_b': jnp.zeros((3 * E,), jnp.float32), 'out_w': jax.random.normal(ks[2], (E, E), jnp.float32) * s, 'out_b': jnp.zeros((E,), jnp.float32), 'mlp_w1': jax.random.normal(ks[3], (E, HID), jnp.float32) * s, 'mlp_b1': jnp.zeros((HID,), jnp.float32), 'mlp_w2': jax.random.normal(ks[4], (HID, E), jnp.float32) * s, 'mlp_b2': jnp.zeros((E,), jnp.float32), 'ln2_g': jnp.ones((E,), jnp.float32), 'ln2_b': jnp.zeros((E,), jnp.float32), 'gate_w': jax.random.normal(ks[5], (NEXP, E), jnp.float32) * s, 'gate_b': jnp.zeros((NEXP,), jnp.float32), 'exp_w1': jax.random.normal(ks[6], (NEXP, E, HID), jnp.float32) * s, 'exp_b1': jnp.zeros((NEXP, HID), jnp.float32), 'exp_w2': jax.random.normal(ks[7], (NEXP, HID, E), jnp.float32) * s, 'exp_b2': jnp.zeros((NEXP, E), jnp.float32)}
    _L0_ffn_all = _L0_ffn_setup()
    _L0_ffn_in = {k: v for k, v in _L0_ffn_all.items() if k in ('ln1_g', 'ln1_b', 'in_w', 'in_b', 'out_w', 'out_b', 'mlp_w1', 'mlp_b1', 'mlp_w2', 'mlp_b2', 'ln2_g', 'ln2_b', 'gate_w', 'gate_b', 'exp_w1', 'exp_b1', 'exp_w2', 'exp_b2')}
    del _L0_ffn_all
    return {'x': x, 'txt': txt, 'L0_tok_ln1_g': _L0_tok_in['ln1_g'], 'L0_tok_ln1_b': _L0_tok_in['ln1_b'], 'L0_tok_W_lin': _L0_tok_in['W_lin'], 'L0_tok_b_lin': _L0_tok_in['b_lin'], 'L0_tok_ln2_g': _L0_tok_in['ln2_g'], 'L0_tok_ln2_b': _L0_tok_in['ln2_b'], 'L0_tok_pos_embedding': _L0_tok_in['pos_embedding'], 'L0_tok_cls_token': _L0_tok_in['cls_token'], 'L0_attn_Wq': _L0_attn_in['Wq'], 'L0_attn_bq': _L0_attn_in['bq'], 'L0_attn_Wk': _L0_attn_in['Wk'], 'L0_attn_bk': _L0_attn_in['bk'], 'L0_attn_Wv': _L0_attn_in['Wv'], 'L0_attn_bv': _L0_attn_in['bv'], 'L0_ffn_ln1_g': _L0_ffn_in['ln1_g'], 'L0_ffn_ln1_b': _L0_ffn_in['ln1_b'], 'L0_ffn_in_w': _L0_ffn_in['in_w'], 'L0_ffn_in_b': _L0_ffn_in['in_b'], 'L0_ffn_out_w': _L0_ffn_in['out_w'], 'L0_ffn_out_b': _L0_ffn_in['out_b'], 'L0_ffn_mlp_w1': _L0_ffn_in['mlp_w1'], 'L0_ffn_mlp_b1': _L0_ffn_in['mlp_b1'], 'L0_ffn_mlp_w2': _L0_ffn_in['mlp_w2'], 'L0_ffn_mlp_b2': _L0_ffn_in['mlp_b2'], 'L0_ffn_ln2_g': _L0_ffn_in['ln2_g'], 'L0_ffn_ln2_b': _L0_ffn_in['ln2_b'], 'L0_ffn_gate_w': _L0_ffn_in['gate_w'], 'L0_ffn_gate_b': _L0_ffn_in['gate_b'], 'L0_ffn_exp_w1': _L0_ffn_in['exp_w1'], 'L0_ffn_exp_b1': _L0_ffn_in['exp_b1'], 'L0_ffn_exp_w2': _L0_ffn_in['exp_w2'], 'L0_ffn_exp_b2': _L0_ffn_in['exp_b2']}

def reference(x, txt, L0_tok_ln1_g, L0_tok_ln1_b, L0_tok_W_lin, L0_tok_b_lin, L0_tok_ln2_g, L0_tok_ln2_b, L0_tok_pos_embedding, L0_tok_cls_token, L0_attn_Wq, L0_attn_bq, L0_attn_Wk, L0_attn_bk, L0_attn_Wv, L0_attn_bv, L0_ffn_ln1_g, L0_ffn_ln1_b, L0_ffn_in_w, L0_ffn_in_b, L0_ffn_out_w, L0_ffn_out_b, L0_ffn_mlp_w1, L0_ffn_mlp_b1, L0_ffn_mlp_w2, L0_ffn_mlp_b2, L0_ffn_ln2_g, L0_ffn_ln2_b, L0_ffn_gate_w, L0_ffn_gate_b, L0_ffn_exp_w1, L0_ffn_exp_b1, L0_ffn_exp_w2, L0_ffn_exp_b2):
    import jax
    import jax.numpy as jnp

    def _L0_tok_ref(img, ln1_g, ln1_b, W_lin, b_lin, ln2_g, ln2_b, pos_embedding, cls_token):
        import jax, jax.numpy as jnp
        import numpy as np
        B, C, H, W = (64, 3, 96, 96)
        P = 16
        NH, NW = (H // P, W // P)
        N = NH * NW
        PATCH_DIM = C * P * P
        DIM = 192

        def _layernorm(x, g, b, eps=1e-05):
            mu = jnp.mean(x, axis=-1, keepdims=True)
            var = jnp.var(x, axis=-1, keepdims=True)
            return (x - mu) * jax.lax.rsqrt(var + eps) * g + b
        b = img.shape[0]
        x = img.reshape(b, C, NH, P, NW, P)
        x = jnp.transpose(x, (0, 2, 4, 3, 5, 1))
        x = x.reshape(b, N, PATCH_DIM)
        x = _layernorm(x, ln1_g, ln1_b)
        x = jnp.einsum('bnp,pd->bnd', x, W_lin) + b_lin
        x = _layernorm(x, ln2_g, ln2_b)
        cls = jnp.broadcast_to(cls_token, (b, 1, DIM))
        x = jnp.concatenate([cls, x], axis=1)
        x = x + pos_embedding[:, :N + 1]
        return x

    def _L0_attn_ref(x, Wq, bq, Wk, bk, Wv, bv):
        import jax, jax.numpy as jnp
        import numpy as np
        import math
        B, S, D = (4, 1024, 192)
        q = jnp.einsum('bsd,ed->bse', x, Wq) + bq
        k = jnp.einsum('bsd,ed->bse', x, Wk) + bk
        v = jnp.einsum('bsd,ed->bse', x, Wv) + bv
        scale = 1.0 / math.sqrt(x.shape[-1])
        scores = jnp.einsum('bsd,btd->bst', q, k) * scale
        return jnp.einsum('bst,btd->bsd', scores, v)

    def _L0_ffn_ref(x, ln1_g, ln1_b, in_w, in_b, out_w, out_b, mlp_w1, mlp_b1, mlp_w2, mlp_b2, ln2_g, ln2_b, gate_w, gate_b, exp_w1, exp_b1, exp_w2, exp_b2):
        import jax, jax.numpy as jnp
        import numpy as np
        E = 192
        H = 12
        D = E // H
        HID = 768
        NEXP = 4
        TOPK = 2
        EPS = 1e-05

        def _ln(x, g, b):
            m = jnp.mean(x, axis=-1, keepdims=True)
            v = jnp.mean(jnp.square(x - m), axis=-1, keepdims=True)
            return (x - m) * jax.lax.rsqrt(v + EPS) * g + b
        B, N, _ = x.shape
        h = _ln(x, ln1_g, ln1_b)
        qkv = h @ in_w.T + in_b
        q, k, v = jnp.split(qkv, 3, axis=-1)
        q = q.reshape(B, N, H, D)
        k = k.reshape(B, N, H, D)
        v = v.reshape(B, N, H, D)
        scores = jnp.einsum('bqhd,bkhd->bhqk', q, k) / jnp.sqrt(jnp.float32(D))
        attn = jax.nn.softmax(scores, axis=-1)
        ctx = jnp.einsum('bhqk,bkhd->bqhd', attn, v).reshape(B, N, E)
        x = x + ctx @ out_w.T + out_b
        x = x + jax.nn.gelu(x @ mlp_w1 + mlp_b1, approximate=False) @ mlp_w2 + mlp_b2
        xm = _ln(x, ln2_g, ln2_b)
        logits = xm @ gate_w.T + gate_b
        topv, topi = jax.lax.top_k(logits, TOPK)
        gates = jax.nn.softmax(topv, axis=-1)
        onehot = jax.nn.one_hot(topi, NEXP, dtype=x.dtype)
        comb = jnp.einsum('bnk,bnke->bne', gates, onehot)
        moe_out = jnp.zeros_like(x)
        for e in range(NEXP):
            he = jax.nn.gelu(xm @ exp_w1[e] + exp_b1[e], approximate=False)
            oe = he @ exp_w2[e] + exp_b2[e]
            moe_out = moe_out + comb[..., e:e + 1] * oe
        return x + moe_out
    h = _L0_tok_ref(x, L0_tok_ln1_g, L0_tok_ln1_b, L0_tok_W_lin, L0_tok_b_lin, L0_tok_ln2_g, L0_tok_ln2_b, L0_tok_pos_embedding, L0_tok_cls_token)
    h = jnp.concatenate([h, txt], axis=1)
    h = h + _L0_attn_ref(_layernorm(h, axis=-1), L0_attn_Wq, L0_attn_bq, L0_attn_Wk, L0_attn_bk, L0_attn_Wv, L0_attn_bv)
    h = h + _L0_ffn_ref(_layernorm(h, axis=-1), L0_ffn_ln1_g, L0_ffn_ln1_b, L0_ffn_in_w, L0_ffn_in_b, L0_ffn_out_w, L0_ffn_out_b, L0_ffn_mlp_w1, L0_ffn_mlp_b1, L0_ffn_mlp_w2, L0_ffn_mlp_b2, L0_ffn_ln2_g, L0_ffn_ln2_b, L0_ffn_gate_w, L0_ffn_gate_b, L0_ffn_exp_w1, L0_ffn_exp_b1, L0_ffn_exp_w2, L0_ffn_exp_b2)
    return h

_drawn_inputs = setup_inputs


def setup_inputs(seed=0):
    import zlib

    import numpy as np

    out = dict(_drawn_inputs(seed))
    spreads = {'L0_tok_ln1_g': (1.0, 0.2),
     'L0_tok_ln1_b': (0.0, 0.269),
     'L0_tok_b_lin': (0.0, 0.1),
     'L0_tok_ln2_g': (1.0, 0.2),
     'L0_tok_ln2_b': (0.0, 0.1),
     'L0_ffn_ln1_g': (1.0, 0.6),
     'L0_ffn_ln1_b': (0.0, 0.8),
     'L0_ffn_in_b': (0.0, 0.682),
     'L0_ffn_out_b': (0.0, 0.445),
     'L0_ffn_mlp_b1': (0.0, 0.549),
     'L0_ffn_mlp_b2': (0.0, 0.398),
     'L0_ffn_ln2_g': (1.0, 0.6),
     'L0_ffn_ln2_b': (0.0, 0.8),
     'L0_ffn_gate_b': (0.0, 0.412),
     'L0_ffn_exp_b1': (0.0, 0.8),
     'L0_ffn_exp_b2': (0.0, 0.289)}
    factors = {'L0_attn_bq': 2.724,
     'L0_attn_bk': 2.902,
     'L0_attn_bv': 2.884,
     'L0_ffn_in_w': 8.0,
     'L0_ffn_out_w': 4.411,
     'L0_ffn_exp_w1': 2.723}
    for name, (base, spread) in spreads.items():
        noise = np.random.default_rng([zlib.crc32(name.encode()), seed]).standard_normal(out[name].shape)
        drawn = base * np.exp(spread * noise) if base else spread * noise
        out[name] = jnp.asarray(drawn.astype(out[name].dtype))
    for name, factor in factors.items():
        out[name] = (out[name] * factor).astype(out[name].dtype)
    return out
```

```python
from contextlib import ExitStack

import numpy as np

import concourse.bass as bass
from concourse import mybir

F32 = mybir.dt.float32
F32R = mybir.dt.float32r
ALU = mybir.AluOpType
ACT = mybir.ActivationFunctionType
AX_X = mybir.AxisListType.X

P = 128
B = 32
NPATCH = 36
NIMG = NPATCH + 1
NTXT = 128
S = NIMG + NTXT
D = 192
DA = D + 1
PD = 768
HID = 768
NH = 12
HD = D // NH
NE = 4
NF = NE + 1
PAIRS = B // 2
KP = PD // P
KH = HID // P
KD = (128, 64)
KA = (128, 65)
EPS = 1e-5
TB = 120
TG = 4
GT = TB * TG
GROUPS = B * S // GT
assert GROUPS * GT == B * S
HEAD_SCALE = float(HD) ** -0.5


class Steps:

    def __init__(self, sem, eng):
        self.sem, self.eng, self.base, self.k = sem, eng, 0, 0

    def at(self, base):
        self.base, self.k = base, 0

    def link(self, ins):
        self.k += 1
        ins.then_inc(self.sem, 1)
        self.eng.wait_ge(self.sem, self.base + self.k)

    def link_aggregate(self, ins, pad):
        self.link(ins)
        self.eng.memset(pad, 0.0)


def build_program(nc, a, out):
    ctx = ExitStack()

    def sem(name):
        return ctx.enter_context(nc.semaphore(name))

    def sb(stack, name, shape, dt=F32):
        return stack.enter_context(nc.sbuf_tensor(name, shape, dt))

    h1d = nc.dram_tensor("h1_scratch", [B, S, D], F32, kind="Internal").ap()
    x1d = nc.dram_tensor("x1_scratch", [B, S, D], F32, kind="Internal").ap()

    PS = ctx.enter_context(nc.psum_tensor("PS", [P, 8, 512], F32))
    ident = sb(ctx, "ident", [P, P])
    eps_half = sb(ctx, "minus_half", [P, 8])

    pad = sb(ctx, "pad", [P, 1])

    one = ExitStack()
    wlin = sb(one, "wlin", [P, KP, D])
    lnp_g = sb(one, "lnp_g", [P, KP])
    lnp_b = sb(one, "lnp_b", [P, KP])
    lnp_rep = sb(one, "lnp_rep", [P, KP, P])
    lin_bias = sb(one, "lin_bias", [P, D])
    g2m = sb(one, "g2m", [P, D])
    b2m = sb(one, "b2m", [P, D])
    clsb = sb(one, "clsb", [P, D])
    wqa = sb(one, "wqa", [P, 2, DA])
    wka = sb(one, "wka", [P, 2, DA])
    AT = sb(one, "AT", [P, 2, DA])
    wva = sb(one, "wva", [P, 2, D])
    fg = sb(one, "fg", [P, 2])
    fb = sb(one, "fb", [P, 2])
    fb_rep = sb(one, "fb_rep", [P, 2, P])
    wqk = sb(one, "wqk", [P, 2, 6, NH // 3, 32])
    wv = sb(one, "wv", [P, 2, D])
    qkb = sb(one, "qkb", [P, 6])
    vb = sb(one, "vb", [P, D])
    vbT = sb(one, "vbT", [P, 2, P])
    ow = sb(one, "ow", [P, 2, D])
    ob = sb(one, "ob", [P, D])
    XP = sb(one, "XP", [P, PD])
    XN = sb(one, "XN", [P, PD])
    XNT = sb(one, "XNT", [P, KP, P])
    Y = sb(one, "Y", [P, D])
    Y2 = sb(one, "Y2", [P, D])
    H = sb(one, "H", [P, 3, D])
    XA = sb(one, "XA", [P, 3, DA])
    XAT = sb(one, "XAT", [P, 2, 2, D])
    GS = sb(one, "GS", [P, 2, 2, DA])
    T1 = sb(one, "T1", [P, 2, 2, D])
    PM = sb(one, "PM", [P, 2, 2, D])
    H1 = sb(one, "H1", [P, 3, D])
    U = sb(one, "U", [P, 3, D])
    UB = sb(one, "UB", [P, 3, D])
    Z = sb(one, "Z", [P, 3, D])
    ZT = sb(one, "ZT", [P, 2, 2, D])
    QK = sb(one, "QK", [P, 6, 2, D])
    VX = sb(one, "VX", [P, 2, 2, NH, 32])
    PX = sb(one, "PX", [P, 2, 6, S])
    PT = sb(one, "PT", [P, 2, NH, 2, D])
    CT = sb(one, "CT", [P, 3, 3 * P])
    rec = sb(one, "rec", [P, 3, NH])
    CN = sb(one, "CN", [P, 3, D])
    CNT = sb(one, "CNT", [P, 2, 3 * P])
    X1 = sb(one, "X1", [P, 3, D])
    st = sb(one, "st", [P, 5, 3, 6])
    mv = sb(one, "mv", [P, 5, 3, 2])
    ve = sb(one, "ve", [P, 5, 3])
    rs = sb(one, "rs", [P, 5, 3])
    mx = sb(one, "mx", [P, 6, 6])
    nb = sb(one, "nb", [P, 6, 6])
    one.close()

    two = ctx
    w1r = sb(two, "w1r", [P, NF, 4, HID], F32R)
    w2r = sb(two, "w2r", [P, NF, KH, 2 * D], F32R)
    b2r = sb(two, "b2r", [33, NF, D], F32R)
    ones33 = sb(two, "ones33", [33, TB], F32R)
    onesf = sb(two, "onesf", [33, TB])
    b1c = sb(two, "b1c", [P, NF, KH])
    g2c = sb(two, "g2c", [P, 2])
    b2c = sb(two, "b2c", [P, 2])
    b2rep = sb(two, "b2rep", [P, 2, P])
    gwr = sb(two, "gwr", [P, 4, NE], F32R)
    gbb = sb(two, "gbb", [P, NE])
    tri = sb(two, "tri", [P, NE, NE])
    raw = ExitStack()
    rw1 = sb(raw, "rw1", [P, 2, 2, HID])
    rw2 = sb(raw, "rw2", [P, 2, KH, D])
    rb2 = sb(raw, "rb2", [1, NF, D])
    gwf = sb(raw, "gwf", [P, 2, NE])
    raw.close()
    X = sb(two, "X", [TB, TG, D])
    HH = sb(two, "HH", [TB, TG, D])
    ACC = sb(two, "ACC", [TB, TG, D])
    X2 = sb(two, "X2", [TB, TG, D])
    Z2 = sb(two, "Z2", [TB, TG, D])
    XH = sb(two, "XH", [P, GT], F32R)
    XL = sb(two, "XL", [P, GT], F32R)
    XS = sb(two, "XS", [P, GT], F32R)
    GF = sb(two, "GF", [P, 3, GT])
    GH = sb(two, "GH", [P, 2, KH, GT], F32R)
    GL = sb(two, "GL", [P, 2, KH, GT], F32R)
    st2 = sb(two, "st2", [TB, TG, 6])
    mv2 = sb(two, "mv2", [TB, TG, 2])
    ve2 = sb(two, "ve2", [TB, TG])
    rs2 = sb(two, "rs2", [TB, TG])
    lg = sb(two, "lg", [TB, TG, NE])
    gtm = sb(two, "gtm", [TB, TG, NE, NE])
    eqm = sb(two, "eqm", [TB, TG, NE, NE])
    rank = sb(two, "rank", [TB, TG, NE])
    top = sb(two, "top", [TB, TG])
    ldf = sb(two, "ldf", [TB, TG, NE])
    lex = sb(two, "lex", [TB, TG, NE])
    gex = sb(two, "gex", [TB, TG, NE])
    den = sb(two, "den", [TB, TG])
    comb = sb(two, "comb", [TB, TG, NE])

    const_in = sem("const_in")
    ident_ready = sem("ident_ready")
    zeroed = sem("zeroed")
    setup_ps = sem("setup_ps")
    setup_dve = sem("setup_dve")
    setup_act = sem("setup_act")
    attn_const_ready = sem("attn_const_ready")
    patches_in = sem("patches_in")
    txt_in = sem("txt_in")
    dve_step = sem("dve_step")
    pool_step = sem("pool_step")
    var_ready = sem("var_ready")
    rstd_ready = sem("rstd_ready")
    xn_ready = sem("xn_ready")
    xnT_ps = sem("xnT_ps")
    xnT_ready = sem("xnT_ready")
    tok_ps = sem("tok_ps")
    xa_ready = sem("xa_ready")
    xaT_ps = sem("xaT_ps")
    xaT_ready = sem("xaT_ready")
    lin_mat_ps = sem("lin_mat_ps")
    lin_mat_ready = sem("lin_mat_ready")
    lin_ps = sem("lin_ps")
    h1_ready = sem("h1_ready")
    h1_stored = sem("h1_stored")
    u_ready = sem("u_ready")
    ub_ready = sem("ub_ready")
    z_ready = sem("z_ready")
    zT_ps = sem("zT_ps")
    zT_ready = sem("zT_ready")
    qk_ps = sem("qk_ps")
    qk_ready = sem("qk_ready")
    v_ps = sem("v_ps")
    v_ready = sem("v_ready")
    score_ps = sem("score_ps")
    max_ready = sem("max_ready")
    prob_ready = sem("prob_ready")
    probT_ps = sem("probT_ps")
    probT_txt_ready = sem("probT_txt_ready")
    probT_img_ready = sem("probT_img_ready")
    ctxT_ps = sem("ctxT_ps")
    ctxT_ready = sem("ctxT_ready")
    ctx_ps = sem("ctx_ps")
    ctx_ready = sem("ctx_ready")
    cnT_ps = sem("cnT_ps")
    cnT_ready = sem("cnT_ready")
    proj_ps = sem("proj_ps")
    x1_ready = sem("x1_ready")
    x1_stored = sem("x1_stored")
    phase_done = sem("phase_done")
    raw_in = [sem("raw_in0"), sem("raw_in1")]
    vec_in = sem("vec_in")
    bias_ps = sem("bias_ps")
    bias_ready = sem("bias_ready")
    hi_ready = sem("hi_ready")
    lo_ready = sem("lo_ready")
    x_in = sem("x_in")
    actT_ps = sem("actT_ps")
    actT_hi = sem("actT_hi")
    actT_ready = sem("actT_ready")
    gate_ps = sem("gate_ps")
    ldiff_ready = sem("ldiff_ready")
    lexp_ready = sem("lexp_ready")
    up_ps = sem("up_ps")
    gelu_ready = sem("gelu_ready")
    hid_ready = sem("hid_ready")
    down_ps = sem("down_ps")
    down_read = sem("down_read")
    var2_ready = sem("var2_ready")
    rstd2_ready = sem("rstd2_ready")
    z2_ready = sem("z2_ready")
    acc_init = sem("acc_init")
    out_ready = sem("out_ready")
    out_stored = sem("out_stored")

    block = ctx.enter_context(nc.Block())
    NCONST = 49
    NVEC = 14

    def bc(ap, n):
        return ap.rearrange("(o d) -> o d", o=1).to_broadcast([n, ap.shape[-1]])

    @block.sync
    def _(sp):
        count = [0]

        def const(dst, src):
            sp.dma_start(dst, src).then_inc(const_in, 16)
            count[0] += 1

        sp.wait_ge(zeroed, 6)

        def load_pair(i):
            for b in range(2):
                sp.dma_start(XP[64 * b + 1:64 * b + NIMG, :],
                             a["patches"][bass.ds(2 * i + b, 1)].rearrange("o n d -> (o n) d")).then_inc(patches_in, 16)
            sp.dma_start(H[:, 0:2, :], a["txt"][bass.ds(2 * i, 2)].rearrange("b p d -> p b d")).then_inc(txt_in, 16)

        load_pair(0)
        const(wlin[:, :, :], a["W_lin"].rearrange("(k p) d -> p k d", p=P))
        const(lnp_g[:, :], a["lnp_g"])
        const(lnp_b[:, :], a["lnp_b"])
        const(lin_bias[:, :], bc(a["b_lin"], P))
        for b in range(2):
            const(g2m[64 * b + 1:64 * b + NIMG, :], bc(a["ln2_g"], NPATCH))
            const(b2m[64 * b:64 * b + NIMG, :], a["pos"][0, 0:NIMG, :])
            const(clsb[64 * b + 1:64 * b + NIMG, :], bc(a["ln2_b"], NPATCH))
            const(clsb[64 * b:64 * b + 1, :], a["cls"][0, :, :])
        for w, wname, bname in ((wqa, "Wq", "bq"), (wka, "Wk", "bk")):
            for k in range(2):
                const(w[0:KD[k], k, 0:D], a[wname][P * k:P * k + KD[k], :])
                const(w[0:KD[k], k, D:DA], a[bname][P * k:P * k + KD[k]].rearrange("(p o) -> p o", o=1))
        for k in range(2):
            const(wva[0:KD[k], k, :], a["WvT"][P * k:P * k + KD[k], :])
            const(fg[0:KD[k], k:k + 1], a["f1_g"][P * k:P * k + KD[k]].rearrange("(p o) -> p o", o=1))
            const(fb[0:KD[k], k:k + 1], a["f1_b"][P * k:P * k + KD[k]].rearrange("(p o) -> p o", o=1))
            const(wv[0:KD[k], k, :], a["in_wT"][P * k:P * k + KD[k], 2 * D:3 * D])
            const(ow[0:KD[k], k, :], a["out_wT"][P * k:P * k + KD[k], :])
            for c in range(3):
                for w in range(2):
                    const(wqk[0:KD[k], k, 2 * c + w, :, 0:HD],
                          a["in_wT"][P * k:P * k + KD[k], w * D + 64 * c:w * D + 64 * c + 64]
                          .rearrange("p (j e) -> p j e", e=HD))
        const(wva[64:65, 1, :], a["bv"].rearrange("(o d) -> o d", o=1))
        for j in range(4):
            const(qkb[32 * j:32 * j + HD, :], a["qk_b"][j, :, :])
        const(vb[:, :], bc(a["in_b"][2 * D:3 * D], P))
        const(ob[:, :], bc(a["out_b"], P))
        assert count[0] == NCONST, count

        def store_tile(i, src, dst, done):
            sp.dma_start(dst[bass.ds(2 * i, 2), NIMG:S, :].rearrange("b p d -> p b d"), src[:, 0:2, :]).then_inc(done, 16)
            for b in range(2):
                sp.dma_start(dst[bass.ds(2 * i + b, 1), 0:NIMG, :].rearrange("o n d -> (o n) d"),
                             src[64 * b:64 * b + NIMG, 2, :]).then_inc(done, 16)

        def pair(i, more):
            sp.wait_ge(h1_ready, i + 1)
            store_tile(i, H1, h1d, h1_stored)
            if more:
                load_pair(i + 1)
            sp.wait_ge(x1_ready, i + 1)
            store_tile(i, X1, x1d, x1_stored)

        with sp.Fori(0, PAIRS - 1) as i:
            pair(i, True)
        pair(PAIRS - 1, False)

        nvec = [0]

        def vec(dst, src):
            sp.dma_start(dst, src).then_inc(vec_in, 16)
            nvec[0] += 1

        sp.wait_ge(phase_done, 4)
        sp.wait_ge(h1_stored, PAIRS * 48 + 1)
        sp.wait_ge(x1_stored, PAIRS * 48 + 1)

        def load_raw(f):
            s = raw_in[f % 2]
            w1 = a["mlp_w1"] if f == 0 else a["exp_w1"][f - 1]
            w2 = a["mlp_w2"] if f == 0 else a["exp_w2"][f - 1]
            sp.dma_start(rw1[:, f % 2, 0, :], w1[0:P, :]).then_inc(s, 16)
            for r in range(2):
                sp.dma_start(rw1[64 * r:64 * r + 64, f % 2, 1, :], w1[P:D, :]).then_inc(s, 16)
            sp.dma_start(rw2[:, f % 2, :, :], w2.rearrange("(k p) d -> p k d", p=P)).then_inc(s, 16)

        load_raw(0)
        vec(b1c[:, 0, :], a["mlp_b1"])
        vec(b1c[:, 1:NF, :], a["exp_b1"])
        for g, name in ((g2c, "f2_g"), (b2c, "f2_b")):
            vec(g[:, 0:1], a[name][0:P].rearrange("(p o) -> p o", o=1))
            for r in range(2):
                vec(g[64 * r:64 * r + 64, 1:2], a[name][P:D].rearrange("(p o) -> p o", o=1))
        vec(rb2[0:1, 0, :], a["mlp_b2"].rearrange("(o d) -> o d", o=1))
        vec(rb2[0:1, 1:NF, :], a["exp_b2"].rearrange("(o e) d -> o e d", o=1))
        vec(gwf[:, 0, :], a["gate_wT"][0:P, :])
        for r in range(2):
            vec(gwf[64 * r:64 * r + 64, 1, :], a["gate_wT"][P:D, :])
        vec(gbb[:, :], bc(a["gate_b"], P))
        load_raw(1)
        for f in range(2, NF):
            sp.wait_ge(lo_ready, f - 1)
            sp.wait_ge(bias_ps, f - 1)
            load_raw(f)

        def load_group(n):
            rows = lambda t: t.rearrange("b s d -> (b s) d")[bass.ds(n * GT, GT), :].rearrange("(a p) d -> p a d", p=TB)
            sp.dma_start(X[:, :, :], rows(x1d)).then_inc(x_in, 16)
            sp.dma_start(HH[:, :, :], rows(h1d)).then_inc(x_in, 16)

        def store_group(n):
            sp.dma_start(out.rearrange("b s d -> (b s) d")[bass.ds(n * GT, GT), :].rearrange("(a p) d -> p a d", p=TB),
                         ACC[:, :, :]).then_inc(out_stored, 16)

        sp.wait_ge(lo_ready, NF)
        sp.wait_ge(bias_ready, 2)
        load_group(0)
        with sp.Fori(0, GROUPS - 1) as n:
            sp.wait_ge(acc_init, n + 1)
            load_group(n + 1)
            sp.wait_ge(out_ready, n + 1)
            store_group(n)
        sp.wait_ge(out_ready, GROUPS)
        store_group(GROUPS - 1)
        sp.wait_ge(out_stored, GROUPS * 16 + 1)
        assert nvec[0] == NVEC, nvec

    @block.gpsimd
    def _(pool):
        nc.gpsimd.memset(XP[:, :], 0.0).then_inc(zeroed, 1)
        nc.gpsimd.memset(g2m[:, :], 0.0).then_inc(zeroed, 1)
        nc.gpsimd.memset(b2m[:, :], 0.0).then_inc(zeroed, 1)
        nc.gpsimd.memset(clsb[:, :], 0.0).then_inc(zeroed, 1)
        nc.gpsimd.memset(wqk[:, :, :, :, :], 0.0).then_inc(zeroed, 1)
        nc.gpsimd.memset(qkb[:, :], 0.0).then_inc(zeroed, 1)
        nc.gpsimd.memset(ident[:, :], 0.0).then_inc(ident_ready, 1)
        pool.wait_ge(ident_ready, 1)
        nc.gpsimd.affine_select(out=ident[:, :], in_=ident[:, :], compare_op=ALU.not_equal, fill=1.0, base=0,
                                pattern=[[-1, P]], channel_multiplier=1).then_inc(ident_ready, 1)
        nc.gpsimd.memset(eps_half[:, :], -0.5).then_inc(pool_step, 1)
        nc.gpsimd.memset(XA[:, :, D:DA], 1.0).then_inc(pool_step, 1)
        nc.gpsimd.memset(VX[:, :, :, :, HD:HD + 1], 1.0).then_inc(pool_step, 1)
        nc.gpsimd.memset(VX[:, :, :, :, HD + 1:32], 0.0).then_inc(pool_step, 1)
        pool.wait_ge(pool_step, 4)
        pool.wait_ge(attn_const_ready, 1)

        def rstd(base, k, n):
            pool.wait_ge(var_ready, base + k)
            nc.gpsimd.tensor_tensor(rs[:, k - 1, 0:n], ve[:, k - 1, 0:n], eps_half[:, 0:n], ALU.pow).then_inc(rstd_ready, 1)

        with pool.Fori(0, PAIRS) as i:
            for k, n in ((1, 1), (2, 1), (3, 3), (4, 3)):
                rstd(i * 5, k, n)
            pool.wait_ge(u_ready, i + 1)
            for t in range(3):
                last = nc.gpsimd.tensor_tensor(UB[:, t, :], U[:, t, :], ob[:, :], ALU.add)
                if t == 0:
                    rstd(i * 5, 5, 3)
            last.then_inc(ub_ready, 1)
        pool.wait_ge(x1_ready, PAIRS)
        nc.gpsimd.memset(onesf[:, :], 1.0).then_inc(phase_done, 1)
        nc.gpsimd.memset(tri[:, :, :], 1.0).then_inc(pool_step, 1)
        pool.wait_ge(pool_step, 5)
        nc.gpsimd.affine_select(out=tri[:, :, :], in_=tri[:, :, :], compare_op=ALU.is_gt, fill=0.0, base=0,
                                pattern=[[1, NE], [-1, NE]], channel_multiplier=0).then_inc(pool_step, 1)
        pool.wait_ge(pool_step, 6)
        with pool.Fori(0, GROUPS) as n:
            pool.wait_ge(var2_ready, n + 1)
            nc.gpsimd.tensor_tensor(rs2[:, :], ve2[:, :], eps_half[0:TB, 0:TG], ALU.pow).then_inc(rstd2_ready, 1)
            pool.wait_ge(out_stored, n * 16 + 1)
            nc.gpsimd.tensor_tensor(ACC[:, :, :], X2[:, :, :], HH[:, :, :], ALU.add).then_inc(acc_init, 1)

    @block.scalar
    def _(act):
        def copy(dst, src, scale=1.0):
            return nc.scalar.activation(dst, src, ACT.Copy, scale=scale)

        act.wait_ge(setup_ps, 1)
        copy(AT[:, 0, :], PS[:, 0, 0:DA], float(D) ** -0.5)
        copy(AT[0:65, 1, :], PS[0:65, 0, DA:2 * DA], float(D) ** -0.5).then_inc(setup_act, 1)
        act.wait_ge(setup_ps, 4)
        copy(vbT[:, 0, :], PS[:, 5, 0:P])
        copy(vbT[0:64, 1, :], PS[0:64, 5, P:2 * P]).then_inc(setup_act, 1)

        def transposed(dst, bank, rows, ready):
            copy(dst[:, 0, :, :], PS[:, bank, 0:2 * D].rearrange("p (b c) -> p b c", b=2))
            copy(dst[0:rows, 1, :, :], PS[0:rows, bank + 1, 0:2 * D].rearrange("p (b c) -> p b c", b=2)).then_inc(ready, 1)

        def exps(i, u):
            act.wait_ge(max_ready, i * 6 + u + 1)
            if u >= 2:
                act.wait_ge(probT_ps, i * 12 + 2 * (u - 2) + 2)
            for s in range(6):
                last = nc.scalar.activation(PX[:, u % 2, s, :], PS[:, 2 * (u % 2) + s // 3, (s % 3) * S:(s % 3 + 1) * S], ACT.Exp,
                                            bias=nb[:, u, s:s + 1], scale=HEAD_SCALE)
            last.then_inc(prob_ready, 1)

        def img_probs(i, u):
            for r in range(2):
                g = 2 * u + r
                h0 = 6 * (u % 2) + 3 * r
                act.wait_ge(probT_ps, i * 12 + g + 1)
                src = PS[0:NIMG, 6 + g % 2, 0:3 * P]
                if u // 2 < 2:
                    last = copy(PT[0:NIMG, 1, h0:h0 + 3, u // 2, 0:P], src.rearrange("p (h q) -> p h q", h=3))
                else:
                    last = copy(PT[0:NIMG, 1, h0:h0 + 3, :, P:D], src.rearrange("p (h b q) -> p h b q", h=3, b=2))
                last.then_inc(probT_img_ready, 1)

        with act.Fori(0, PAIRS) as i:
            act.wait_ge(xnT_ps, i + 1)
            copy(XNT[:, 0:4, :], PS[:, 0, :].rearrange("p (k c) -> p k c", k=4))
            copy(XNT[:, 4:6, :], PS[:, 1, 0:2 * P].rearrange("p (k c) -> p k c", k=2)).then_inc(xnT_ready, 1)
            act.wait_ge(xaT_ps, i + 1)
            transposed(XAT, 3, 65, xaT_ready)
            for step, dst in enumerate((GS, T1, PM)):
                w = DA if step == 0 else D
                for b in range(2):
                    bank = ((5, 6), (0, 1), (2, 7))[step][b]
                    act.wait_ge(lin_mat_ps, i * 6 + 2 * step + b + 1)
                    copy(dst[:, b, 0, 0:w], PS[:, bank, 0:w])
                    copy(dst[0:65, b, 1, 0:w], PS[0:65, bank, w:2 * w]).then_inc(lin_mat_ready, 1)
            act.wait_ge(zT_ps, i + 1)
            transposed(ZT, 5, 64, zT_ready)
            for m in range(6):
                act.wait_ge(qk_ps, i * 6 + m + 1)
                nc.scalar.activation(QK[:, m, :, :], PS[:, (0, 1, 2, 3, 4, 7)[m], 0:2 * D].rearrange("p (b c) -> p b c", b=2),
                                     ACT.Identity, bias=qkb[:, m:m + 1], scale=1.0).then_inc(qk_ready, 1)
            exps(i, 0)
            for u in range(1, 6):
                exps(i, u)
                img_probs(i, u - 1)
            img_probs(i, 5)
            for b in range(2):
                act.wait_ge(ctxT_ps, i * 3 + b + 1)
                src = PS[:, b, 0:2 * D].rearrange("p (c q) -> p c q", c=2)
                copy(CT[:, 0:2, P * b:P * b + P], src[:, :, 0:P])
                copy(CT[:, 0:2, 2 * P + 64 * b:2 * P + 64 * b + 64], src[:, :, P:D]).then_inc(ctxT_ready, 1)
            act.wait_ge(ctxT_ps, i * 3 + 3)
            src = PS[:, 2, 0:2 * D].rearrange("p (b q) -> p b q", b=2)
            copy(CT[:, 2, 0:2 * P].rearrange("p (b q) -> p b q", b=2), src[:, :, 0:P])
            copy(CT[:, 2, 2 * P:3 * P].rearrange("p (b q) -> p b q", b=2), src[:, :, P:D]).then_inc(ctxT_ready, 1)
            act.wait_ge(cnT_ps, i + 1)
            copy(CNT[:, 0, :], PS[:, 6, 0:3 * P])
            copy(CNT[0:64, 1, :], PS[0:64, 7, 0:3 * P]).then_inc(cnT_ready, 1)

        act.wait_ge(x1_ready, PAIRS)
        nc.scalar.activation(ones33[:, :], ident[0:33, 0:TB], ACT.Copy, scale=0.0, bias=1.0).then_inc(phase_done, 1)
        act.wait_ge(vec_in, NVEC * 16)
        act.wait_ge(phase_done, 4)
        for f in range(NF):
            act.wait_ge(raw_in[f % 2], (f // 2 + 1) * 64)
            for k in range(2):
                nc.scalar.activation(w1r[:, f, 2 * k, :], rw1[:, f % 2, k, :], ACT.Copy, scale=(g2c[:, k:k + 1] if f else 1.0))
            copy(w2r[:, f, :, 0:D], rw2[:, f % 2, :, :]).then_inc(hi_ready, 1)

        def split_high(i, q):
            act.wait_ge(actT_ps, i * 2 + q + 1)
            copy(XH[:, :], PS[:, 0, 0:GT])
            copy(XS[0:64, :], PS[0:64, 1, 0:GT]).then_inc(actT_hi, 1)

        def gelus(n, slot):
            for m in range(KH):
                q = slot * KH + m
                act.wait_ge(up_ps, n * (NF * KH) + q + 1)
                act.wait_ge(hid_ready, n * (NF * KH) + q + 1)
                nc.scalar.activation(GF[:, q % 3, :], PS[:, 2 + q % 2, 0:GT], ACT.Gelu,
                                     bias=b1c[:, slot, m:m + 1], scale=1.0).then_inc(gelu_ready, 1)

        with act.Fori(0, GROUPS) as n:
            split_high(n, 0)
            gelus(n, 0)
            split_high(n, 1)
            act.wait_ge(ldiff_ready, n + 1)
            nc.scalar.activation(lex[:, :, :], ldf[:, :, :], ACT.Exp).then_inc(lexp_ready, 1)
            for slot in range(1, NF):
                gelus(n, slot)

    @block.vector
    def _(dve):
        steps = Steps(dve_step, dve)
        tt, ts, cp = nc.vector.tensor_tensor, nc.vector.tensor_scalar, nc.vector.tensor_copy
        stt = nc.vector.scalar_tensor_tensor

        dve.wait_ge(const_in, NCONST * 16)
        cp(lnp_rep[:, :, :], lnp_b[:, :].unsqueeze(2).to_broadcast([P, KP, P]))
        cp(fb_rep[:, 0, :], fb[:, 0:1].to_broadcast([P, P]))
        cp(fb_rep[0:64, 1, :], fb[0:64, 1:2].to_broadcast([64, P])).then_inc(setup_dve, 1)
        tt(b2m[:, :], b2m[:, :], clsb[:, :], ALU.add)
        dve.wait_ge(setup_ps, 3)
        tt(lin_bias[:, :], lin_bias[:, :], PS[:, 2, 0:D], ALU.add)
        tt(qkb[:, :], qkb[:, :], PS[:, 3, 0:6], ALU.add)
        tt(vb[:, :], vb[:, :], PS[:, 4, 0:D], ALU.add).then_inc(setup_dve, 1)
        for k in range(KP):
            ts(wlin[:, k, :], wlin[:, k, :], lnp_g[:, k:k + 1], None, ALU.mult)
        for k in range(2):
            r = KD[k]
            ts(wqk[0:r, k, :, :, :], wqk[0:r, k, :, :, :], fg[0:r, k:k + 1], None, ALU.mult)
            ts(wv[0:r, k, :], wv[0:r, k, :], fg[0:r, k:k + 1], None, ALU.mult)
        dve.wait_ge(setup_ps, 5)
        steps.link(tt(ob[:, :], ob[:, :], PS[:, 6, 0:D], ALU.add))
        nc.vector.memset(mx[:, 0, 0:1], 0.0).then_inc(h1_stored, 1)
        nc.vector.memset(mx[:, 0, 1:2], 0.0).then_inc(x1_stored, 1)
        dve.wait_ge(pool_step, 4)
        nc.vector.memset(mx[:, 0, 2:3], 0.0).then_inc(attn_const_ready, 1)
        setup_steps = steps.k

        def norm(i, k, src, dst, n, width=D):
            for t in range(n):
                if width > 512:
                    for c in range(2):
                        last = nc.vector.bn_stats(st[:, k - 1, c, :], src[:, c * width // 2:(c + 1) * width // 2])
                else:
                    last = nc.vector.bn_stats(st[:, k - 1, t, :], src(t))
            steps.link_aggregate(last, pad[:, 0:1])
            for t in range(n):
                last = nc.vector.bn_aggr(mv[:, k - 1, t, :], st[:, k - 1, 0:2, :] if width > 512 else st[:, k - 1, t, :])
            steps.link(last)
            ts(ve[:, k - 1, 0:n], mv[:, k - 1, 0:n, 1], EPS, None, ALU.add).then_inc(var_ready, 1)
            dve.wait_ge(rstd_ready, i * 5 + k)
            if dst is None:
                return None
            for t in range(n):
                last = ts(dst(t), src if width > 512 else src(t), mv[:, k - 1, t, 0:1], rs[:, k - 1, t:t + 1],
                          ALU.subtract, ALU.mult)
            return last

        def maxima(i, u):
            dve.wait_ge(score_ps, i * 6 + u + 1)
            src = PS[:, 2 * (u % 2):2 * (u % 2) + 2, 0:3 * S].rearrange("p a (s k) -> p a s k", s=3)
            steps.link(nc.vector.tensor_reduce(mx[:, u, :].rearrange("p (a s) -> p a s", a=2), src, AX_X, ALU.max))
            ts(nb[:, u, :], mx[:, u, :], -HEAD_SCALE, None, ALU.mult).then_inc(max_ready, 1)

        def txt_probs(i, u):
            for r in range(2):
                g = 2 * u + r
                h0 = 6 * (u % 2) + 3 * r
                dve.wait_ge(probT_ps, i * 12 + g + 1)
                src = PS[:, 4 + g % 2, 0:3 * P]
                if u // 2 < 2:
                    last = cp(PT[:, 0, h0:h0 + 3, u // 2, 0:P], src.rearrange("p (h q) -> p h q", h=3))
                else:
                    last = cp(PT[:, 0, h0:h0 + 3, :, P:D], src.rearrange("p (h b q) -> p h b q", h=3, b=2))
                last.then_inc(probT_txt_ready, 1)

        N_STEPS = 23
        with dve.Fori(0, PAIRS) as i:
            steps.at(setup_steps + i * N_STEPS)
            dve.wait_ge(patches_in, i * 32 + 32)
            norm(i, 1, XP[:, :], lambda t: XN[:, :], 1, PD).then_inc(xn_ready, 1)
            dve.wait_ge(tok_ps, i + 1)
            steps.link(tt(Y[:, :], PS[:, 2, 0:D], lin_bias[:, :], ALU.add))
            norm(i, 2, lambda t: Y[:, :], None, 1)
            steps.link(stt(Y2[:, :], Y[:, :], mv[:, 1, 0, 0:1], g2m[:, :], ALU.subtract, ALU.mult))
            steps.link(stt(H[:, 2, :], Y2[:, :], rs[:, 1, 0:1], b2m[:, :], ALU.mult, ALU.add))
            dve.wait_ge(txt_in, i * 16 + 16)
            norm(i, 3, lambda t: H[:, t, :], lambda t: XA[:, t, 0:D], 3).then_inc(xa_ready, 1)
            dve.wait_ge(lin_ps, i + 1)
            dve.wait_ge(h1_stored, i * 48 + 1)
            tt(H1[:, 0:2, :], PS[:, 3, 0:2 * D].rearrange("p (t d) -> p t d", t=2), H[:, 0:2, :], ALU.add)
            tt(H1[:, 2, :], PS[:, 4, 0:D], H[:, 2, :], ALU.add).then_inc(h1_ready, 1)
            dve.wait_ge(h1_ready, i + 1)
            steps.link(norm(i, 4, lambda t: H1[:, t, :], lambda t: U[:, t, :], 3))
            cp(mx[:, 0, 0:1], mv[:, 3, 0, 0:1]).then_inc(u_ready, 1)
            norm(i, 5, lambda t: U[:, t, :], lambda t: Z[:, t, :], 3).then_inc(z_ready, 1)
            dve.wait_ge(v_ps, i + 1)
            cp(VX[:, 0, :, :, 0:HD], PS[:, 5, 0:2 * D].rearrange("p (b h e) -> p b h e", b=2, h=NH))
            cp(VX[0:NIMG, 1, :, :, 0:HD], PS[0:NIMG, 6, 0:2 * D].rearrange("p (b h e) -> p b h e", b=2, h=NH)).then_inc(v_ready, 1)
            maxima(i, 0)
            for u in range(1, 6):
                maxima(i, u)
                txt_probs(i, u - 1)
            txt_probs(i, 5)
            for t in range(3):
                dve.wait_ge(ctx_ps, i * 3 + t + 1)
                src = PS[:, 3 + t, 0:NH * 32].rearrange("p (h e) -> p h e", h=NH)
                steps.link(nc.vector.reciprocal(rec[:, t, :], src[:, :, HD]))
                last = tt(CN[:, t, :].rearrange("p (h e) -> p h e", h=NH), src[:, :, 0:HD],
                          rec[:, t, :].unsqueeze(2).to_broadcast([P, NH, HD]), ALU.mult)
                last.then_inc(ctx_ready, 1)
            dve.wait_ge(proj_ps, i + 1)
            dve.wait_ge(ub_ready, i + 1)
            dve.wait_ge(x1_stored, i * 48 + 1)
            tt(X1[:, 0:2, :], PS[:, 0, 0:2 * D].rearrange("p (t d) -> p t d", t=2), UB[:, 0:2, :], ALU.add)
            tt(X1[:, 2, :], PS[:, 1, 0:D], UB[:, 2, :], ALU.add).then_inc(x1_ready, 1)
            assert steps.k == N_STEPS, steps.k
        steps.at(setup_steps + PAIRS * N_STEPS)

        dve.wait_ge(x1_stored, PAIRS * 48 + 1)
        dve.wait_ge(h1_stored, PAIRS * 48 + 1)
        steps.link(nc.vector.memset(b2r[:, :, :].bitcast(F32), 0.0))
        cp(comb[:, 0, 0:1], ident[0:TB, 0:1]).then_inc(phase_done, 2)
        dve.wait_ge(phase_done, 4)
        dve.wait_ge(vec_in, NVEC * 16)
        steps.link(cp(b2r[0:1, :, :], rb2[:, :, :]))
        tt(b2r[32:33, :, :], rb2[:, :, :], b2r[0:1, :, :].bitcast(F32), ALU.subtract)
        cp(b2rep[:, :, :], b2c[:, :].unsqueeze(2).to_broadcast([P, 2, P])).then_inc(bias_ready, 1)
        for k in range(2):
            steps.link(ts(gwr[:, 2 * k, :], gwf[:, k, :], g2c[:, k:k + 1], None, ALU.mult))
            stt(gwr[:, 2 * k + 1, :], gwf[:, k, :], g2c[:, k:k + 1], gwr[:, 2 * k, :].bitcast(F32), ALU.mult, ALU.subtract)
        for f in range(NF):
            dve.wait_ge(hi_ready, f + 1)
            for k in range(2):
                hi = w1r[:, f, 2 * k, :].bitcast(F32)
                if f:
                    stt(w1r[:, f, 2 * k + 1, :], rw1[:, f % 2, k, :], g2c[:, k:k + 1], hi, ALU.mult, ALU.subtract)
                else:
                    tt(w1r[:, f, 2 * k + 1, :], rw1[:, f % 2, k, :], hi, ALU.subtract)
            tt(w2r[:, f, :, D:2 * D], rw2[:, f % 2, :, :], w2r[:, f, :, 0:D].bitcast(F32), ALU.subtract).then_inc(lo_ready, 1)
        dve.wait_ge(bias_ps, NE + 2)
        tt(b1c[:, 1:NF, :], b1c[:, 1:NF, :], PS[:, 0, 0:NE * KH].rearrange("p (e k) -> p e k", e=NE), ALU.add)
        tt(gbb[:, :], gbb[:, :], PS[:, 1, 0:NE], ALU.add).then_inc(bias_ready, 1)
        cp(den[:, 0:1], ident[0:TB, 0:1]).then_inc(hid_ready, 3)
        cp(den[:, 1:2], ident[0:TB, 0:1]).then_inc(gelu_ready, 2)
        cp(den[:, 2:3], ident[0:TB, 0:1]).then_inc(down_read, 4)
        cp(den[:, 3:4], ident[0:TB, 0:1]).then_inc(out_stored, 1)

        def split_low(n, q):
            dve.wait_ge(actT_hi, n * 2 + q + 1)
            tt(XL[:, :], PS[:, 0, 0:GT], XH[:, :].bitcast(F32), ALU.subtract)
            tt(XS[64:P, :], PS[0:64, 1, 0:GT], XS[0:64, :].bitcast(F32), ALU.subtract).then_inc(actT_ready, 1)

        def hidden(n, slot):
            for m in range(KH):
                q = slot * KH + m
                dve.wait_ge(gelu_ready, n * (NF * KH) + q + 1 + 2)
                steps.link(cp(GH[:, slot % 2, m, :], GF[:, q % 3, :]))
                tt(GL[:, slot % 2, m, :], GF[:, q % 3, :], GH[:, slot % 2, m, :].bitcast(F32), ALU.subtract).then_inc(hid_ready, 1)

        def accumulate(n, slot):
            for t in range(TG):
                dve.wait_ge(down_ps, n * (NF * TG) + slot * TG + t + 1)
                w = comb[:, t, slot - 1:slot]
                steps.link(stt(ACC[:, t, :], PS[0:TB, 4 + t, 0:D], w, ACC[:, t, :], ALU.mult, ALU.add))
                last = stt(ACC[:, t, :], PS[0:TB, 4 + t, D:2 * D], w, ACC[:, t, :], ALU.mult, ALU.add)
                last.then_inc(down_read, 1)
                if slot == NF - 1 and t == TG - 1:
                    dve.wait_ge(down_read, (n + 1) * (NF * TG) + 4)
                    cp(den[:, 0:1], den[:, 1:2]).then_inc(out_ready, 1)

        first = setup_steps + PAIRS * N_STEPS + steps.k
        N2 = 59
        with dve.Fori(0, GROUPS) as n:
            steps.at(first + n * N2)
            split_low(n, 0)
            hidden(n, 0)
            for t in range(TG):
                dve.wait_ge(down_ps, n * (NF * TG) + t + 1)
            steps.link(tt(X2[:, :, :], PS[0:TB, 4:8, 0:D], X[:, :, :], ALU.add))
            last = tt(X2[:, :, :], PS[0:TB, 4:8, D:2 * D], X2[:, :, :], ALU.add)
            steps.link(last)
            cp(den[:, 0:1], X2[:, 0, 0:1]).then_inc(down_read, 4)
            for t in range(TG):
                last = nc.vector.bn_stats(st2[:, t, :], X2[:, t, :])
            steps.link_aggregate(last, pad[:, 0:1])
            for t in range(TG):
                last = nc.vector.bn_aggr(mv2[:, t, :], st2[:, t, :])
            steps.link(last)
            ts(ve2[:, :], mv2[:, :, 1], EPS, None, ALU.add).then_inc(var2_ready, 1)
            dve.wait_ge(rstd2_ready, n + 1)
            for t in range(TG):
                last = ts(Z2[:, t, :], X2[:, t, :], mv2[:, t, 0:1], rs2[:, t:t + 1], ALU.subtract, ALU.mult)
            last.then_inc(z2_ready, 1)
            split_low(n, 1)
            dve.wait_ge(gate_ps, n + 1)
            steps.link(tt(lg[:, :, :], PS[0:TB, 1, 0:TG * NE].rearrange("p (t e) -> p t e", t=TG),
                          gbb[0:TB, :].unsqueeze(1).to_broadcast([TB, TG, NE]), ALU.add))
            nc.vector.tensor_reduce(top[:, :], lg[:, :, :], AX_X, ALU.max)
            for t in range(TG):
                lj = lg[:, t, :].unsqueeze(1).to_broadcast([TB, NE, NE])
                le = lg[:, t, :].unsqueeze(2).to_broadcast([TB, NE, NE])
                tt(gtm[:, t, :, :], lj, le, ALU.is_gt)
                last = tt(eqm[:, t, :, :], lj, le, ALU.is_equal)
            steps.link(last)
            tt(ldf[:, :, :], lg[:, :, :], top[:, :].unsqueeze(2).to_broadcast([TB, TG, NE]), ALU.subtract).then_inc(ldiff_ready, 1)
            steps.link(tt(eqm[:, :, :, :], eqm[:, :, :, :],
                          tri[0:TB, :, :].unsqueeze(1).to_broadcast([TB, TG, NE, NE]), ALU.mult))
            steps.link(tt(gtm[:, :, :, :], gtm[:, :, :, :], eqm[:, :, :, :], ALU.add))
            steps.link(nc.vector.tensor_reduce(rank[:, :, :], gtm[:, :, :, :], AX_X, ALU.add))
            dve.wait_ge(lexp_ready, n + 1)
            steps.link(stt(gex[:, :, :], rank[:, :, :], 2.0, lex[:, :, :], ALU.is_lt, ALU.mult))
            steps.link(nc.vector.tensor_reduce(den[:, :], gex[:, :, :], AX_X, ALU.add))
            steps.link(nc.vector.reciprocal(den[:, :], den[:, :]))
            steps.link(tt(comb[:, :, :], gex[:, :, :], den[:, :].unsqueeze(2).to_broadcast([TB, TG, NE]), ALU.mult))
            hidden(n, 1)
            hidden(n, 2)
            dve.wait_ge(acc_init, n + 1)
            accumulate(n, 1)
            hidden(n, 3)
            accumulate(n, 2)
            hidden(n, 4)
            accumulate(n, 3)
            accumulate(n, 4)
            assert steps.k == N2, steps.k

    @block.tensor
    def _(pe):
        def mm(o, l, r, start=True, stop=True):
            return nc.tensor.matmul(o, l, r, start=start, stop=stop)

        def tr(o, x, rows=P):
            return nc.tensor.transpose(o, x, ident[0:rows, 0:rows])

        pe.wait_ge(const_in, NCONST * 16)
        pe.wait_ge(ident_ready, 2)
        for m in range(2):
            for k in range(2):
                last = mm(PS[0:KA[m], 0, m * DA:(m + 1) * DA], wka[0:KD[k], k, P * m:P * m + KA[m]], wqa[0:KD[k], k, :], k == 0, k == 1)
        last.then_inc(setup_ps, 1)
        pe.wait_ge(setup_dve, 1)
        for k in range(KP):
            last = mm(PS[:, 2, 0:D], lnp_rep[:, k, :], wlin[:, k, :], k == 0, k == KP - 1)
        last.then_inc(setup_ps, 1)
        for m in range(6):
            for k in range(2):
                mm(PS[:, 3, m:m + 1], wqk[0:KD[k], k, m, :, :], fb[0:KD[k], k:k + 1], k == 0, k == 1)
        for k in range(2):
            last = mm(PS[:, 4, 0:D], fb_rep[0:KD[k], k, :], wv[0:KD[k], k, :], k == 0, k == 1)
        last.then_inc(setup_ps, 1)
        pe.wait_ge(setup_dve, 2)
        tr(PS[:, 5, 0:P], vb[:, 0:P])
        tr(PS[0:64, 5, P:2 * P], vb[:, P:D]).then_inc(setup_ps, 1)
        pe.wait_ge(setup_act, 2)
        for k in range(2):
            last = mm(PS[:, 6, 0:D], vbT[0:KD[k], k, :], ow[0:KD[k], k, :], k == 0, k == 1)
        last.then_inc(setup_ps, 1)
        pe.wait_ge(attn_const_ready, 1)

        def transpose_set(x, bank, rows, ps):
            for k in range(2):
                w = rows[k]
                o = PS[0:w, bank + k, 0:2 * D].rearrange("p (b c) -> p b c", b=2)
                for b in range(2):
                    tr(o[:, b, 0:P], x[:, b, P * k:P * k + w])
                last = tr(o[:, :, P:D], x[:, 2, P * k:P * k + w])
            last.then_inc(ps, 1)

        def scores(i, u):
            t = u // 2
            if u >= 2:
                pe.wait_ge(prob_ready, i * 6 + u - 1)
            for s in range(3):
                for r in range(2):
                    j = 2 * (u % 2) + r
                    bank, col = 2 * (u % 2) + r, s * S
                    q, k = QK[32 * j:32 * j + HD, 2 * s, :, :], QK[32 * j:32 * j + HD, 2 * s + 1, :, :]
                    if t < 2:
                        last = mm(PS[:, bank, col:col + S], q[:, t, 0:P], k[:, t, 0:S])
                    else:
                        for b in range(2):
                            last = mm(PS[64 * b:64 * b + 64, bank, col:col + S], q[:, b, P:D], k[:, b, 0:S])
            last.then_inc(score_ps, 1)

        def transpose_probs(i, u):
            pe.wait_ge(prob_ready, i * 6 + u + 1)
            for r in range(2):
                g = 2 * u + r
                if g >= 2:
                    pe.wait_ge(probT_txt_ready, i * 12 + g - 1)
                    pe.wait_ge(probT_img_ready, i * 12 + g - 1)
                for s in range(3):
                    tr(PS[:, 4 + g % 2, P * s:P * s + P], PX[:, u % 2, 3 * r + s, 0:P])
                    last = tr(PS[0:NIMG, 6 + g % 2, P * s:P * s + P], PX[:, u % 2, 3 * r + s, P:S])
                last.then_inc(probT_ps, 1)

        with pe.Fori(0, PAIRS) as i:
            pe.wait_ge(xn_ready, i + 1)
            for k in range(KP):
                last = tr(PS[:, k // 4, P * (k % 4):P * (k % 4) + P], XN[:, P * k:P * k + P])
            last.then_inc(xnT_ps, 1)
            pe.wait_ge(xnT_ready, i + 1)
            for k in range(KP):
                last = mm(PS[:, 2, 0:D], XNT[:, k, :], wlin[:, k, :], k == 0, k == KP - 1)
            last.then_inc(tok_ps, 1)
            pe.wait_ge(xa_ready, i + 1)
            transpose_set(XA, 3, KA, xaT_ps)
            for b in range(2):
                for m in range(2):
                    o = PS[0:KA[m], 5 + b, m * DA:(m + 1) * DA]
                    mm(o, XA[:, b, P * m:P * m + KA[m]], XA[:, b, :], True, False)
                    last = mm(o, XA[64 * b:64 * b + NIMG, 2, P * m:P * m + KA[m]], XA[64 * b:64 * b + NIMG, 2, :], False, True)
                last.then_inc(lin_mat_ps, 1)
            for b in range(2):
                pe.wait_ge(lin_mat_ready, i * 6 + b + 1)
                for m in range(2):
                    for k in range(2):
                        last = mm(PS[0:KA[m], b, m * D:(m + 1) * D], GS[0:KA[k], b, k, P * m:P * m + KA[m]], wva[0:KA[k], k, :], k == 0, k == 1)
                last.then_inc(lin_mat_ps, 1)
            for b in range(2):
                pe.wait_ge(lin_mat_ready, i * 6 + 2 + b + 1)
                for m in range(2):
                    for k in range(2):
                        last = mm(PS[0:KA[m], (2, 7)[b], m * D:(m + 1) * D], AT[0:KA[k], k, P * m:P * m + KA[m]], T1[0:KA[k], b, k, :], k == 0, k == 1)
                last.then_inc(lin_mat_ps, 1)
            pe.wait_ge(xaT_ready, i + 1)
            for b in range(2):
                pe.wait_ge(lin_mat_ready, i * 6 + 4 + b + 1)
                for k in range(2):
                    mm(PS[:, 3, b * D:(b + 1) * D], XAT[0:KA[k], k, b, 0:P], PM[0:KA[k], b, k, :], k == 0, k == 1)
                for k in range(2):
                    last = mm(PS[64 * b:64 * b + 64, 4, 0:D], XAT[0:KA[k], k, b, P:D], PM[0:KA[k], b, k, :], k == 0, k == 1)
            last.then_inc(lin_ps, 1)
            pe.wait_ge(z_ready, i + 1)
            transpose_set(Z, 5, KD, zT_ps)
            pe.wait_ge(zT_ready, i + 1)
            for m in range(6):
                for k in range(2):
                    last = mm(PS[:, (0, 1, 2, 3, 4, 7)[m], 0:2 * D], wqk[0:KD[k], k, m, :, :], ZT[0:KD[k], k, :, :], k == 0, k == 1)
                last.then_inc(qk_ps, 1)
            for b in range(2):
                for k in range(2):
                    mm(PS[:, 5, b * D:(b + 1) * D], ZT[0:KD[k], k, b, 0:P], wv[0:KD[k], k, :], k == 0, k == 1)
                for k in range(2):
                    last = mm(PS[0:NIMG, 6, b * D:(b + 1) * D], ZT[0:KD[k], k, b, P:P + NIMG], wv[0:KD[k], k, :], k == 0, k == 1)
            last.then_inc(v_ps, 1)
            pe.wait_ge(qk_ready, i * 6 + 6)
            pe.wait_ge(v_ready, i + 1)
            scores(i, 0)
            scores(i, 1)
            for u in range(6):
                transpose_probs(i, u)
                if u < 4:
                    scores(i, u + 2)
            pe.wait_ge(probT_txt_ready, i * 12 + 12)
            pe.wait_ge(probT_img_ready, i * 12 + 12)
            rows = (NTXT, NIMG)
            for c, b in ((0, 0), (1, 0), (0, 1), (1, 1), (2, 0), (2, 1)):
                bank, col = (b, c * D) if c < 2 else (2, b * D)
                for k in range(2):
                    for j in range(4):
                        last = mm(PS[32 * j:32 * j + 32, bank, col:col + D], VX[0:rows[k], k, b, 4 * c + j, :],
                                  PT[0:rows[k], k, 3 * j + c, b, :], k == 0, k == 1)
                if c == 1 or (c, b) == (2, 1):
                    last.then_inc(ctxT_ps, 1)
            pe.wait_ge(ctxT_ready, i * 3 + 3)
            for t in range(3):
                for c in range(3):
                    last = tr(PS[:, 3 + t, P * c:P * c + P], CT[:, c, P * t:P * t + P])
                last.then_inc(ctx_ps, 1)
            for t in range(3):
                pe.wait_ge(ctx_ready, i * 3 + t + 1)
                for k in range(2):
                    last = tr(PS[0:KD[k], 6 + k, P * t:P * t + P], CN[:, t, P * k:P * k + KD[k]])
            last.then_inc(cnT_ps, 1)
            pe.wait_ge(cnT_ready, i + 1)
            for t in range(3):
                o = PS[:, 0, t * D:(t + 1) * D] if t < 2 else PS[:, 1, 0:D]
                for k in range(2):
                    last = mm(o, CNT[0:KD[k], k, P * t:P * t + P], ow[0:KD[k], k, :], k == 0, k == 1)
            last.then_inc(proj_ps, 1)

        pe.wait_ge(phase_done, 4)
        pe.wait_ge(bias_ready, 1)
        for f in range(NF):
            pe.wait_ge(raw_in[f % 2], (f // 2 + 1) * 64)
            if f == 0:
                for k in range(2):
                    last = mm(PS[:, 1, 0:NE], b2rep[0:KD[k], k, :], gwf[0:KD[k], k, :], k == 0, k == 1)
                last.then_inc(bias_ps, 1)
                continue
            for m in range(KH):
                c = (f - 1) * KH + m
                for k in range(2):
                    last = mm(PS[:, 0, c:c + 1], rw1[0:KD[k], f % 2, k, P * m:P * m + P], b2c[0:KD[k], k:k + 1], k == 0, k == 1)
            last.then_inc(bias_ps, 2 if f == NF - 1 else 1)
        pe.wait_ge(lo_ready, NF)
        pe.wait_ge(bias_ready, 2)
        pe.wait_ge(out_stored, 1)

        def transpose_group(x, ps):
            for t in range(TG):
                for k in range(2):
                    last = tr(PS[0:KD[k], k, TB * t:TB * t + TB], x[:, t, P * k:P * k + KD[k]], TB)
            last.then_inc(ps, 1)

        def up(n, slot):
            for m in range(KH):
                q = slot * KH + m
                o = PS[:, 2 + q % 2, 0:GT]
                w = w1r[:, slot, :, P * m:P * m + P]
                pe.wait_ge(gelu_ready, n * (NF * KH) + q + 1)
                mm(o, w[:, 0, :], XH[:, :], True, False)
                mm(o, w[:, 0, :], XL[:, :], False, False)
                mm(o, w[:, 1, :], XH[:, :], False, False)
                mm(o, w[:, 2, :], XS[:, :], False, False)
                mm(o, w[0:64, 3, :], XS[0:64, :], False, True).then_inc(up_ps, 1)

        def down(n, slot):
            for t in range(TG):
                bank = PS[0:TB, 4 + t, :]
                if t == 0:
                    pe.wait_ge(hid_ready, n * (NF * KH) + (slot + 1) * KH + 3)
                pe.wait_ge(down_read, n * (NF * TG) + slot * TG + t + 1)
                for k in range(KH):
                    mm(bank[:, 0:2 * D], GH[:, slot % 2, k, TB * t:TB * t + TB], w2r[:, slot, k, :], k == 0, False)
                    mm(bank[:, 0:D], GL[:, slot % 2, k, TB * t:TB * t + TB], w2r[:, slot, k, 0:D], False, False)
                mm(bank[:, 0:D], ones33[:, :], b2r[:, slot, :], False, True).then_inc(down_ps, 1)

        with pe.Fori(0, GROUPS) as n:
            pe.wait_ge(x_in, n * 32 + 32)
            transpose_group(X, actT_ps)
            pe.wait_ge(actT_ready, n * 2 + 1)
            up(n, 0)
            down(n, 0)
            pe.wait_ge(z2_ready, n + 1)
            transpose_group(Z2, actT_ps)
            pe.wait_ge(actT_ready, n * 2 + 2)
            for t in range(TG):
                o = PS[0:TB, 1, NE * t:NE * t + NE]
                cols = slice(TB * t, TB * t + TB)
                mm(o, XH[:, cols], gwr[:, 0, :], True, False)
                mm(o, XL[:, cols], gwr[:, 0, :], False, False)
                mm(o, XH[:, cols], gwr[:, 1, :], False, False)
                mm(o, XS[:, cols], gwr[:, 2, :], False, False)
                last = mm(o, XS[0:64, cols], gwr[0:64, 3, :], False, True)
            last.then_inc(gate_ps, 1)
            up(n, 1)
            up(n, 2)
            down(n, 1)
            up(n, 3)
            down(n, 2)
            up(n, 4)
            down(n, 3)
            down(n, 4)

    ctx.close()


_RENAMED = {
    "txt": "txt", "lnp_g": "L0_tok_ln1_g", "lnp_b": "L0_tok_ln1_b", "W_lin": "L0_tok_W_lin", "b_lin": "L0_tok_b_lin",
    "ln2_g": "L0_tok_ln2_g", "ln2_b": "L0_tok_ln2_b", "pos": "L0_tok_pos_embedding", "cls": "L0_tok_cls_token",
    "Wq": "L0_attn_Wq", "bq": "L0_attn_bq", "Wk": "L0_attn_Wk", "bk": "L0_attn_bk", "bv": "L0_attn_bv",
    "f1_g": "L0_ffn_ln1_g", "f1_b": "L0_ffn_ln1_b", "in_b": "L0_ffn_in_b", "out_b": "L0_ffn_out_b",
    "mlp_w1": "L0_ffn_mlp_w1", "mlp_b1": "L0_ffn_mlp_b1", "mlp_w2": "L0_ffn_mlp_w2", "mlp_b2": "L0_ffn_mlp_b2",
    "f2_g": "L0_ffn_ln2_g", "f2_b": "L0_ffn_ln2_b", "gate_b": "L0_ffn_gate_b",
    "exp_w1": "L0_ffn_exp_w1", "exp_b1": "L0_ffn_exp_b1", "exp_w2": "L0_ffn_exp_w2", "exp_b2": "L0_ffn_exp_b2",
}
_TRANSPOSED = {"WvT": "L0_attn_Wv", "in_wT": "L0_ffn_in_w", "out_wT": "L0_ffn_out_w", "gate_wT": "L0_ffn_gate_w"}


def kernel(**inputs):
    import numpy as _np
    import concourse.bacc as _bacc
    from concourse import mybir as _mybir
    from concourse.bass_utils import run_bass_kernel_spmd as _run

    nc = _bacc.Bacc("TRN2", target_bir_lowering=False, num_devices=1)
    laid = {name: _np.ascontiguousarray(inputs[source]) for name, source in _RENAMED.items()}
    laid |= {name: _np.ascontiguousarray(_np.asarray(inputs[source]).T) for name, source in _TRANSPOSED.items()}
    for name in ("lnp_g", "lnp_b", "mlp_b1"):
        laid[name] = _np.ascontiguousarray(laid[name].reshape(-1, 128).T)
    laid["exp_b1"] = _np.ascontiguousarray(laid["exp_b1"].reshape(4, -1, 128).transpose(2, 0, 1))
    laid["qk_b"] = _np.ascontiguousarray(laid["in_b"][0:384].reshape(2, 3, 4, 16).transpose(2, 3, 1, 0)).reshape(4, 16, 6)
    x = _np.asarray(inputs["x"]).reshape(32, 3, 6, 16, 6, 16)
    laid["patches"] = _np.ascontiguousarray(x.transpose(0, 2, 4, 3, 5, 1)).reshape(32, 36, 768)
    arrays, args = {}, {}
    for name, v in laid.items():
        arrays[f"in_{name}"] = v
        args[name] = nc.dram_tensor(f"in_{name}", v.shape, _mybir.dt.from_np(v.dtype), kind="ExternalInput").ap()
    out = nc.dram_tensor("out", (32, 165, 192), _mybir.dt.from_np(_np.dtype("float32")), kind="ExternalOutput").ap()
    build_program(nc, args, out)
    r = _run(nc, [arrays], core_ids=[0])
    return r.results[0]["out"]
```

```python
from contextlib import ExitStack

import numpy as np

import concourse.bass as bass
from concourse import mybir

F32 = mybir.dt.float32
F32R = mybir.dt.float32r
ALU = mybir.AluOpType
ACT = mybir.ActivationFunctionType
AX_X = mybir.AxisListType.X

P = 128
B = 32
NPATCH = 36
NIMG = NPATCH + 1
NTXT = 128
S = NIMG + NTXT
D = 192
DA = D + 1
PD = 768
HID = 768
NH = 12
HD = D // NH
NE = 4
NF = NE + 1
PAIRS = B // 2
KP = PD // P
KH = HID // P
KD = (128, 64)
KA = (128, 65)
EPS = 1e-5
TB = 120
TG = 4
GT = TB * TG
GROUPS = B * S // GT
assert GROUPS * GT == B * S
PXW = NTXT + 64 + S
TILE_OF = (0, 2, 1)
HEAD_SCALE = float(HD) ** -0.5


class Steps:

    def __init__(self, sem, eng):
        self.sem, self.eng, self.base, self.k = sem, eng, 0, 0

    def at(self, base):
        self.base, self.k = base, 0

    def link(self, ins):
        self.k += 1
        ins.then_inc(self.sem, 1)
        self.eng.wait_ge(self.sem, self.base + self.k)

    def link_aggregate(self, ins, pad):
        self.link(ins)
        self.eng.memset(pad, 0.0)


def build_program(nc, a, out):
    ctx = ExitStack()

    def sem(name):
        return ctx.enter_context(nc.semaphore(name))

    def sb(stack, name, shape, dt=F32):
        return stack.enter_context(nc.sbuf_tensor(name, shape, dt))

    h1d = nc.dram_tensor("h1_scratch", [B, S, D], F32, kind="Internal").ap()
    x1d = nc.dram_tensor("x1_scratch", [B, S, D], F32, kind="Internal").ap()

    PS = ctx.enter_context(nc.psum_tensor("PS", [P, 8, 512], F32))
    ident = sb(ctx, "ident", [P, P])
    eps_half = sb(ctx, "minus_half", [P, 8])

    pad = sb(ctx, "pad", [P, 1])

    one = ExitStack()
    wlin = sb(one, "wlin", [P, KP, D])
    lnp_g = sb(one, "lnp_g", [P, KP])
    lnp_b = sb(one, "lnp_b", [P, KP])
    lnp_rep = sb(one, "lnp_rep", [P, KP, P])
    lin_bias = sb(one, "lin_bias", [P, D])
    g2m = sb(one, "g2m", [P, D])
    b2m = sb(one, "b2m", [P, D])
    clsb = sb(one, "clsb", [P, D])
    wqa = sb(one, "wqa", [P, 2, DA])
    wka = sb(one, "wka", [P, 2, DA])
    AT = sb(one, "AT", [P, 2, DA])
    wva = sb(one, "wva", [P, 2, D])
    fg = sb(one, "fg", [P, 2])
    fb = sb(one, "fb", [P, 2])
    fb_rep = sb(one, "fb_rep", [P, 2, P])
    wqk = sb(one, "wqk", [P, 2, 6, NH // 3, 32])
    wv = sb(one, "wv", [P, 2, D])
    qkb = sb(one, "qkb", [P, 6])
    vb = sb(one, "vb", [P, D])
    vbT = sb(one, "vbT", [P, 2, P])
    ow = sb(one, "ow", [P, 2, D])
    ob = sb(one, "ob", [P, D])
    XP = sb(one, "XP", [P, PD])
    XN = sb(one, "XN", [P, PD])
    XNT = sb(one, "XNT", [P, KP, P])
    Y = sb(one, "Y", [P, D])
    Y2 = sb(one, "Y2", [P, D])
    H = sb(one, "H", [P, 3, D])
    XA = sb(one, "XA", [P, 3, DA])
    XAT = sb(one, "XAT", [P, 2, 2, D])
    GS = sb(one, "GS", [P, 2, 2, DA])
    T1 = sb(one, "T1", [P, 2, 2, D])
    PM = sb(one, "PM", [P, 2, 2, D])
    H1 = sb(one, "H1", [P, 3, D])
    U = sb(one, "U", [P, 3, D])
    UB = sb(one, "UB", [P, 3, D])
    Z = sb(one, "Z", [P, 3, D])
    ZT = sb(one, "ZT", [P, 2, 2, D])
    parity = sb(one, "parity", [P, 2])
    qb = sb(one, "qb", [P, 3, 2])
    Q = sb(one, "Q", [P, 3, 2, 2, D])
    K = sb(one, "K", [P, 3, 2, D])
    VX = sb(one, "VX", [P, 2, 2, NH, 32])
    PX = sb(one, "PX", [P, 2, 3, PXW])
    PT = sb(one, "PT", [P, 6, 3, 2 * D])
    CT = sb(one, "CT", [P, 3, 3 * P])
    rec = sb(one, "rec", [P, 3, NH])
    CN = sb(one, "CN", [P, 3, D])
    CNT = sb(one, "CNT", [P, 2, 3 * P])
    X1 = sb(one, "X1", [P, 3, D])
    st = sb(one, "st", [P, 5, 3, 6])
    mv = sb(one, "mv", [P, 5, 3, 2])
    ve = sb(one, "ve", [P, 5, 3])
    rs = sb(one, "rs", [P, 5, 3])
    mx = sb(one, "mx", [P, 6, 6])
    nb = sb(one, "nb", [P, 6, 6])
    one.close()

    two = ctx
    w1r = sb(two, "w1r", [P, NF, 4, HID], F32R)
    w2r = sb(two, "w2r", [P, NF, KH, 2 * D], F32R)
    b2r = sb(two, "b2r", [33, NF, D], F32R)
    ones33 = sb(two, "ones33", [33, TB], F32R)
    onesf = sb(two, "onesf", [33, TB])
    b1c = sb(two, "b1c", [P, NF, KH])
    g2c = sb(two, "g2c", [P, 2])
    b2c = sb(two, "b2c", [P, 2])
    b2rep = sb(two, "b2rep", [P, 2, P])
    gwr = sb(two, "gwr", [P, 4, NE], F32R)
    gbb = sb(two, "gbb", [P, NE])
    tri = sb(two, "tri", [P, NE, NE])
    raw = ExitStack()
    rw1 = sb(raw, "rw1", [P, 2, 2, HID])
    rw2 = sb(raw, "rw2", [P, 2, KH, D])
    rb2 = sb(raw, "rb2", [1, NF, D])
    gwf = sb(raw, "gwf", [P, 2, NE])
    raw.close()
    X = sb(two, "X", [TB, TG, D])
    HH = sb(two, "HH", [TB, TG, D])
    ACC = sb(two, "ACC", [TB, TG, D])
    X2 = sb(two, "X2", [TB, TG, D])
    Z2 = sb(two, "Z2", [TB, TG, D])
    XH = sb(two, "XH", [P, GT], F32R)
    XL = sb(two, "XL", [P, GT], F32R)
    XS = sb(two, "XS", [P, GT], F32R)
    GF = sb(two, "GF", [P, 3, GT])
    GH = sb(two, "GH", [P, 2, KH, GT], F32R)
    GL = sb(two, "GL", [P, 2, KH, GT], F32R)
    st2 = sb(two, "st2", [TB, TG, 6])
    mv2 = sb(two, "mv2", [TB, TG, 2])
    ve2 = sb(two, "ve2", [TB, TG])
    rs2 = sb(two, "rs2", [TB, TG])
    lg = sb(two, "lg", [TB, TG, NE])
    gtm = sb(two, "gtm", [TB, TG, NE, NE])
    eqm = sb(two, "eqm", [TB, TG, NE, NE])
    rank = sb(two, "rank", [TB, TG, NE])
    top = sb(two, "top", [TB, TG])
    ldf = sb(two, "ldf", [TB, TG, NE])
    lex = sb(two, "lex", [TB, TG, NE])
    gex = sb(two, "gex", [TB, TG, NE])
    den = sb(two, "den", [TB, TG])
    comb = sb(two, "comb", [TB, TG, NE])

    const_in = sem("const_in")
    ident_ready = sem("ident_ready")
    zeroed = sem("zeroed")
    setup_ps = sem("setup_ps")
    setup_dve = sem("setup_dve")
    setup_act = sem("setup_act")
    attn_const_ready = sem("attn_const_ready")
    patches_in = sem("patches_in")
    txt_in = sem("txt_in")
    dve_step = sem("dve_step")
    pool_step = sem("pool_step")
    var_ready = sem("var_ready")
    rstd_ready = sem("rstd_ready")
    xn_ready = sem("xn_ready")
    xnT_ps = sem("xnT_ps")
    xnT_ready = sem("xnT_ready")
    tok_ps = sem("tok_ps")
    xa_ready = sem("xa_ready")
    xaT_ps = sem("xaT_ps")
    xaT_ready = sem("xaT_ready")
    lin_mat_ps = sem("lin_mat_ps")
    lin_mat_ready = sem("lin_mat_ready")
    lin_ps = sem("lin_ps")
    h1_ready = sem("h1_ready")
    h1_stored = sem("h1_stored")
    u_ready = sem("u_ready")
    ub_ready = sem("ub_ready")
    z_ready = sem("z_ready")
    zT_ps = sem("zT_ps")
    zT_ready = sem("zT_ready")
    qk_ps = sem("qk_ps")
    qk_ready = sem("qk_ready")
    v_ps = sem("v_ps")
    v_ready = sem("v_ready")
    score_ps = sem("score_ps")
    max_ready = sem("max_ready")
    prob_ready = sem("prob_ready")
    probT_ps = sem("probT_ps")
    probT_dve_ready = sem("probT_dve_ready")
    probT_act_ready = sem("probT_act_ready")
    ctxT_ps = sem("ctxT_ps")
    ctxT_ready = sem("ctxT_ready")
    ctxT2_ready = sem("ctxT2_ready")
    ctx_ps = sem("ctx_ps")
    ctx_ready = sem("ctx_ready")
    cnT_ps = sem("cnT_ps")
    cnT_ready = sem("cnT_ready")
    proj_ps = sem("proj_ps")
    x1_ready = sem("x1_ready")
    x1_stored = sem("x1_stored")
    phase_done = sem("phase_done")
    raw_in = [sem("raw_in0"), sem("raw_in1")]
    vec_in = sem("vec_in")
    bias_ps = sem("bias_ps")
    bias_ready = sem("bias_ready")
    hi_ready = sem("hi_ready")
    lo_ready = sem("lo_ready")
    x_in = sem("x_in")
    actT_ps = sem("actT_ps")
    actT_hi = sem("actT_hi")
    actT_ready = sem("actT_ready")
    gate_ps = sem("gate_ps")
    ldiff_ready = sem("ldiff_ready")
    lexp_ready = sem("lexp_ready")
    up_ps = sem("up_ps")
    gelu_ready = sem("gelu_ready")
    hid_ready = sem("hid_ready")
    down_ps = sem("down_ps")
    down_read = sem("down_read")
    var2_ready = sem("var2_ready")
    rstd2_ready = sem("rstd2_ready")
    z2_ready = sem("z2_ready")
    acc_init = sem("acc_init")
    out_ready = sem("out_ready")
    out_stored = sem("out_stored")

    def probT_views(g):
        u, c = g // 3, g % 3
        t, half = TILE_OF[u // 2], u % 2
        src = PS[:, 4 + g % 2, 0:3 * P]
        dst = PT[:, 3 * half + c, :, :]
        if t < 2:
            return dst[:, :, D * t:D * t + P], src.rearrange("p (h q) -> p h q", h=3)
        return dst.rearrange("p h (b q) -> p h b q", b=2)[:, :, :, P:D], src.rearrange("p (h b q) -> p h b q", h=3, b=2)

    block = ctx.enter_context(nc.Block())
    NCONST = 49
    NVEC = 14

    def bc(ap, n):
        return ap.rearrange("(o d) -> o d", o=1).to_broadcast([n, ap.shape[-1]])

    @block.sync
    def _(sp):
        count = [0]

        def const(dst, src):
            sp.dma_start(dst, src).then_inc(const_in, 16)
            count[0] += 1

        sp.wait_ge(zeroed, 6)

        def load_pair(i):
            for b in range(2):
                sp.dma_start(XP[64 * b + 1:64 * b + NIMG, :],
                             a["patches"][bass.ds(2 * i + b, 1)].rearrange("o n d -> (o n) d")).then_inc(patches_in, 16)
            sp.dma_start(H[:, 0:2, :], a["txt"][bass.ds(2 * i, 2)].rearrange("b p d -> p b d")).then_inc(txt_in, 16)

        load_pair(0)
        const(wlin[:, :, :], a["W_lin"].rearrange("(k p) d -> p k d", p=P))
        const(lnp_g[:, :], a["lnp_g"])
        const(lnp_b[:, :], a["lnp_b"])
        const(lin_bias[:, :], bc(a["b_lin"], P))
        for b in range(2):
            const(g2m[64 * b + 1:64 * b + NIMG, :], bc(a["ln2_g"], NPATCH))
            const(b2m[64 * b:64 * b + NIMG, :], a["pos"][0, 0:NIMG, :])
            const(clsb[64 * b + 1:64 * b + NIMG, :], bc(a["ln2_b"], NPATCH))
            const(clsb[64 * b:64 * b + 1, :], a["cls"][0, :, :])
        for w, wname, bname in ((wqa, "Wq", "bq"), (wka, "Wk", "bk")):
            for k in range(2):
                const(w[0:KD[k], k, 0:D], a[wname][P * k:P * k + KD[k], :])
                const(w[0:KD[k], k, D:DA], a[bname][P * k:P * k + KD[k]].rearrange("(p o) -> p o", o=1))
        for k in range(2):
            const(wva[0:KD[k], k, :], a["WvT"][P * k:P * k + KD[k], :])
            const(fg[0:KD[k], k:k + 1], a["f1_g"][P * k:P * k + KD[k]].rearrange("(p o) -> p o", o=1))
            const(fb[0:KD[k], k:k + 1], a["f1_b"][P * k:P * k + KD[k]].rearrange("(p o) -> p o", o=1))
            const(wv[0:KD[k], k, :], a["in_wT"][P * k:P * k + KD[k], 2 * D:3 * D])
            const(ow[0:KD[k], k, :], a["out_wT"][P * k:P * k + KD[k], :])
            for c in range(3):
                for w in range(2):
                    const(wqk[0:KD[k], k, 2 * c + w, :, 0:HD],
                          a["in_wT"][P * k:P * k + KD[k], w * D + 64 * c:w * D + 64 * c + 64]
                          .rearrange("p (j e) -> p j e", e=HD))
        const(wva[64:65, 1, :], a["bv"].rearrange("(o d) -> o d", o=1))
        for j in range(4):
            const(qkb[32 * j:32 * j + HD, :], a["qk_b"][j, :, :])
        const(vb[:, :], bc(a["in_b"][2 * D:3 * D], P))
        const(ob[:, :], bc(a["out_b"], P))
        assert count[0] == NCONST, count

        def store_tile(i, src, dst, done):
            sp.dma_start(dst[bass.ds(2 * i, 2), NIMG:S, :].rearrange("b p d -> p b d"), src[:, 0:2, :]).then_inc(done, 16)
            for b in range(2):
                sp.dma_start(dst[bass.ds(2 * i + b, 1), 0:NIMG, :].rearrange("o n d -> (o n) d"),
                             src[64 * b:64 * b + NIMG, 2, :]).then_inc(done, 16)

        def pair(i, more):
            sp.wait_ge(h1_ready, i + 1)
            store_tile(i, H1, h1d, h1_stored)
            if more:
                load_pair(i + 1)

        def x1_store(i):
            sp.wait_ge(x1_ready, i + 1)
            store_tile(i, X1, x1d, x1_stored)

        pair(0, True)
        with sp.Fori(0, PAIRS - 2) as i:
            pair(i + 1, True)
            x1_store(i)
        pair(PAIRS - 1, False)
        x1_store(PAIRS - 2)
        x1_store(PAIRS - 1)

        nvec = [0]

        def vec(dst, src):
            sp.dma_start(dst, src).then_inc(vec_in, 16)
            nvec[0] += 1

        sp.wait_ge(phase_done, 4)
        sp.wait_ge(h1_stored, PAIRS * 48 + 1)
        sp.wait_ge(x1_stored, PAIRS * 48 + 1)

        def load_raw(f):
            s = raw_in[f % 2]
            w1 = a["mlp_w1"] if f == 0 else a["exp_w1"][f - 1]
            w2 = a["mlp_w2"] if f == 0 else a["exp_w2"][f - 1]
            sp.dma_start(rw1[:, f % 2, 0, :], w1[0:P, :]).then_inc(s, 16)
            for r in range(2):
                sp.dma_start(rw1[64 * r:64 * r + 64, f % 2, 1, :], w1[P:D, :]).then_inc(s, 16)
            sp.dma_start(rw2[:, f % 2, :, :], w2.rearrange("(k p) d -> p k d", p=P)).then_inc(s, 16)

        load_raw(0)
        vec(b1c[:, 0, :], a["mlp_b1"])
        vec(b1c[:, 1:NF, :], a["exp_b1"])
        for g, name in ((g2c, "f2_g"), (b2c, "f2_b")):
            vec(g[:, 0:1], a[name][0:P].rearrange("(p o) -> p o", o=1))
            for r in range(2):
                vec(g[64 * r:64 * r + 64, 1:2], a[name][P:D].rearrange("(p o) -> p o", o=1))
        vec(rb2[0:1, 0, :], a["mlp_b2"].rearrange("(o d) -> o d", o=1))
        vec(rb2[0:1, 1:NF, :], a["exp_b2"].rearrange("(o e) d -> o e d", o=1))
        vec(gwf[:, 0, :], a["gate_wT"][0:P, :])
        for r in range(2):
            vec(gwf[64 * r:64 * r + 64, 1, :], a["gate_wT"][P:D, :])
        vec(gbb[:, :], bc(a["gate_b"], P))
        load_raw(1)
        for f in range(2, NF):
            sp.wait_ge(lo_ready, f - 1)
            sp.wait_ge(bias_ps, f - 1)
            load_raw(f)

        def load_group(n):
            rows = lambda t: t.rearrange("b s d -> (b s) d")[bass.ds(n * GT, GT), :].rearrange("(a p) d -> p a d", p=TB)
            sp.dma_start(X[:, :, :], rows(x1d)).then_inc(x_in, 16)
            sp.dma_start(HH[:, :, :], rows(h1d)).then_inc(x_in, 16)

        def store_group(n):
            sp.dma_start(out.rearrange("b s d -> (b s) d")[bass.ds(n * GT, GT), :].rearrange("(a p) d -> p a d", p=TB),
                         ACC[:, :, :]).then_inc(out_stored, 16)

        sp.wait_ge(lo_ready, NF)
        sp.wait_ge(bias_ready, 2)
        load_group(0)
        with sp.Fori(0, GROUPS - 1) as n:
            sp.wait_ge(acc_init, n + 1)
            load_group(n + 1)
            sp.wait_ge(out_ready, n + 1)
            store_group(n)
        sp.wait_ge(out_ready, GROUPS)
        store_group(GROUPS - 1)
        sp.wait_ge(out_stored, GROUPS * 16 + 1)
        assert nvec[0] == NVEC, nvec

    @block.gpsimd
    def _(pool):
        nc.gpsimd.memset(XP[:, :], 0.0).then_inc(zeroed, 1)
        nc.gpsimd.memset(g2m[:, :], 0.0).then_inc(zeroed, 1)
        nc.gpsimd.memset(b2m[:, :], 0.0).then_inc(zeroed, 1)
        nc.gpsimd.memset(clsb[:, :], 0.0).then_inc(zeroed, 1)
        nc.gpsimd.memset(wqk[:, :, :, :, :], 0.0).then_inc(zeroed, 1)
        nc.gpsimd.memset(qkb[:, :], 0.0).then_inc(zeroed, 1)
        nc.gpsimd.memset(ident[:, :], 0.0).then_inc(ident_ready, 1)
        pool.wait_ge(ident_ready, 1)
        nc.gpsimd.affine_select(out=ident[:, :], in_=ident[:, :], compare_op=ALU.not_equal, fill=1.0, base=0,
                                pattern=[[-1, P]], channel_multiplier=1).then_inc(ident_ready, 1)
        nc.gpsimd.memset(eps_half[:, :], -0.5).then_inc(pool_step, 1)
        nc.gpsimd.memset(XA[:, :, D:DA], 1.0).then_inc(pool_step, 1)
        nc.gpsimd.memset(VX[:, :, :, :, HD:HD + 1], 1.0).then_inc(pool_step, 1)
        nc.gpsimd.memset(VX[:, :, :, :, HD + 1:32], 0.0)
        nc.gpsimd.memset(PX[:, :, :, S:NTXT + 64], 0.0).then_inc(pool_step, 1)
        pool.wait_ge(pool_step, 4)
        pool.wait_ge(attn_const_ready, 1)

        def rstd(base, k, n):
            pool.wait_ge(var_ready, base + k)
            nc.gpsimd.tensor_tensor(rs[:, k - 1, 0:n], ve[:, k - 1, 0:n], eps_half[:, 0:n], ALU.pow).then_inc(rstd_ready, 1)

        def pre(j, x1_before):
            for k, n in ((1, 1), (2, 1), (3, 3), (4, 3), (5, 3)):
                rstd(j * 5, k, n)
            pool.wait_ge(u_ready, j + 1)
            if x1_before is not None:
                pool.wait_ge(x1_ready, x1_before)
            for t in range(3):
                last = nc.gpsimd.tensor_tensor(UB[:, t, :], U[:, t, :], ob[:, :], ALU.add)
            last.then_inc(ub_ready, 1)

        pre(0, None)
        with pool.Fori(0, PAIRS - 1) as i:
            pre(i + 1, i + 1)
        pool.wait_ge(x1_ready, PAIRS)
        nc.gpsimd.memset(onesf[:, :], 1.0).then_inc(phase_done, 1)
        nc.gpsimd.memset(tri[:, :, :], 1.0).then_inc(pool_step, 1)
        pool.wait_ge(pool_step, 5)
        nc.gpsimd.affine_select(out=tri[:, :, :], in_=tri[:, :, :], compare_op=ALU.is_gt, fill=0.0, base=0,
                                pattern=[[1, NE], [-1, NE]], channel_multiplier=0).then_inc(pool_step, 1)
        pool.wait_ge(pool_step, 6)
        with pool.Fori(0, GROUPS) as n:
            pool.wait_ge(var2_ready, n + 1)
            nc.gpsimd.tensor_tensor(rs2[:, :], ve2[:, :], eps_half[0:TB, 0:TG], ALU.pow).then_inc(rstd2_ready, 1)
            pool.wait_ge(out_stored, n * 16 + 1)
            nc.gpsimd.tensor_tensor(ACC[:, :, :], X2[:, :, :], HH[:, :, :], ALU.add).then_inc(acc_init, 1)

    @block.scalar
    def _(act):
        def copy(dst, src, scale=1.0):
            return nc.scalar.activation(dst, src, ACT.Copy, scale=scale)

        act.wait_ge(setup_ps, 1)
        copy(AT[:, 0, :], PS[:, 0, 0:DA], float(D) ** -0.5)
        copy(AT[0:65, 1, :], PS[0:65, 0, DA:2 * DA], float(D) ** -0.5).then_inc(setup_act, 1)
        act.wait_ge(setup_ps, 4)
        copy(vbT[:, 0, :], PS[:, 5, 0:P])
        copy(vbT[0:64, 1, :], PS[0:64, 5, P:2 * P]).then_inc(setup_act, 1)

        def transposed(dst, bank, rows, ready):
            copy(dst[:, 0, :, :], PS[:, bank, 0:2 * D].rearrange("p (b c) -> p b c", b=2))
            copy(dst[0:rows, 1, :, :], PS[0:rows, bank + 1, 0:2 * D].rearrange("p (b c) -> p b c", b=2)).then_inc(ready, 1)

        def exps(i, u):
            act.wait_ge(max_ready, i * 6 + u + 1)
            if u >= 2:
                act.wait_ge(probT_ps, i * 18 + 3 * (u - 2) + 3)
            for c in range(3):
                for r in range(2):
                    to = r * (NTXT + 64)
                    last = nc.scalar.activation(PX[:, u % 2, c, to:to + S], PS[:, 2 * (u % 2) + r, c * S:(c + 1) * S], ACT.Exp,
                                                bias=nb[:, u, 3 * r + c:3 * r + c + 1], scale=HEAD_SCALE)
            last.then_inc(prob_ready, 1)

        def probsT(i, *gs):
            for g in gs:
                act.wait_ge(probT_ps, i * 18 + g + 1)
                copy(*probT_views(g)).then_inc(probT_act_ready, 1)

        def xnT(j):
            act.wait_ge(xnT_ps, j + 1)
            copy(XNT[:, 0:4, :], PS[:, 6, :].rearrange("p (k c) -> p k c", k=4))
            copy(XNT[:, 4:6, :], PS[:, 7, 0:2 * P].rearrange("p (k c) -> p k c", k=2)).then_inc(xnT_ready, 1)

        def xaT(j):
            act.wait_ge(xaT_ps, j + 1)
            transposed(XAT, 6, 65, xaT_ready)

        def lin_mat(j, step):
            dst, w = ((GS, DA), (T1, D), (PM, D))[step]
            for b in range(2):
                act.wait_ge(lin_mat_ps, j * 6 + 2 * step + b + 1)
                copy(dst[:, b, 0, 0:w], PS[:, 6 + b, 0:w])
                copy(dst[0:65, b, 1, 0:w], PS[0:65, 6 + b, w:2 * w]).then_inc(lin_mat_ready, 1)

        def zT(j):
            act.wait_ge(zT_ps, j + 1)
            transposed(ZT, 6, 64, zT_ready)

        def qk(j, ms):
            for m in ms:
                act.wait_ge(qk_ps, j * 6 + m + 1)
                src = PS[:, 6 + m % 2, 0:2 * D].rearrange("p (b c) -> p b c", b=2)
                if m % 2 == 0:
                    for r in range(2):
                        last = nc.scalar.activation(Q[:, m // 2, r, :, :], src, ACT.Identity, bias=qb[:, m // 2, r:r + 1],
                                                    scale=parity[:, r:r + 1])
                else:
                    last = nc.scalar.activation(K[:, m // 2, :, :], src, ACT.Identity, bias=qkb[:, m:m + 1], scale=1.0)
                last.then_inc(qk_ready, 1)

        def contextsT(i, b):
            act.wait_ge(ctxT_ps, i * 2 + b + 1)
            src = PS[:, 2 * b, 0:2 * D].rearrange("p (c q) -> p c q", c=2)
            copy(CT[:, 0:2, P * b:P * b + P], src[:, :, 0:P])
            copy(CT[:, 0:2, 2 * P + 64 * b:2 * P + 64 * b + 64], src[:, :, P:D]).then_inc(ctxT_ready, 1)

        def normedT(i):
            act.wait_ge(cnT_ps, i + 1)
            copy(CNT[:, 0, :], PS[:, 0, 0:3 * P])
            copy(CNT[0:64, 1, :], PS[0:64, 1, 0:3 * P]).then_inc(cnT_ready, 1)

        def body(i, j):
            core, pre = i is not None, j is not None
            core and exps(i, 0)
            pre and xnT(j)
            core and probsT(i, 1)
            core and exps(i, 1)
            core and exps(i, 2)
            core and probsT(i, 3)
            core and probsT(i, 5, 7)
            core and exps(i, 3)
            core and probsT(i, 9)
            pre and xaT(j)
            core and probsT(i, 11)
            core and exps(i, 4)
            pre and lin_mat(j, 0)
            pre and lin_mat(j, 1)
            pre and lin_mat(j, 2)
            core and exps(i, 5)
            core and probsT(i, 13)
            core and contextsT(i, 0)
            core and probsT(i, 15, 17)
            core and contextsT(i, 1)
            pre and zT(j)
            pre and qk(j, (0, 1))
            core and normedT(i)
            pre and qk(j, (2, 3, 4, 5))

        body(None, 0)
        with act.Fori(0, PAIRS - 1) as i:
            body(i, i + 1)
        body(PAIRS - 1, None)

        act.wait_ge(x1_ready, PAIRS)
        nc.scalar.activation(ones33[:, :], ident[0:33, 0:TB], ACT.Copy, scale=0.0, bias=1.0).then_inc(phase_done, 1)
        act.wait_ge(vec_in, NVEC * 16)
        act.wait_ge(phase_done, 4)
        for f in range(NF):
            act.wait_ge(raw_in[f % 2], (f // 2 + 1) * 64)
            for k in range(2):
                nc.scalar.activation(w1r[:, f, 2 * k, :], rw1[:, f % 2, k, :], ACT.Copy, scale=(g2c[:, k:k + 1] if f else 1.0))
            copy(w2r[:, f, :, 0:D], rw2[:, f % 2, :, :]).then_inc(hi_ready, 1)

        def split_high(i, q):
            act.wait_ge(actT_ps, i * 2 + q + 1)
            copy(XH[:, :], PS[:, 0, 0:GT])
            copy(XS[0:64, :], PS[0:64, 1, 0:GT]).then_inc(actT_hi, 1)

        def gelus(n, slot):
            for m in range(KH):
                q = slot * KH + m
                act.wait_ge(up_ps, n * (NF * KH) + q + 1)
                act.wait_ge(hid_ready, n * (NF * KH) + q + 1)
                nc.scalar.activation(GF[:, q % 3, :], PS[:, 2 + q % 2, 0:GT], ACT.Gelu,
                                     bias=b1c[:, slot, m:m + 1], scale=1.0).then_inc(gelu_ready, 1)

        with act.Fori(0, GROUPS) as n:
            split_high(n, 0)
            gelus(n, 0)
            split_high(n, 1)
            act.wait_ge(ldiff_ready, n + 1)
            nc.scalar.activation(lex[:, :, :], ldf[:, :, :], ACT.Exp).then_inc(lexp_ready, 1)
            for slot in range(1, NF):
                gelus(n, slot)

    @block.vector
    def _(dve):
        steps = Steps(dve_step, dve)
        tt, ts, cp = nc.vector.tensor_tensor, nc.vector.tensor_scalar, nc.vector.tensor_copy
        stt = nc.vector.scalar_tensor_tensor

        for j in range(4):
            for r in range(2):
                last = nc.vector.memset(parity[32 * j:32 * j + 32, r:r + 1], float(j % 2 == r))
        steps.link(last)
        dve.wait_ge(const_in, NCONST * 16)
        cp(lnp_rep[:, :, :], lnp_b[:, :].unsqueeze(2).to_broadcast([P, KP, P]))
        cp(fb_rep[:, 0, :], fb[:, 0:1].to_broadcast([P, P]))
        cp(fb_rep[0:64, 1, :], fb[0:64, 1:2].to_broadcast([64, P])).then_inc(setup_dve, 1)
        tt(b2m[:, :], b2m[:, :], clsb[:, :], ALU.add)
        dve.wait_ge(setup_ps, 3)
        tt(lin_bias[:, :], lin_bias[:, :], PS[:, 2, 0:D], ALU.add)
        tt(qkb[:, :], qkb[:, :], PS[:, 3, 0:6], ALU.add)
        tt(vb[:, :], vb[:, :], PS[:, 4, 0:D], ALU.add).then_inc(setup_dve, 1)
        for k in range(KP):
            ts(wlin[:, k, :], wlin[:, k, :], lnp_g[:, k:k + 1], None, ALU.mult)
        for k in range(2):
            r = KD[k]
            ts(wqk[0:r, k, :, :, :], wqk[0:r, k, :, :, :], fg[0:r, k:k + 1], None, ALU.mult)
            ts(wv[0:r, k, :], wv[0:r, k, :], fg[0:r, k:k + 1], None, ALU.mult)
        dve.wait_ge(setup_ps, 5)
        steps.link(tt(ob[:, :], ob[:, :], PS[:, 6, 0:D], ALU.add))
        dve.wait_ge(pool_step, 4)
        tt(qb[:, :, :], qkb[:, :].rearrange("p (c w) -> p c w", w=2)[:, :, 0:1].to_broadcast([P, 3, 2]),
           parity[:, :].unsqueeze(1).to_broadcast([P, 3, 2]), ALU.mult)
        nc.vector.memset(mx[:, 0, 0:1], 0.0).then_inc(h1_stored, 1)
        nc.vector.memset(mx[:, 0, 1:2], 0.0).then_inc(x1_stored, 1)
        nc.vector.memset(mx[:, 0, 2:3], 0.0).then_inc(attn_const_ready, 1)
        setup_steps = steps.k

        def stats(j, k, src, n, wide=False):
            for t in range(2 if wide else n):
                last = nc.vector.bn_stats(st[:, k - 1, t, :], src(t))
            steps.link_aggregate(last, pad[:, 0:1])
            for t in range(n):
                last = nc.vector.bn_aggr(mv[:, k - 1, t, :], st[:, k - 1, 0:2, :] if wide else st[:, k - 1, t, :])
            steps.link(last)
            ts(ve[:, k - 1, 0:n], mv[:, k - 1, 0:n, 1], EPS, None, ALU.add).then_inc(var_ready, 1)

        def normed(j, k, src, dst, n):
            dve.wait_ge(rstd_ready, j * 5 + k)
            for t in range(n):
                last = ts(dst(t), src(t), mv[:, k - 1, t, 0:1], rs[:, k - 1, t:t + 1], ALU.subtract, ALU.mult)
            return last

        def patch_stats(j):
            dve.wait_ge(patches_in, j * 32 + 32)
            stats(j, 1, lambda c: XP[:, c * PD // 2:(c + 1) * PD // 2], 1, True)

        def patch_normed(j):
            normed(j, 1, lambda t: XP[:, :], lambda t: XN[:, :], 1).then_inc(xn_ready, 1)

        def token_stats(j):
            dve.wait_ge(tok_ps, j + 1)
            steps.link(tt(Y[:, :], PS[:, 6, 0:D], lin_bias[:, :], ALU.add))
            stats(j, 2, lambda t: Y[:, :], 1)

        def tokens(j):
            dve.wait_ge(rstd_ready, j * 5 + 2)
            steps.link(stt(Y2[:, :], Y[:, :], mv[:, 1, 0, 0:1], g2m[:, :], ALU.subtract, ALU.mult))
            steps.link(stt(H[:, 2, :], Y2[:, :], rs[:, 1, 0:1], b2m[:, :], ALU.mult, ALU.add))
            dve.wait_ge(txt_in, j * 16 + 16)
            stats(j, 3, lambda t: H[:, t, :], 3)

        def lin_in(j):
            normed(j, 3, lambda t: H[:, t, :], lambda t: XA[:, t, 0:D], 3).then_inc(xa_ready, 1)

        def lin_out(j):
            dve.wait_ge(lin_ps, j + 1)
            dve.wait_ge(h1_stored, j * 48 + 1)
            tt(H1[:, 0:2, :], PS[:, 6, 0:2 * D].rearrange("p (t d) -> p t d", t=2), H[:, 0:2, :], ALU.add)
            tt(H1[:, 2, :], PS[:, 7, 0:D], H[:, 2, :], ALU.add).then_inc(h1_ready, 1)
            dve.wait_ge(h1_ready, j + 1)
            stats(j, 4, lambda t: H1[:, t, :], 3)

        def u_stats(j, ub_before):
            if ub_before is not None:
                dve.wait_ge(ub_ready, ub_before)
            normed(j, 4, lambda t: H1[:, t, :], lambda t: U[:, t, :], 3).then_inc(u_ready, 1)
            dve.wait_ge(u_ready, j + 1)
            stats(j, 5, lambda t: U[:, t, :], 3)

        def z_out(j):
            normed(j, 5, lambda t: U[:, t, :], lambda t: Z[:, t, :], 3).then_inc(z_ready, 1)

        def values(j):
            dve.wait_ge(v_ps, j + 1)
            cp(VX[:, 0, :, :, 0:HD], PS[:, 6, 0:2 * D].rearrange("p (b h e) -> p b h e", b=2, h=NH))
            for r in range(2):
                dst = VX[64 * r:64 * r + NIMG, 1, :, :, 0:HD].rearrange("p b (g r) e -> p (b g) r e", r=2)[:, :, r, :]
                src = PS[0:NIMG, 7, 0:2 * D].rearrange("p (g r e) -> p g r e", r=2, e=HD)[:, :, r, :]
                last = cp(dst, src)
            last.then_inc(v_ready, 1)

        def maxima(i, u):
            dve.wait_ge(score_ps, i * 6 + u + 1)
            src = PS[:, 2 * (u % 2):2 * (u % 2) + 2, 0:3 * S].rearrange("p a (s k) -> p a s k", s=3)
            steps.link(nc.vector.tensor_reduce(mx[:, u, :].rearrange("p (a s) -> p a s", a=2), src, AX_X, ALU.max))
            ts(nb[:, u, :], mx[:, u, :], -HEAD_SCALE, None, ALU.mult).then_inc(max_ready, 1)

        def probsT(i, *gs):
            for g in gs:
                dve.wait_ge(probT_ps, i * 18 + g + 1)
                cp(*probT_views(g)).then_inc(probT_dve_ready, 1)

        def contextsT(i):
            dve.wait_ge(ctxT_ps, i * 2 + 2)
            src = PS[:, 1, 0:2 * D].rearrange("p (b q) -> p b q", b=2)
            cp(CT[:, 2, 0:2 * P].rearrange("p (b q) -> p b q", b=2), src[:, :, 0:P])
            cp(CT[:, 2, 2 * P:3 * P].rearrange("p (b q) -> p b q", b=2), src[:, :, P:D]).then_inc(ctxT2_ready, 1)

        def contexts(i):
            for t in range(3):
                dve.wait_ge(ctx_ps, i * 3 + t + 1)
                src = PS[:, 3 + t, 0:NH * 32].rearrange("p (h e) -> p h e", h=NH)
                steps.link(nc.vector.reciprocal(rec[:, t, :], src[:, :, HD]))
                tt(CN[:, t, :].rearrange("p (h e) -> p h e", h=NH), src[:, :, 0:HD],
                   rec[:, t, :].unsqueeze(2).to_broadcast([P, NH, HD]), ALU.mult).then_inc(ctx_ready, 1)

        def x1_out(i):
            dve.wait_ge(proj_ps, i + 1)
            dve.wait_ge(ub_ready, i + 1)
            dve.wait_ge(x1_stored, i * 48 + 1)
            tt(X1[:, 0:2, :], PS[:, 2, 0:2 * D].rearrange("p (t d) -> p t d", t=2), UB[:, 0:2, :], ALU.add)
            tt(X1[:, 2, :], PS[:, 3, 0:D], UB[:, 2, :], ALU.add).then_inc(x1_ready, 1)

        def body(i, j):
            core, pre = i is not None, j is not None
            pre and patch_stats(j)
            core and maxima(i, 0)
            pre and patch_normed(j)
            core and values(i)
            core and maxima(i, 1)
            core and probsT(i, 0)
            core and maxima(i, 2)
            core and probsT(i, 2)
            pre and token_stats(j)
            core and probsT(i, 4)
            pre and tokens(j)
            core and maxima(i, 3)
            core and probsT(i, 6)
            pre and lin_in(j)
            core and probsT(i, 8)
            core and maxima(i, 4)
            core and probsT(i, 10)
            pre and lin_out(j)
            core and maxima(i, 5)
            core and probsT(i, 12)
            pre and u_stats(j, j if core else None)
            core and probsT(i, 14)
            pre and z_out(j)
            core and probsT(i, 16)
            core and contextsT(i)
            core and contexts(i)
            core and x1_out(i)

        body(None, 0)
        before = steps.base + steps.k
        N_STEPS = 22
        with dve.Fori(0, PAIRS - 1) as i:
            steps.at(before + i * N_STEPS)
            body(i, i + 1)
            assert steps.k == N_STEPS, steps.k
        steps.at(before + (PAIRS - 1) * N_STEPS)
        body(PAIRS - 1, None)
        steps.at(steps.base + steps.k)

        dve.wait_ge(x1_stored, PAIRS * 48 + 1)
        dve.wait_ge(h1_stored, PAIRS * 48 + 1)
        steps.link(nc.vector.memset(b2r[:, :, :].bitcast(F32), 0.0))
        cp(comb[:, 0, 0:1], ident[0:TB, 0:1]).then_inc(phase_done, 2)
        dve.wait_ge(phase_done, 4)
        dve.wait_ge(vec_in, NVEC * 16)
        steps.link(cp(b2r[0:1, :, :], rb2[:, :, :]))
        tt(b2r[32:33, :, :], rb2[:, :, :], b2r[0:1, :, :].bitcast(F32), ALU.subtract)
        cp(b2rep[:, :, :], b2c[:, :].unsqueeze(2).to_broadcast([P, 2, P])).then_inc(bias_ready, 1)
        for k in range(2):
            steps.link(ts(gwr[:, 2 * k, :], gwf[:, k, :], g2c[:, k:k + 1], None, ALU.mult))
            stt(gwr[:, 2 * k + 1, :], gwf[:, k, :], g2c[:, k:k + 1], gwr[:, 2 * k, :].bitcast(F32), ALU.mult, ALU.subtract)
        for f in range(NF):
            dve.wait_ge(hi_ready, f + 1)
            for k in range(2):
                hi = w1r[:, f, 2 * k, :].bitcast(F32)
                if f:
                    stt(w1r[:, f, 2 * k + 1, :], rw1[:, f % 2, k, :], g2c[:, k:k + 1], hi, ALU.mult, ALU.subtract)
                else:
                    tt(w1r[:, f, 2 * k + 1, :], rw1[:, f % 2, k, :], hi, ALU.subtract)
            tt(w2r[:, f, :, D:2 * D], rw2[:, f % 2, :, :], w2r[:, f, :, 0:D].bitcast(F32), ALU.subtract).then_inc(lo_ready, 1)
        dve.wait_ge(bias_ps, NE + 2)
        tt(b1c[:, 1:NF, :], b1c[:, 1:NF, :], PS[:, 0, 0:NE * KH].rearrange("p (e k) -> p e k", e=NE), ALU.add)
        tt(gbb[:, :], gbb[:, :], PS[:, 1, 0:NE], ALU.add).then_inc(bias_ready, 1)
        cp(den[:, 0:1], ident[0:TB, 0:1]).then_inc(hid_ready, 3)
        cp(den[:, 1:2], ident[0:TB, 0:1]).then_inc(gelu_ready, 2)
        cp(den[:, 2:3], ident[0:TB, 0:1]).then_inc(down_read, 4)
        cp(den[:, 3:4], ident[0:TB, 0:1]).then_inc(out_stored, 1)

        def split_low(n, q):
            dve.wait_ge(actT_hi, n * 2 + q + 1)
            tt(XL[:, :], PS[:, 0, 0:GT], XH[:, :].bitcast(F32), ALU.subtract)
            tt(XS[64:P, :], PS[0:64, 1, 0:GT], XS[0:64, :].bitcast(F32), ALU.subtract).then_inc(actT_ready, 1)

        def hidden(n, slot):
            for m in range(KH):
                q = slot * KH + m
                dve.wait_ge(gelu_ready, n * (NF * KH) + q + 1 + 2)
                steps.link(cp(GH[:, slot % 2, m, :], GF[:, q % 3, :]))
                tt(GL[:, slot % 2, m, :], GF[:, q % 3, :], GH[:, slot % 2, m, :].bitcast(F32), ALU.subtract).then_inc(hid_ready, 1)

        def accumulate(n, slot):
            for t in range(TG):
                dve.wait_ge(down_ps, n * (NF * TG) + slot * TG + t + 1)
                w = comb[:, t, slot - 1:slot]
                steps.link(stt(ACC[:, t, :], PS[0:TB, 4 + t, 0:D], w, ACC[:, t, :], ALU.mult, ALU.add))
                last = stt(ACC[:, t, :], PS[0:TB, 4 + t, D:2 * D], w, ACC[:, t, :], ALU.mult, ALU.add)
                last.then_inc(down_read, 1)
                if slot == NF - 1 and t == TG - 1:
                    dve.wait_ge(down_read, (n + 1) * (NF * TG) + 4)
                    cp(den[:, 0:1], den[:, 1:2]).then_inc(out_ready, 1)

        first = steps.base + steps.k
        N2 = 59
        with dve.Fori(0, GROUPS) as n:
            steps.at(first + n * N2)
            split_low(n, 0)
            hidden(n, 0)
            for t in range(TG):
                dve.wait_ge(down_ps, n * (NF * TG) + t + 1)
            steps.link(tt(X2[:, :, :], PS[0:TB, 4:8, 0:D], X[:, :, :], ALU.add))
            last = tt(X2[:, :, :], PS[0:TB, 4:8, D:2 * D], X2[:, :, :], ALU.add)
            steps.link(last)
            cp(den[:, 0:1], X2[:, 0, 0:1]).then_inc(down_read, 4)
            for t in range(TG):
                last = nc.vector.bn_stats(st2[:, t, :], X2[:, t, :])
            steps.link_aggregate(last, pad[:, 0:1])
            for t in range(TG):
                last = nc.vector.bn_aggr(mv2[:, t, :], st2[:, t, :])
            steps.link(last)
            ts(ve2[:, :], mv2[:, :, 1], EPS, None, ALU.add).then_inc(var2_ready, 1)
            dve.wait_ge(rstd2_ready, n + 1)
            for t in range(TG):
                last = ts(Z2[:, t, :], X2[:, t, :], mv2[:, t, 0:1], rs2[:, t:t + 1], ALU.subtract, ALU.mult)
            last.then_inc(z2_ready, 1)
            split_low(n, 1)
            dve.wait_ge(gate_ps, n + 1)
            steps.link(tt(lg[:, :, :], PS[0:TB, 1, 0:TG * NE].rearrange("p (t e) -> p t e", t=TG),
                          gbb[0:TB, :].unsqueeze(1).to_broadcast([TB, TG, NE]), ALU.add))
            nc.vector.tensor_reduce(top[:, :], lg[:, :, :], AX_X, ALU.max)
            for t in range(TG):
                lj = lg[:, t, :].unsqueeze(1).to_broadcast([TB, NE, NE])
                le = lg[:, t, :].unsqueeze(2).to_broadcast([TB, NE, NE])
                tt(gtm[:, t, :, :], lj, le, ALU.is_gt)
                last = tt(eqm[:, t, :, :], lj, le, ALU.is_equal)
            steps.link(last)
            tt(ldf[:, :, :], lg[:, :, :], top[:, :].unsqueeze(2).to_broadcast([TB, TG, NE]), ALU.subtract).then_inc(ldiff_ready, 1)
            steps.link(tt(eqm[:, :, :, :], eqm[:, :, :, :],
                          tri[0:TB, :, :].unsqueeze(1).to_broadcast([TB, TG, NE, NE]), ALU.mult))
            steps.link(tt(gtm[:, :, :, :], gtm[:, :, :, :], eqm[:, :, :, :], ALU.add))
            steps.link(nc.vector.tensor_reduce(rank[:, :, :], gtm[:, :, :, :], AX_X, ALU.add))
            dve.wait_ge(lexp_ready, n + 1)
            steps.link(stt(gex[:, :, :], rank[:, :, :], 2.0, lex[:, :, :], ALU.is_lt, ALU.mult))
            steps.link(nc.vector.tensor_reduce(den[:, :], gex[:, :, :], AX_X, ALU.add))
            steps.link(nc.vector.reciprocal(den[:, :], den[:, :]))
            steps.link(tt(comb[:, :, :], gex[:, :, :], den[:, :].unsqueeze(2).to_broadcast([TB, TG, NE]), ALU.mult))
            hidden(n, 1)
            hidden(n, 2)
            dve.wait_ge(acc_init, n + 1)
            accumulate(n, 1)
            hidden(n, 3)
            accumulate(n, 2)
            hidden(n, 4)
            accumulate(n, 3)
            accumulate(n, 4)
            assert steps.k == N2, steps.k

    @block.tensor
    def _(pe):
        def mm(o, l, r, start=True, stop=True):
            return nc.tensor.matmul(o, l, r, start=start, stop=stop)

        def tr(o, x, rows=P):
            return nc.tensor.transpose(o, x, ident[0:rows, 0:rows])

        pe.wait_ge(const_in, NCONST * 16)
        pe.wait_ge(ident_ready, 2)
        for m in range(2):
            for k in range(2):
                last = mm(PS[0:KA[m], 0, m * DA:(m + 1) * DA], wka[0:KD[k], k, P * m:P * m + KA[m]], wqa[0:KD[k], k, :], k == 0, k == 1)
        last.then_inc(setup_ps, 1)
        pe.wait_ge(setup_dve, 1)
        for k in range(KP):
            last = mm(PS[:, 2, 0:D], lnp_rep[:, k, :], wlin[:, k, :], k == 0, k == KP - 1)
        last.then_inc(setup_ps, 1)
        for m in range(6):
            for k in range(2):
                mm(PS[:, 3, m:m + 1], wqk[0:KD[k], k, m, :, :], fb[0:KD[k], k:k + 1], k == 0, k == 1)
        for k in range(2):
            last = mm(PS[:, 4, 0:D], fb_rep[0:KD[k], k, :], wv[0:KD[k], k, :], k == 0, k == 1)
        last.then_inc(setup_ps, 1)
        pe.wait_ge(setup_dve, 2)
        tr(PS[:, 5, 0:P], vb[:, 0:P])
        tr(PS[0:64, 5, P:2 * P], vb[:, P:D]).then_inc(setup_ps, 1)
        pe.wait_ge(setup_act, 2)
        for k in range(2):
            last = mm(PS[:, 6, 0:D], vbT[0:KD[k], k, :], ow[0:KD[k], k, :], k == 0, k == 1)
        last.then_inc(setup_ps, 1)
        pe.wait_ge(attn_const_ready, 1)

        def transpose_set(x, bank, rows, ps):
            for k in range(2):
                w = rows[k]
                o = PS[0:w, bank + k, 0:2 * D].rearrange("p (b c) -> p b c", b=2)
                for b in range(2):
                    tr(o[:, b, 0:P], x[:, b, P * k:P * k + w])
                last = tr(o[:, :, P:D], x[:, 2, P * k:P * k + w])
            last.then_inc(ps, 1)

        def scores(i, u):
            t = TILE_OF[u // 2]
            if u == 0:
                pe.wait_ge(qk_ready, i * 6 + 6)
            if u == 1:
                pe.wait_ge(max_ready, i * 6 + 1)
            for c in range(3):
                for r in range(2):
                    rows = slice(64 * (u % 2), 64 * (u % 2) + 64)
                    bank, col = 2 * (u % 2) + r, c * S
                    q, k = Q[rows, c, r, :, :], K[rows, c, :, :]
                    spans = ((0, 0, S),) if r == 0 else ((0, P, NIMG), (NIMG, 0, NTXT))
                    for at, key, n in spans:
                        if t < 2:
                            last = mm(PS[:, bank, col + at:col + at + n], q[:, t, 0:P], k[:, t, key:key + n])
                        else:
                            for b in range(2):
                                last = mm(PS[64 * b:64 * b + 64, bank, col + at:col + at + n], q[:, b, P:D], k[:, b, key:key + n])
            last.then_inc(score_ps, 1)

        def transpose_probs(i, u, cs=range(3)):
            for c in cs:
                g = 3 * u + c
                if c == 0:
                    pe.wait_ge(prob_ready, i * 6 + u + 1)
                if g >= 2:
                    if g % 2:
                        pe.wait_ge(probT_act_ready, i * 9 + g // 2)
                    else:
                        pe.wait_ge(probT_dve_ready, i * 9 + g // 2)
                for slot, col in enumerate((0, PXW - NTXT, NTXT)):
                    last = tr(PS[:, 4 + g % 2, P * slot:P * slot + P], PX[:, u % 2, c, col:col + P])
                last.then_inc(probT_ps, 1)

        def patches_T(j, core):
            pe.wait_ge(xn_ready, j + 1)
            if core:
                pe.wait_ge(v_ready, j)
            for k in range(KP):
                last = tr(PS[:, 6 + k // 4, P * (k % 4):P * (k % 4) + P], XN[:, P * k:P * k + P])
            last.then_inc(xnT_ps, 1)

        def patch_tokens(j):
            pe.wait_ge(xnT_ready, j + 1)
            for k in range(KP):
                last = mm(PS[:, 6, 0:D], XNT[:, k, :], wlin[:, k, :], k == 0, k == KP - 1)
            last.then_inc(tok_ps, 1)

        def tokens_T(j):
            pe.wait_ge(xa_ready, j + 1)
            transpose_set(XA, 6, KA, xaT_ps)

        def lin_gram(j):
            pe.wait_ge(xaT_ready, j + 1)
            for b in range(2):
                for m in range(2):
                    o = PS[0:KA[m], 6 + b, m * DA:(m + 1) * DA]
                    mm(o, XA[:, b, P * m:P * m + KA[m]], XA[:, b, :], True, False)
                    last = mm(o, XA[64 * b:64 * b + NIMG, 2, P * m:P * m + KA[m]], XA[64 * b:64 * b + NIMG, 2, :], False, True)
                last.then_inc(lin_mat_ps, 1)

        def lin_product(j, step):
            for b in range(2):
                pe.wait_ge(lin_mat_ready, j * 6 + 2 * step + b + 1)
                for m in range(2):
                    for k in range(2):
                        l = (GS[0:KA[k], b, k, P * m:P * m + KA[m]], AT[0:KA[k], k, P * m:P * m + KA[m]])[step]
                        r = (wva[0:KA[k], k, :], T1[0:KA[k], b, k, :])[step]
                        last = mm(PS[0:KA[m], 6 + b, m * D:(m + 1) * D], l, r, k == 0, k == 1)
                last.then_inc(lin_mat_ps, 1)

        def lin_tokens(j):
            pe.wait_ge(lin_mat_ready, j * 6 + 6)
            for b in range(2):
                for k in range(2):
                    mm(PS[:, 6, b * D:(b + 1) * D], XAT[0:KA[k], k, b, 0:P], PM[0:KA[k], b, k, :], k == 0, k == 1)
                for k in range(2):
                    last = mm(PS[64 * b:64 * b + 64, 7, 0:D], XAT[0:KA[k], k, b, P:D], PM[0:KA[k], b, k, :], k == 0, k == 1)
            last.then_inc(lin_ps, 1)

        def z_T(j):
            pe.wait_ge(z_ready, j + 1)
            transpose_set(Z, 6, KD, zT_ps)

        def queries_keys(j, ms):
            for m in ms:
                if m == 0:
                    pe.wait_ge(zT_ready, j + 1)
                if m >= 2:
                    pe.wait_ge(qk_ready, j * 6 + m - 1)
                for k in range(2):
                    last = mm(PS[:, 6 + m % 2, 0:2 * D], wqk[0:KD[k], k, m, :, :], ZT[0:KD[k], k, :, :], k == 0, k == 1)
                last.then_inc(qk_ps, 1)

        def values(j):
            pe.wait_ge(qk_ready, j * 6 + 6)
            for b in range(2):
                for k in range(2):
                    mm(PS[:, 6, b * D:(b + 1) * D], ZT[0:KD[k], k, b, 0:P], wv[0:KD[k], k, :], k == 0, k == 1)
                for k in range(2):
                    last = mm(PS[0:NIMG, 7, b * D:(b + 1) * D], ZT[0:KD[k], k, b, P:P + NIMG], wv[0:KD[k], k, :], k == 0, k == 1)
            last.then_inc(v_ps, 1)

        def contexts_T(i, b):
            if b == 0:
                pe.wait_ge(v_ready, i + 1)
            pe.wait_ge(probT_act_ready, i * 9 + (6, 9)[b])
            pe.wait_ge(probT_dve_ready, i * 9 + (6, 9)[b])
            for c in range(3):
                bank, col = (2 * b, c * D) if c < 2 else (1, b * D)
                for k in range(2):
                    for j in range(4):
                        half, r = j // 2, j % 2
                        rows = slice(0, P) if k == 0 else slice(64 * r, 64 * r + NIMG)
                        last = mm(PS[32 * j:32 * j + 32, bank, col:col + D], VX[rows, k, b, 4 * c + j, :],
                                  PT[rows, 3 * half + c, r if k == 0 else 2, D * b:D * b + D], k == 0, k == 1)
            last.then_inc(ctxT_ps, 1)

        def contexts(i):
            pe.wait_ge(ctxT_ready, i * 2 + 2)
            pe.wait_ge(ctxT2_ready, i + 1)
            for t in range(3):
                for c in range(3):
                    last = tr(PS[:, 3 + t, P * c:P * c + P], CT[:, c, P * t:P * t + P])
                last.then_inc(ctx_ps, 1)

        def normed_T(i):
            for t in range(3):
                pe.wait_ge(ctx_ready, i * 3 + t + 1)
                for k in range(2):
                    last = tr(PS[0:KD[k], k, P * t:P * t + P], CN[:, t, P * k:P * k + KD[k]])
            last.then_inc(cnT_ps, 1)

        def project(i):
            pe.wait_ge(cnT_ready, i + 1)
            for t in range(3):
                o = PS[:, 2, t * D:(t + 1) * D] if t < 2 else PS[:, 3, 0:D]
                for k in range(2):
                    last = mm(o, CNT[0:KD[k], k, P * t:P * t + P], ow[0:KD[k], k, :], k == 0, k == 1)
            last.then_inc(proj_ps, 1)

        def body(i, j):
            core, pre = i is not None, j is not None
            core and scores(i, 0)
            core and values(i)
            core and scores(i, 1)
            pre and patches_T(j, core)
            core and transpose_probs(i, 0, (0, 1))
            core and scores(i, 2)
            core and transpose_probs(i, 0, (2,))
            pre and patch_tokens(j)
            core and transpose_probs(i, 1, (0, 1))
            core and scores(i, 3)
            core and transpose_probs(i, 1, (2,))
            core and transpose_probs(i, 2, (0, 1))
            core and scores(i, 4)
            core and transpose_probs(i, 2, (2,))
            core and transpose_probs(i, 3, (0, 1))
            pre and tokens_T(j)
            core and transpose_probs(i, 3, (2,))
            pre and lin_gram(j)
            pre and lin_product(j, 0)
            pre and lin_product(j, 1)
            pre and lin_tokens(j)
            core and scores(i, 5)
            core and transpose_probs(i, 4)
            core and contexts_T(i, 0)
            core and transpose_probs(i, 5)
            core and contexts_T(i, 1)
            pre and z_T(j)
            core and contexts(i)
            pre and queries_keys(j, (0, 1))
            core and normed_T(i)
            pre and queries_keys(j, (2, 3, 4, 5))
            core and project(i)

        body(None, 0)
        with pe.Fori(0, PAIRS - 1) as i:
            body(i, i + 1)
        body(PAIRS - 1, None)

        pe.wait_ge(phase_done, 4)
        pe.wait_ge(bias_ready, 1)
        for f in range(NF):
            pe.wait_ge(raw_in[f % 2], (f // 2 + 1) * 64)
            if f == 0:
                for k in range(2):
                    last = mm(PS[:, 1, 0:NE], b2rep[0:KD[k], k, :], gwf[0:KD[k], k, :], k == 0, k == 1)
                last.then_inc(bias_ps, 1)
                continue
            for m in range(KH):
                c = (f - 1) * KH + m
                for k in range(2):
                    last = mm(PS[:, 0, c:c + 1], rw1[0:KD[k], f % 2, k, P * m:P * m + P], b2c[0:KD[k], k:k + 1], k == 0, k == 1)
            last.then_inc(bias_ps, 2 if f == NF - 1 else 1)
        pe.wait_ge(lo_ready, NF)
        pe.wait_ge(bias_ready, 2)
        pe.wait_ge(out_stored, 1)

        def transpose_group(x, ps):
            for t in range(TG):
                for k in range(2):
                    last = tr(PS[0:KD[k], k, TB * t:TB * t + TB], x[:, t, P * k:P * k + KD[k]], TB)
            last.then_inc(ps, 1)

        def up(n, slot):
            for m in range(KH):
                q = slot * KH + m
                o = PS[:, 2 + q % 2, 0:GT]
                w = w1r[:, slot, :, P * m:P * m + P]
                pe.wait_ge(gelu_ready, n * (NF * KH) + q + 1)
                mm(o, w[:, 0, :], XH[:, :], True, False)
                mm(o, w[:, 0, :], XL[:, :], False, False)
                mm(o, w[:, 1, :], XH[:, :], False, False)
                mm(o, w[:, 2, :], XS[:, :], False, False)
                mm(o, w[0:64, 3, :], XS[0:64, :], False, True).then_inc(up_ps, 1)

        def down(n, slot):
            for t in range(TG):
                bank = PS[0:TB, 4 + t, :]
                if t == 0:
                    pe.wait_ge(hid_ready, n * (NF * KH) + (slot + 1) * KH + 3)
                pe.wait_ge(down_read, n * (NF * TG) + slot * TG + t + 1)
                for k in range(KH):
                    mm(bank[:, 0:2 * D], GH[:, slot % 2, k, TB * t:TB * t + TB], w2r[:, slot, k, :], k == 0, False)
                    mm(bank[:, 0:D], GL[:, slot % 2, k, TB * t:TB * t + TB], w2r[:, slot, k, 0:D], False, False)
                mm(bank[:, 0:D], ones33[:, :], b2r[:, slot, :], False, True).then_inc(down_ps, 1)

        with pe.Fori(0, GROUPS) as n:
            pe.wait_ge(x_in, n * 32 + 32)
            transpose_group(X, actT_ps)
            pe.wait_ge(actT_ready, n * 2 + 1)
            up(n, 0)
            down(n, 0)
            pe.wait_ge(z2_ready, n + 1)
            transpose_group(Z2, actT_ps)
            pe.wait_ge(actT_ready, n * 2 + 2)
            for t in range(TG):
                o = PS[0:TB, 1, NE * t:NE * t + NE]
                cols = slice(TB * t, TB * t + TB)
                mm(o, XH[:, cols], gwr[:, 0, :], True, False)
                mm(o, XL[:, cols], gwr[:, 0, :], False, False)
                mm(o, XH[:, cols], gwr[:, 1, :], False, False)
                mm(o, XS[:, cols], gwr[:, 2, :], False, False)
                last = mm(o, XS[0:64, cols], gwr[0:64, 3, :], False, True)
            last.then_inc(gate_ps, 1)
            up(n, 1)
            up(n, 2)
            down(n, 1)
            up(n, 3)
            down(n, 2)
            up(n, 4)
            down(n, 3)
            down(n, 4)

    ctx.close()


_RENAMED = {
    "txt": "txt", "lnp_g": "L0_tok_ln1_g", "lnp_b": "L0_tok_ln1_b", "W_lin": "L0_tok_W_lin", "b_lin": "L0_tok_b_lin",
    "ln2_g": "L0_tok_ln2_g", "ln2_b": "L0_tok_ln2_b", "pos": "L0_tok_pos_embedding", "cls": "L0_tok_cls_token",
    "Wq": "L0_attn_Wq", "bq": "L0_attn_bq", "Wk": "L0_attn_Wk", "bk": "L0_attn_bk", "bv": "L0_attn_bv",
    "f1_g": "L0_ffn_ln1_g", "f1_b": "L0_ffn_ln1_b", "in_b": "L0_ffn_in_b", "out_b": "L0_ffn_out_b",
    "mlp_w1": "L0_ffn_mlp_w1", "mlp_b1": "L0_ffn_mlp_b1", "mlp_w2": "L0_ffn_mlp_w2", "mlp_b2": "L0_ffn_mlp_b2",
    "f2_g": "L0_ffn_ln2_g", "f2_b": "L0_ffn_ln2_b", "gate_b": "L0_ffn_gate_b",
    "exp_w1": "L0_ffn_exp_w1", "exp_b1": "L0_ffn_exp_b1", "exp_w2": "L0_ffn_exp_w2", "exp_b2": "L0_ffn_exp_b2",
}
_TRANSPOSED = {"WvT": "L0_attn_Wv", "in_wT": "L0_ffn_in_w", "out_wT": "L0_ffn_out_w", "gate_wT": "L0_ffn_gate_w"}


def kernel(**inputs):
    import numpy as _np
    import concourse.bacc as _bacc
    from concourse import mybir as _mybir
    from concourse.bass_utils import run_bass_kernel_spmd as _run

    nc = _bacc.Bacc("TRN2", target_bir_lowering=False, num_devices=1)
    laid = {name: _np.ascontiguousarray(inputs[source]) for name, source in _RENAMED.items()}
    laid |= {name: _np.ascontiguousarray(_np.asarray(inputs[source]).T) for name, source in _TRANSPOSED.items()}
    for name in ("lnp_g", "lnp_b", "mlp_b1"):
        laid[name] = _np.ascontiguousarray(laid[name].reshape(-1, 128).T)
    laid["exp_b1"] = _np.ascontiguousarray(laid["exp_b1"].reshape(4, -1, 128).transpose(2, 0, 1))
    laid["qk_b"] = _np.ascontiguousarray(laid["in_b"][0:384].reshape(2, 3, 4, 16).transpose(2, 3, 1, 0)).reshape(4, 16, 6)
    x = _np.asarray(inputs["x"]).reshape(32, 3, 6, 16, 6, 16)
    laid["patches"] = _np.ascontiguousarray(x.transpose(0, 2, 4, 3, 5, 1)).reshape(32, 36, 768)
    arrays, args = {}, {}
    for name, v in laid.items():
        arrays[f"in_{name}"] = v
        args[name] = nc.dram_tensor(f"in_{name}", v.shape, _mybir.dt.from_np(v.dtype), kind="ExternalInput").ap()
    out = nc.dram_tensor("out", (32, 165, 192), _mybir.dt.from_np(_np.dtype("float32")), kind="ExternalOutput").ap()
    build_program(nc, args, out)
    r = _run(nc, [arrays], core_ids=[0])
    return r.results[0]["out"]
```

```python
from contextlib import ExitStack

import numpy as np

import concourse.bass as bass
from concourse import mybir

F32 = mybir.dt.float32
F32R = mybir.dt.float32r
ALU = mybir.AluOpType
ACT = mybir.ActivationFunctionType
AX_X = mybir.AxisListType.X

P = 128
B = 32
NPATCH = 36
NIMG = NPATCH + 1
NTXT = 128
S = NIMG + NTXT
D = 192
DA = D + 1
PD = 768
HID = 768
NH = 12
HD = D // NH
NE = 4
NF = NE + 1
PAIRS = B // 2
KP = PD // P
KH = HID // P
KD = (128, 64)
KA = (128, 65)
EPS = 1e-5
TB = 120
TG = 4
GT = TB * TG
GROUPS = B * S // GT
assert GROUPS * GT == B * S
PXW = NTXT + 64 + S
TILE_OF = (0, 2, 1)
HEAD_SCALE = float(HD) ** -0.5

SETUP_COLS = (("wqa", (2, DA)), ("wka", (2, DA)), ("wqk", (2, 6, NH // 3, 32)), ("wv", (2, D)), ("fg", (2,)), ("fb", (2,)),
              ("lnp_g", (KP,)), ("lnp_b", (KP,)), ("clsb", (D,)))
CONST_COLS = (("wlin", (KP, D)), ("lin_bias", (D,)), ("g2m", (D,)), ("b2m", (D,)), ("qkb", (6,)), ("vb", (D,)), ("wva", (2, D)),
              ("ob", (D,)))


def width(cols):
    return sum(int(np.prod(shape)) for _, shape in cols)


class Steps:

    def __init__(self, sem, eng):
        self.sem, self.eng, self.base, self.k = sem, eng, 0, 0

    def at(self, base):
        self.base, self.k = base, 0

    def link(self, ins):
        self.k += 1
        ins.then_inc(self.sem, 1)
        self.eng.wait_ge(self.sem, self.base + self.k)

    def link_aggregate(self, ins, pad):
        self.link(ins)
        self.eng.memset(pad, 0.0)


def build_program(nc, a, out):
    ctx = ExitStack()

    def sem(name):
        return ctx.enter_context(nc.semaphore(name))

    def sb(stack, name, shape, dt=F32):
        return stack.enter_context(nc.sbuf_tensor(name, shape, dt))

    h1d = nc.dram_tensor("h1_scratch", [B, S, D], F32, kind="Internal").ap()
    x1d = nc.dram_tensor("x1_scratch", [B, S, D], F32, kind="Internal").ap()

    PS = ctx.enter_context(nc.psum_tensor("PS", [P, 8, 512], F32))
    ident = sb(ctx, "ident", [P, P])
    eps_half = sb(ctx, "minus_half", [P, 8])

    pad = sb(ctx, "pad", [P, 1])
    euler = sb(ctx, "euler", [TB, TG, NE])
    b1c = sb(ctx, "b1c", [P, NF, KH])
    g2c = sb(ctx, "g2c", [P, 2])
    b2c = sb(ctx, "b2c", [P, 2])
    gwf = sb(ctx, "gwf", [P, 2, NE])
    gbb = sb(ctx, "gbb", [P, NE])

    one = ExitStack()
    consts = sb(one, "consts", [P, width(CONST_COLS)])
    AT = sb(one, "AT", [P, 2, DA])
    XP = sb(one, "XP", [P, PD])
    XN = sb(one, "XN", [P, PD])
    XNT = sb(one, "XNT", [P, KP, P])
    Y = sb(one, "Y", [P, D])
    Y2 = sb(one, "Y2", [P, D])
    H = sb(one, "H", [P, 3, D])
    XA = sb(one, "XA", [P, 3, DA])
    XAT = sb(one, "XAT", [P, 2, 2, D])
    GS = sb(one, "GS", [P, 2, 2, DA])
    T1 = sb(one, "T1", [P, 2, 2, D])
    PM = sb(one, "PM", [P, 2, 2, D])
    U = sb(one, "U", [P, 3, D])
    Z = sb(one, "Z", [P, 3, D])
    ZH = sb(one, "ZH", [P, 2 * D], F32R)
    ZL = sb(one, "ZL", [P, 2 * D], F32R)
    ZS = sb(one, "ZS", [P, 2 * D], F32R)
    wqkr = sb(one, "wqkr", [P, 4, 6, P], F32R)
    wvr = sb(one, "wvr", [P, 4, D], F32R)
    UB = sb(one, "UB", [P, 3, D])
    parity = sb(one, "parity", [P, 2])
    qb = sb(one, "qb", [P, 3, 2])
    Q = sb(one, "Q", [P, 3, 2, 2 * D])
    K = sb(one, "K", [P, 3, 2 * D])
    VX = sb(one, "VX", [P, 2, 2, NH, 32])
    PX = sb(one, "PX", [P, 2, 3, PXW])
    CT = sb(one, "CT", [P, 3, 3 * P])
    ow = sb(one, "ow", [P, 2, D])
    rec = sb(one, "rec", [P, 3, NH])
    CN = sb(one, "CN", [P, 3, D])
    CNT = sb(one, "CNT", [P, 2, 3 * P])
    st = sb(one, "st", [P, 5, 3, 6])
    mv = sb(one, "mv", [P, 5, 3, 2])
    ve = sb(one, "ve", [P, 5, 3])
    rs = sb(one, "rs", [P, 5, 3])
    mx = sb(one, "mx", [P, 6, 6])
    nb = sb(one, "nb", [P, 6, 6])
    setup = ExitStack()
    lnp_rep = sb(setup, "lnp_rep", [P, KP, P])
    fb_rep = sb(setup, "fb_rep", [P, 2, P])
    vbT = sb(setup, "vbT", [P, 2, P])
    setup_consts = sb(setup, "setup_consts", [P, width(SETUP_COLS)])
    setup.close()
    runs = {}
    for tensor, cols in ((setup_consts, SETUP_COLS), (consts, CONST_COLS)):
        at = 0
        for name, shape in cols:
            n = int(np.prod(shape))
            runs[name] = tensor[:, at:at + n]
            at += n
    wlin = runs["wlin"].rearrange("p (k d) -> p k d", k=KP)
    wqk = runs["wqk"].rearrange("p (k m j e) -> p k m j e", k=2, m=6, j=NH // 3)
    wqa, wka, wv, wva = (runs[name].rearrange("p (k d) -> p k d", k=2) for name in ("wqa", "wka", "wv", "wva"))
    lnp_g, lnp_b, fg, fb = (runs[name] for name in ("lnp_g", "lnp_b", "fg", "fb"))
    lin_bias, g2m, b2m, clsb, qkb, vb, ob = (runs[name] for name in ("lin_bias", "g2m", "b2m", "clsb", "qkb", "vb", "ob"))
    PT = sb(one, "PT", [P, 6, 3, 2 * D])
    H1 = sb(one, "H1", [P, 3, D])
    X1 = sb(one, "X1", [P, 3, D])
    rb2 = sb(one, "rb2", [1, NF, D])
    rw1 = sb(one, "rw1", [P, NF, 2, HID])
    rw2 = sb(one, "rw2", [P, NF, KH, D])
    one.close()

    two = ctx
    w1r = sb(two, "w1r", [P, NF, 4, HID], F32R)
    w2r = sb(two, "w2r", [P, NF, KH, 2 * D], F32R)
    b2r = sb(two, "b2r", [33, NF, D], F32R)
    ones33 = sb(two, "ones33", [33, TB], F32R)
    onesf = sb(two, "onesf", [33, TB])
    gwr = sb(two, "gwr", [P, 4, NE], F32R)
    tri = sb(two, "tri", [P, NE, NE])
    st2 = sb(two, "st2", [TB, TG, 6])
    mv2 = sb(two, "mv2", [TB, TG, 2])
    ve2 = sb(two, "ve2", [TB, TG])
    rs2 = sb(two, "rs2", [TB, TG])
    lg = sb(two, "lg", [TB, TG, NE])
    gtm = sb(two, "gtm", [TB, TG, NE, NE])
    eqm = sb(two, "eqm", [TB, TG, NE, NE])
    rank = sb(two, "rank", [TB, TG, NE])
    top = sb(two, "top", [TB, TG])
    ldf = sb(two, "ldf", [TB, TG, NE])
    lex = sb(two, "lex", [TB, TG, NE])
    gex = sb(two, "gex", [TB, TG, NE])
    den = sb(two, "den", [TB, TG])
    comb = sb(two, "comb", [TB, TG, NE])
    X = sb(two, "X", [TB, TG, D])
    HH = sb(two, "HH", [TB, TG, D])
    ACC = sb(two, "ACC", [TB, TG, D])
    X2 = sb(two, "X2", [TB, TG, D])
    Z2 = sb(two, "Z2", [TB, TG, D])
    XH = sb(two, "XH", [P, 2, GT], F32R)
    XL = sb(two, "XL", [P, 2, GT], F32R)
    XS = sb(two, "XS", [P, 2, GT], F32R)
    ZF = sb(two, "ZF", [P, 2, GT])
    GF = sb(two, "GF", [P, 3, GT])
    GH = sb(two, "GH", [P, 2, KH, GT], F32R)
    GL = sb(two, "GL", [P, 2, KH, GT], F32R)

    const_in = sem("const_in")
    ident_ready = sem("ident_ready")
    zeroed = sem("zeroed")
    setup_ps = sem("setup_ps")
    setup_dve = sem("setup_dve")
    setup_act = sem("setup_act")
    attn_const_ready = sem("attn_const_ready")
    patches_in = sem("patches_in")
    txt_in = sem("txt_in")
    dve_step = sem("dve_step")
    pool_step = sem("pool_step")
    var_ready = sem("var_ready")
    rstd_ready = sem("rstd_ready")
    xn_ready = sem("xn_ready")
    xnT_ps = sem("xnT_ps")
    xnT_ready = sem("xnT_ready")
    tok_ps = sem("tok_ps")
    xa_ready = sem("xa_ready")
    xaT_ps = sem("xaT_ps")
    xaT_ready = sem("xaT_ready")
    lin_mat_ps = sem("lin_mat_ps")
    lin_mat_ready = sem("lin_mat_ready")
    lin_ps = sem("lin_ps")
    h1_ready = sem("h1_ready")
    h1_stored = sem("h1_stored")
    u_ready = sem("u_ready")
    ub_ready = sem("ub_ready")
    z_ready = sem("z_ready")
    zT_ps = sem("zT_ps")
    zT_high = sem("zT_high")
    zT_ready = sem("zT_ready")
    qk_ps = sem("qk_ps")
    qk_ready = sem("qk_ready")
    v_ps = sem("v_ps")
    v_ready = sem("v_ready")
    score_ps = sem("score_ps")
    max_ready = sem("max_ready")
    prob_ready = sem("prob_ready")
    probT_ps = sem("probT_ps")
    probT_dve_ready = sem("probT_dve_ready")
    probT_act_ready = sem("probT_act_ready")
    ctxT_ps = sem("ctxT_ps")
    ctxT_ready = sem("ctxT_ready")
    ctxT2_ready = sem("ctxT2_ready")
    ctx_ps = sem("ctx_ps")
    ctx_ready = sem("ctx_ready")
    cnT_ps = sem("cnT_ps")
    cnT_ready = sem("cnT_ready")
    proj_ps = sem("proj_ps")
    x1_ready = sem("x1_ready")
    x1_stored = sem("x1_stored")
    phase_done = sem("phase_done")
    raw_in = [sem(f"raw_in{f}") for f in range(NF)]
    vec_in = sem("vec_in")
    w1hi_ready = sem("w1hi_ready")
    w1lo_ready = sem("w1lo_ready")
    w2hi_ready = sem("w2hi_ready")
    w2lo_ready = sem("w2lo_ready")
    x_in = sem("x_in")
    hh_in = sem("hh_in")
    actT_ps = sem("actT_ps")
    actT_hi = sem("actT_hi")
    actT_ready = sem("actT_ready")
    gate_ps = sem("gate_ps")
    ldiff_ready = sem("ldiff_ready")
    lexp_ready = sem("lexp_ready")
    up_ps = sem("up_ps")
    gelu_ready = sem("gelu_ready")
    high_ready = sem("high_ready")
    hid_ready = sem("hid_ready")
    down_ps = sem("down_ps")
    down_read = sem("down_read")
    var2_ready = sem("var2_ready")
    rstd2_ready = sem("rstd2_ready")
    z2_ready = sem("z2_ready")
    acc_init = sem("acc_init")
    out_ready = sem("out_ready")
    out_stored = sem("out_stored")

    def qk_bank(m):
        return 6 + (m + 1) % 2 if m else 2

    def probT_views(g):
        u, c = g // 3, g % 3
        t, r = TILE_OF[u // 2], u % 2
        src = PS[:, 4 + g % 2, 0:3 * P]
        dst = PT[:, 3 * r + c, :, :]
        if t < 2:
            return dst[:, :, D * t:D * t + P], src.rearrange("p (h q) -> p h q", h=3)
        return dst.rearrange("p h (b q) -> p h b q", b=2)[:, :, :, P:D], src.rearrange("p (h b q) -> p h b q", h=3, b=2)

    UPS = NF * KH
    DOWNS = NF * TG
    HALF = (range(KH // 2), range(KH // 2, KH))

    def order(more):
        return (1, 0, 2, 3, 4) if more else (1, 2, 3, 4)

    def high_by_act(slot, m):
        return slot == 0

    def place(slot, more):
        return order(more).index(slot) % 2

    block = ctx.enter_context(nc.Block())
    NCONST = 4
    NVEC = 14

    def bc(ap, n):
        return ap.rearrange("(o d) -> o d", o=1).to_broadcast([n, ap.shape[-1]])

    @block.sync
    def _(sp):
        sp.wait_ge(zeroed, 1)

        def load_pair(i):
            for b in range(2):
                sp.dma_start(XP[64 * b + 1:64 * b + NIMG, :],
                             a["patches"][bass.ds(2 * i + b, 1)].rearrange("o n d -> (o n) d")).then_inc(patches_in, 16)
            sp.dma_start(H[:, 0:2, :], a["txt"][bass.ds(2 * i, 2)].rearrange("b p d -> p b d")).then_inc(txt_in, 16)

        sp.dma_start(setup_consts[:, :], a["setup_const"]).then_inc(const_in, 16)
        sp.dma_start(consts[:, :], a["attn_const"]).then_inc(const_in, 16)
        for k in range(2):
            sp.dma_start(ow[0:KD[k], k, :], a["out_wT"][P * k:P * k + KD[k], :]).then_inc(const_in, 16)
        load_pair(0)

        def store_tile(i, src, dst, done):
            sp.dma_start(dst[bass.ds(2 * i, 2), NIMG:S, :].rearrange("b p d -> p b d"), src[:, 0:2, :]).then_inc(done, 16)
            for b in range(2):
                sp.dma_start(dst[bass.ds(2 * i + b, 1), 0:NIMG, :].rearrange("o n d -> (o n) d"),
                             src[64 * b:64 * b + NIMG, 2, :]).then_inc(done, 16)

        def pair(i, more):
            sp.wait_ge(h1_ready, i + 1)
            store_tile(i, H1, h1d, h1_stored)
            if more:
                load_pair(i + 1)

        def x1_store(i):
            sp.wait_ge(x1_ready, i + 1)
            store_tile(i, X1, x1d, x1_stored)

        pair(0, True)

        nvec = [0]

        def vec(dst, src):
            sp.dma_start(dst, src).then_inc(vec_in, 16)
            nvec[0] += 1

        def load_raw(f):
            s = raw_in[f]
            w1 = a["mlp_w1"] if f == 0 else a["exp_w1"][f - 1]
            w2 = a["mlp_w2"] if f == 0 else a["exp_w2"][f - 1]
            sp.dma_start(rw1[:, f, 0, :], w1[0:P, :]).then_inc(s, 16)
            for r in range(2):
                sp.dma_start(rw1[64 * r:64 * r + 64, f, 1, :], w1[P:D, :]).then_inc(s, 16)
            sp.dma_start(rw2[:, f, :, :], w2.rearrange("(k p) d -> p k d", p=P)).then_inc(s, 16)

        vec(b1c[:, 0, :], a["mlp_b1"])
        vec(b1c[:, 1:NF, :], a["exp_b1"])
        for g, name in ((g2c, "f2_g"), (b2c, "f2_b")):
            vec(g[:, 0:1], a[name][0:P].rearrange("(p o) -> p o", o=1))
            for r in range(2):
                vec(g[64 * r:64 * r + 64, 1:2], a[name][P:D].rearrange("(p o) -> p o", o=1))
        vec(rb2[0:1, 0, :], a["mlp_b2"].rearrange("(o d) -> o d", o=1))
        vec(rb2[0:1, 1:NF, :], a["exp_b2"].rearrange("(o e) d -> o e d", o=1))
        vec(gwf[:, 0, :], a["gate_wT"][0:P, :])
        for r in range(2):
            vec(gwf[64 * r:64 * r + 64, 1, :], a["gate_wT"][P:D, :])
        vec(gbb[:, :], bc(a["gate_b"], P))
        for f in range(NF):
            load_raw(f)

        with sp.Fori(0, PAIRS - 2) as i:
            pair(i + 1, True)
            x1_store(i)
        pair(PAIRS - 1, False)
        x1_store(PAIRS - 2)
        x1_store(PAIRS - 1)

        sp.wait_ge(h1_stored, PAIRS * 48 + 1)
        sp.wait_ge(x1_stored, PAIRS * 48 + 1)

        def rows(t, n):
            return t.rearrange("b s d -> (b s) d")[bass.ds(n * GT, GT), :].rearrange("(a p) d -> p a d", p=TB)

        def load_x(n):
            sp.dma_start(X[:, :, :], rows(x1d, n)).then_inc(x_in, 16)

        def load_hh(n):
            sp.dma_start(HH[:, :, :], rows(h1d, n)).then_inc(hh_in, 16)

        def group(n, x_load, hh_load):
            if hh_load:
                sp.wait_ge(acc_init, n + 1)
                load_hh(n + 1)
            if x_load:
                sp.wait_ge(var2_ready, n + 2)
                load_x(n + 2)
            sp.wait_ge(out_ready, n + 1)
            sp.dma_start(rows(out, n), ACC[:, :, :]).then_inc(out_stored, 16)

        load_x(0)
        load_hh(0)
        sp.wait_ge(var2_ready, 1)
        load_x(1)
        with sp.Fori(0, GROUPS - 2) as n:
            group(n, True, True)
        group(GROUPS - 2, False, True)
        group(GROUPS - 1, False, False)
        sp.wait_ge(out_stored, GROUPS * 16 + 1)
        assert nvec[0] == NVEC, nvec

    @block.gpsimd
    def _(pool):
        nc.gpsimd.memset(XP[:, :], 0.0).then_inc(zeroed, 1)
        nc.gpsimd.memset(ident[:, :], 0.0).then_inc(ident_ready, 1)
        pool.wait_ge(ident_ready, 1)
        nc.gpsimd.affine_select(out=ident[:, :], in_=ident[:, :], compare_op=ALU.not_equal, fill=1.0, base=0,
                                pattern=[[-1, P]], channel_multiplier=1).then_inc(ident_ready, 1)
        nc.gpsimd.memset(eps_half[:, :], -0.5).then_inc(pool_step, 1)
        nc.gpsimd.memset(XA[:, :, D:DA], 1.0).then_inc(pool_step, 1)
        nc.gpsimd.memset(VX[:, :, :, :, HD:HD + 1], 1.0).then_inc(pool_step, 1)
        nc.gpsimd.memset(VX[:, :, :, :, HD + 1:32], 0.0)
        nc.gpsimd.memset(PX[:, :, :, S:NTXT + 64], 0.0).then_inc(pool_step, 1)
        pool.wait_ge(pool_step, 4)
        pool.wait_ge(attn_const_ready, 1)

        def rstd(base, k, n):
            pool.wait_ge(var_ready, base + k)
            nc.gpsimd.tensor_tensor(rs[:, k - 1, 0:n], ve[:, k - 1, 0:n], eps_half[:, 0:n], ALU.pow).then_inc(rstd_ready, 1)

        def pre(j, x1_before):
            for k, n in ((1, 1), (2, 1), (3, 3), (4, 3), (5, 3)):
                rstd(j * 5, k, n)
            pool.wait_ge(u_ready, j + 1)
            if x1_before is not None:
                pool.wait_ge(x1_ready, x1_before)
            for t in range(3):
                last = nc.gpsimd.tensor_tensor(UB[:, t, :], U[:, t, :], ob[:, :], ALU.add)
            last.then_inc(ub_ready, 1)

        pre(0, None)
        with pool.Fori(0, PAIRS - 1) as i:
            pre(i + 1, i + 1)
        pool.wait_ge(x1_ready, PAIRS)
        nc.gpsimd.memset(onesf[:, :], 1.0).then_inc(phase_done, 1)
        nc.gpsimd.memset(euler[:, :, :], float(np.e))
        nc.gpsimd.memset(tri[:, :, :], 1.0).then_inc(pool_step, 1)
        pool.wait_ge(pool_step, 5)
        nc.gpsimd.affine_select(out=tri[:, :, :], in_=tri[:, :, :], compare_op=ALU.is_gt, fill=0.0, base=0,
                                pattern=[[1, NE], [-1, NE]], channel_multiplier=0).then_inc(pool_step, 1)
        pool.wait_ge(pool_step, 6)

        def rstd2(n):
            pool.wait_ge(var2_ready, n + 1)
            nc.gpsimd.tensor_tensor(rs2[:, :], ve2[:, :], eps_half[0:TB, 0:TG], ALU.pow).then_inc(rstd2_ready, 1)

        def gates_and_acc(n):
            pool.wait_ge(ldiff_ready, n + 1)
            nc.gpsimd.tensor_tensor(lex[:, :, :], euler[:, :, :], ldf[:, :, :], ALU.pow).then_inc(lexp_ready, 1)
            pool.wait_ge(hh_in, n * 16 + 16)
            pool.wait_ge(out_stored, n * 16 + 1)
            nc.gpsimd.tensor_tensor(ACC[:, :, :], X2[:, :, :], HH[:, :, :], ALU.add).then_inc(acc_init, 1)

        rstd2(0)
        with pool.Fori(0, GROUPS - 1) as n:
            gates_and_acc(n)
            rstd2(n + 1)
        gates_and_acc(GROUPS - 1)

    @block.scalar
    def _(act):
        def copy(dst, src, scale=1.0):
            return nc.scalar.activation(dst, src, ACT.Copy, scale=scale)

        act.wait_ge(setup_ps, 1)
        copy(AT[:, 0, :], PS[:, 0, 0:DA], float(D) ** -0.5)
        copy(AT[0:65, 1, :], PS[0:65, 0, DA:2 * DA], float(D) ** -0.5).then_inc(setup_act, 1)
        act.wait_ge(setup_ps, 4)
        copy(vbT[:, 0, :], PS[:, 5, 0:P])
        copy(vbT[0:64, 1, :], PS[0:64, 5, P:2 * P]).then_inc(setup_act, 1)

        def transposed(dst, bank, rows, ready):
            copy(dst[:, 0, :, :], PS[:, bank, 0:2 * D].rearrange("p (b c) -> p b c", b=2))
            copy(dst[0:rows, 1, :, :], PS[0:rows, bank + 1, 0:2 * D].rearrange("p (b c) -> p b c", b=2)).then_inc(ready, 1)

        def exps(i, u):
            act.wait_ge(max_ready, i * 6 + u + 1)
            if u >= 2:
                act.wait_ge(probT_ps, i * 18 + 3 * (u - 2) + 3)
            for c in range(3):
                for r in range(2):
                    to = r * (NTXT + 64)
                    last = nc.scalar.activation(PX[:, u % 2, c, to:to + S], PS[:, 2 * (u % 2) + r, c * S:(c + 1) * S], ACT.Exp,
                                                bias=nb[:, u, 3 * r + c:3 * r + c + 1], scale=HEAD_SCALE)
            last.then_inc(prob_ready, 1)

        def probsT(i, *gs):
            for g in gs:
                act.wait_ge(probT_ps, i * 18 + g + 1)
                copy(*probT_views(g)).then_inc(probT_act_ready, 1)

        def xnT(j):
            act.wait_ge(xnT_ps, j + 1)
            copy(XNT[:, 0:4, :], PS[:, 6, :].rearrange("p (k c) -> p k c", k=4))
            copy(XNT[:, 4:6, :], PS[:, 7, 0:2 * P].rearrange("p (k c) -> p k c", k=2)).then_inc(xnT_ready, 1)

        def xaT(j):
            act.wait_ge(xaT_ps, j + 1)
            transposed(XAT, 6, 65, xaT_ready)

        def lin_mat(j, step):
            dst, w = ((GS, DA), (T1, D), (PM, D))[step]
            for b in range(2):
                act.wait_ge(lin_mat_ps, j * 6 + 2 * step + b + 1)
                copy(dst[:, b, 0, 0:w], PS[:, 6 + b, 0:w])
                copy(dst[0:65, b, 1, 0:w], PS[0:65, 6 + b, w:2 * w]).then_inc(lin_mat_ready, 1)

        def zT(j):
            act.wait_ge(zT_ps, j + 1)
            copy(ZH[:, :], PS[:, 6, 0:2 * D])
            copy(ZS[0:64, :], PS[0:64, 7, 0:2 * D]).then_inc(zT_high, 1)

        def qk(j, ms):
            for m in ms:
                act.wait_ge(qk_ps, j * 6 + m + 1)
                src = PS[:, qk_bank(m), 0:2 * D]
                if m % 2 == 0:
                    for r in range(2):
                        last = nc.scalar.activation(Q[:, m // 2, r, :], src, ACT.Identity, bias=qb[:, m // 2, r:r + 1],
                                                    scale=parity[:, r:r + 1])
                else:
                    last = nc.scalar.activation(K[:, m // 2, :], src, ACT.Identity, bias=qkb[:, m:m + 1], scale=1.0)
                last.then_inc(qk_ready, 1)

        def contextsT(i, b):
            act.wait_ge(ctxT_ps, i * 2 + b + 1)
            src = PS[:, 2 * b, 0:2 * D].rearrange("p (c q) -> p c q", c=2)
            copy(CT[:, 0:2, P * b:P * b + P], src[:, :, 0:P])
            copy(CT[:, 0:2, 2 * P + 64 * b:2 * P + 64 * b + 64], src[:, :, P:D]).then_inc(ctxT_ready, 1)

        def w1_high(f):
            if f == 0:
                act.wait_ge(v_ready, PAIRS)
                act.wait_ge(ub_ready, PAIRS)
            act.wait_ge(raw_in[f], 64)
            for k in range(2):
                last = copy(w1r[:, f, 2 * k, :], rw1[:, f, k, :])
            last.then_inc(w1hi_ready, 1)

        def w2_high(f):
            copy(w2r[:, f, :, 0:D], rw2[:, f, :, :]).then_inc(w2hi_ready, 1)

        def body(i, j):
            core, pre = i is not None, j is not None
            core and exps(i, 0)
            pre and xnT(j)
            core and probsT(i, 1)
            core and exps(i, 1)
            core and exps(i, 2)
            core and probsT(i, 3)
            pre or w1_high(0)
            core and probsT(i, 5, 7)
            core and exps(i, 3)
            pre and xaT(j)
            core and probsT(i, 9)
            pre or w1_high(1)
            core and probsT(i, 11)
            pre and lin_mat(j, 0)
            core and exps(i, 4)
            pre or w1_high(2)
            pre and lin_mat(j, 1)
            pre and lin_mat(j, 2)
            core and exps(i, 5)
            core and probsT(i, 13)
            core and contextsT(i, 0)
            core and probsT(i, 15, 17)
            core and contextsT(i, 1)
            pre or w1_high(3)
            pre and zT(j)
            pre and qk(j, (0, 1))
            pre and qk(j, (2, 3, 4, 5))

        body(None, 0)
        with act.Fori(0, PAIRS - 1) as i:
            body(i, i + 1)
        body(PAIRS - 1, None)

        act.wait_ge(x1_ready, PAIRS)
        nc.scalar.activation(ones33[:, :], ident[0:33, 0:TB], ACT.Copy, scale=0.0, bias=1.0).then_inc(phase_done, 1)
        act.wait_ge(phase_done, 3)
        w2_high(0)
        w1_high(NF - 1)
        for f in range(1, NF):
            w2_high(f)

        def split_high(n, which):
            act.wait_ge(actT_ps, n * 2 + which + 1)
            if which == 0:
                copy(XH[:, which, :], PS[:, 0, 0:GT])
                copy(XS[0:64, which, :], PS[0:64, 1, 0:GT]).then_inc(actT_hi, 1)
                return
            for k, high in ((0, XH[:, which, :]), (1, XS[0:64, which, :])):
                for to in (ZF[0:KD[k], k, :], high):
                    last = nc.scalar.activation(to, PS[0:KD[k], k, 0:GT], ACT.Identity,
                                                bias=b2c[0:KD[k], k:k + 1], scale=g2c[0:KD[k], k:k + 1])
            last.then_inc(actT_hi, 1)

        def gelus(base, slot, at, ms=range(KH)):
            for m in ms:
                act.wait_ge(up_ps, base + m + 1)
                act.wait_ge(hid_ready, base + m + 1)
                nc.scalar.activation(GF[:, m % 3, :], PS[:, 2 + m % 2, 0:GT], ACT.Gelu,
                                     bias=b1c[:, slot, m:m + 1], scale=1.0).then_inc(gelu_ready, 1)
                if high_by_act(slot, m):
                    act.wait_ge(gelu_ready, base + m + 1 + 2)
                    copy(GH[:, at, m, :], GF[:, m % 3, :]).then_inc(high_ready, 1)

        def group(n, more):
            gelus(n * UPS + KH, 1, 0, HALF[0])
            if more:
                split_high(n + 1, 0)
            gelus(n * UPS + KH, 1, 0, HALF[1])
            for turn, slot in list(enumerate(order(more)))[1:]:
                gelus(n * UPS + KH + turn * KH, slot, turn % 2)
            if more:
                split_high(n + 1, 1)

        act.wait_ge(w2lo_ready, 1)
        split_high(0, 0)
        gelus(0, 0, 0)
        split_high(0, 1)
        with act.Fori(0, GROUPS - 1) as n:
            group(n, True)
        group(GROUPS - 1, False)

    @block.vector
    def _(dve):
        steps = Steps(dve_step, dve)
        tt, ts, cp = nc.vector.tensor_tensor, nc.vector.tensor_scalar, nc.vector.tensor_copy
        stt = nc.vector.scalar_tensor_tensor

        for j in range(4):
            for r in range(2):
                last = nc.vector.memset(parity[32 * j:32 * j + 32, r:r + 1], float(j % 2 == r))
        steps.link(last)
        dve.wait_ge(const_in, NCONST * 16)
        cp(lnp_rep[:, :, :], lnp_b[:, :].unsqueeze(2).to_broadcast([P, KP, P]))
        cp(fb_rep[:, 0, :], fb[:, 0:1].to_broadcast([P, P]))
        cp(fb_rep[0:64, 1, :], fb[0:64, 1:2].to_broadcast([64, P])).then_inc(setup_dve, 1)
        tt(b2m[:, :], b2m[:, :], clsb[:, :], ALU.add)
        dve.wait_ge(setup_ps, 3)
        tt(lin_bias[:, :], lin_bias[:, :], PS[:, 2, 0:D], ALU.add)
        tt(qkb[:, :], qkb[:, :], PS[:, 3, 0:6], ALU.add)
        tt(vb[:, :], vb[:, :], PS[:, 4, 0:D], ALU.add).then_inc(setup_dve, 1)
        for k in range(KP):
            ts(wlin[:, k, :], wlin[:, k, :], lnp_g[:, k:k + 1], None, ALU.mult)
        for k in range(2):
            qk_all = wqk[:, k, :, :, :].rearrange("p m j e -> p m (j e)")
            for to, w in ((wqkr, qk_all), (wvr, wv[:, k, :])):
                steps.link(ts(to[:, 2 * k], w, fg[:, k:k + 1], None, ALU.mult))
                stt(to[:, 2 * k + 1], w, fg[:, k:k + 1], to[:, 2 * k].bitcast(F32), ALU.mult, ALU.subtract)
        dve.wait_ge(setup_ps, 5)
        steps.link(tt(ob[:, :], ob[:, :], PS[:, 6, 0:D], ALU.add))
        dve.wait_ge(pool_step, 4)
        tt(qb[:, :, :], qkb[:, :].rearrange("p (c w) -> p c w", w=2)[:, :, 0:1].to_broadcast([P, 3, 2]),
           parity[:, :].unsqueeze(1).to_broadcast([P, 3, 2]), ALU.mult)
        nc.vector.memset(mx[:, 0, 0:1], 0.0).then_inc(h1_stored, 1)
        nc.vector.memset(mx[:, 0, 1:2], 0.0).then_inc(x1_stored, 1)
        nc.vector.memset(mx[:, 0, 2:3], 0.0).then_inc(attn_const_ready, 1)
        setup_steps = steps.k

        def stats(j, k, src, n, wide=False):
            for t in range(2 if wide else n):
                last = nc.vector.bn_stats(st[:, k - 1, t, :], src(t))
            steps.link_aggregate(last, pad[:, 0:1])
            for t in range(n):
                last = nc.vector.bn_aggr(mv[:, k - 1, t, :], st[:, k - 1, 0:2, :] if wide else st[:, k - 1, t, :])
            steps.link(last)
            ts(ve[:, k - 1, 0:n], mv[:, k - 1, 0:n, 1], EPS, None, ALU.add).then_inc(var_ready, 1)

        def normed(j, k, src, dst, n):
            dve.wait_ge(rstd_ready, j * 5 + k)
            for t in range(n):
                last = ts(dst(t), src(t), mv[:, k - 1, t, 0:1], rs[:, k - 1, t:t + 1], ALU.subtract, ALU.mult)
            return last

        def patch_stats(j):
            dve.wait_ge(patches_in, j * 32 + 32)
            stats(j, 1, lambda c: XP[:, c * PD // 2:(c + 1) * PD // 2], 1, True)

        def patch_normed(j):
            normed(j, 1, lambda t: XP[:, :], lambda t: XN[:, :], 1).then_inc(xn_ready, 1)

        def token_stats(j):
            dve.wait_ge(tok_ps, j + 1)
            steps.link(tt(Y[:, :], PS[:, 6, 0:D], lin_bias[:, :], ALU.add))
            stats(j, 2, lambda t: Y[:, :], 1)

        def tokens(j):
            dve.wait_ge(rstd_ready, j * 5 + 2)
            steps.link(stt(Y2[:, :], Y[:, :], mv[:, 1, 0, 0:1], g2m[:, :], ALU.subtract, ALU.mult))
            steps.link(stt(H[:, 2, :], Y2[:, :], rs[:, 1, 0:1], b2m[:, :], ALU.mult, ALU.add))
            dve.wait_ge(txt_in, j * 16 + 16)
            stats(j, 3, lambda t: H[:, t, :], 3)

        def lin_in(j):
            normed(j, 3, lambda t: H[:, t, :], lambda t: XA[:, t, 0:D], 3).then_inc(xa_ready, 1)

        def lin_out(j):
            dve.wait_ge(lin_ps, j + 1)
            dve.wait_ge(h1_stored, j * 48 + 1)
            tt(H1[:, 0:2, :], PS[:, 6, 0:2 * D].rearrange("p (t d) -> p t d", t=2), H[:, 0:2, :], ALU.add)
            tt(H1[:, 2, :], PS[:, 7, 0:D], H[:, 2, :], ALU.add).then_inc(h1_ready, 1)
            dve.wait_ge(h1_ready, j + 1)
            stats(j, 4, lambda t: H1[:, t, :], 3)

        def u_stats(j, ub_before):
            if ub_before is not None:
                dve.wait_ge(ub_ready, ub_before)
            normed(j, 4, lambda t: H1[:, t, :], lambda t: U[:, t, :], 3).then_inc(u_ready, 1)
            dve.wait_ge(u_ready, j + 1)
            stats(j, 5, lambda t: U[:, t, :], 3)

        def z_low(j):
            dve.wait_ge(zT_high, j + 1)
            tt(ZL[:, :], PS[:, 6, 0:2 * D], ZH[:, :].bitcast(F32), ALU.subtract)
            tt(ZS[64:P, :], PS[0:64, 7, 0:2 * D], ZS[0:64, :].bitcast(F32), ALU.subtract).then_inc(zT_ready, 1)

        def z_out(j):
            normed(j, 5, lambda t: U[:, t, :], lambda t: Z[:, t, :], 3).then_inc(z_ready, 1)

        def values(j):
            dve.wait_ge(v_ps, j + 1)
            cp(VX[:, 0, :, :, 0:HD], PS[:, 6, 0:2 * D].rearrange("p (b h e) -> p b h e", b=2, h=NH))
            for half in range(2):
                dst = VX[64 * half:64 * half + NIMG, 1, :, :, 0:HD].rearrange("p b (g s r) e -> p (b g) s r e", s=2, r=2)[:, :, half]
                src = PS[0:NIMG, 7, 0:2 * D].rearrange("p (g s f) -> p g s f", g=6, s=2)[:, :, half, :]
                last = cp(dst, src.rearrange("p g (r e) -> p g r e", r=2))
            last.then_inc(v_ready, 1)

        def maxima(i, u):
            dve.wait_ge(score_ps, i * 6 + u + 1)
            src = PS[:, 2 * (u % 2):2 * (u % 2) + 2, 0:3 * S].rearrange("p a (s k) -> p a s k", s=3)
            steps.link(nc.vector.tensor_reduce(mx[:, u, :].rearrange("p (a s) -> p a s", a=2), src, AX_X, ALU.max))
            ts(nb[:, u, :], mx[:, u, :], -HEAD_SCALE, None, ALU.mult).then_inc(max_ready, 1)

        def probsT(i, *gs):
            for g in gs:
                dve.wait_ge(probT_ps, i * 18 + g + 1)
                cp(*probT_views(g)).then_inc(probT_dve_ready, 1)

        def contextsT(i):
            dve.wait_ge(ctxT_ps, i * 2 + 2)
            src = PS[:, 1, 0:2 * D].rearrange("p (b q) -> p b q", b=2)
            cp(CT[:, 2, 0:2 * P].rearrange("p (b q) -> p b q", b=2), src[:, :, 0:P])
            cp(CT[:, 2, 2 * P:3 * P].rearrange("p (b q) -> p b q", b=2), src[:, :, P:D]).then_inc(ctxT2_ready, 1)

        def contexts(i):
            for t in range(3):
                dve.wait_ge(ctx_ps, i * 3 + t + 1)
                src = PS[:, 3 + t, 0:NH * 32].rearrange("p (h e) -> p h e", h=NH)
                steps.link(nc.vector.reciprocal(rec[:, t, :], src[:, :, HD]))
                tt(CN[:, t, :].rearrange("p (h e) -> p h e", h=NH), src[:, :, 0:HD],
                   rec[:, t, :].unsqueeze(2).to_broadcast([P, NH, HD]), ALU.mult).then_inc(ctx_ready, 1)

        def normedT(i):
            dve.wait_ge(cnT_ps, i + 1)
            cp(CNT[:, 0, :], PS[:, 0, 0:3 * P])
            cp(CNT[0:64, 1, :], PS[0:64, 1, 0:3 * P]).then_inc(cnT_ready, 1)

        def x1_out(i):
            dve.wait_ge(proj_ps, i + 1)
            dve.wait_ge(ub_ready, i + 1)
            dve.wait_ge(x1_stored, i * 48 + 1)
            tt(X1[:, 0:2, :], PS[:, 2, 0:2 * D].rearrange("p (t d) -> p t d", t=2), UB[:, 0:2, :], ALU.add)
            tt(X1[:, 2, :], PS[:, 3, 0:D], UB[:, 2, :], ALU.add).then_inc(x1_ready, 1)

        def w1_low(f):
            dve.wait_ge(w1hi_ready, f + 1)
            for k in range(2):
                last = tt(w1r[:, f, 2 * k + 1, :], rw1[:, f, k, :], w1r[:, f, 2 * k, :].bitcast(F32), ALU.subtract)
            last.then_inc(w1lo_ready, 1)

        def w2_low(f):
            dve.wait_ge(w2hi_ready, f + 1)
            tt(w2r[:, f, :, D:2 * D], rw2[:, f, :, :], w2r[:, f, :, 0:D].bitcast(F32), ALU.subtract).then_inc(w2lo_ready, 1)

        def body(i, j):
            core, pre = i is not None, j is not None
            pre and patch_stats(j)
            core and maxima(i, 0)
            pre and patch_normed(j)
            core and values(i)
            core and maxima(i, 1)
            core and probsT(i, 0)
            core and maxima(i, 2)
            core and probsT(i, 2)
            pre and token_stats(j)
            core and probsT(i, 4)
            pre and tokens(j)
            core and maxima(i, 3)
            core and probsT(i, 6)
            pre and lin_in(j)
            pre or w1_low(0)
            core and probsT(i, 8)
            core and maxima(i, 4)
            core and probsT(i, 10)
            pre or w1_low(1)
            pre and lin_out(j)
            core and probsT(i, 12)
            core and maxima(i, 5)
            pre and u_stats(j, j if core else None)
            core and probsT(i, 14)
            pre and z_out(j)
            core and probsT(i, 16)
            core and contextsT(i)
            pre or w1_low(2)
            pre and z_low(j)
            core and contexts(i)
            core and normedT(i)
            pre or w1_low(3)
            core and x1_out(i)

        body(None, 0)
        before = steps.base + steps.k
        N_STEPS = 22
        with dve.Fori(0, PAIRS - 1) as i:
            steps.at(before + i * N_STEPS)
            body(i, i + 1)
            assert steps.k == N_STEPS, steps.k
        steps.at(before + (PAIRS - 1) * N_STEPS)
        body(PAIRS - 1, None)
        steps.at(steps.base + steps.k)

        steps.link(nc.vector.memset(b2r[:, :, :].bitcast(F32), 0.0))
        cp(pad[:, :], ident[:, 0:1]).then_inc(phase_done, 1)
        dve.wait_ge(phase_done, 3)
        dve.wait_ge(vec_in, NVEC * 16)
        steps.link(cp(b2r[0:1, :, :], rb2[:, :, :]))
        tt(b2r[32:33, :, :], rb2[:, :, :], b2r[0:1, :, :].bitcast(F32), ALU.subtract)
        for k in range(2):
            steps.link(cp(gwr[:, 2 * k, :], gwf[:, k, :]))
            tt(gwr[:, 2 * k + 1, :], gwf[:, k, :], gwr[:, 2 * k, :].bitcast(F32), ALU.subtract)
        w2_low(0)
        w1_low(NF - 1)
        for f in range(1, NF):
            w2_low(f)
        cp(den[:, 0:1], ident[0:TB, 0:1]).then_inc(hid_ready, 3)
        cp(den[:, 1:2], ident[0:TB, 0:1]).then_inc(gelu_ready, 2)
        cp(den[:, 2:3], ident[0:TB, 0:1]).then_inc(down_read, 4)
        cp(den[:, 3:4], ident[0:TB, 0:1]).then_inc(out_stored, 1)

        def split_low(n, which):
            dve.wait_ge(actT_hi, n * 2 + which + 1)
            full = (ZF[:, 0, :], ZF[0:64, 1, :]) if which else (PS[:, 0, 0:GT], PS[0:64, 1, 0:GT])
            tt(XL[:, which, :], full[0], XH[:, which, :].bitcast(F32), ALU.subtract)
            tt(XS[64:P, which, :], full[1], XS[0:64, which, :].bitcast(F32), ALU.subtract).then_inc(actT_ready, 1)

        highs = [0]
        highs_base = lambda: highs_before[0]
        highs_before = [0]

        def hidden(base, slot, at, ms=range(KH)):
            for m in ms:
                if high_by_act(slot, m):
                    highs[0] += 1
                    dve.wait_ge(high_ready, highs_base() + highs[0])
                else:
                    dve.wait_ge(gelu_ready, base + m + 1 + 2)
                    steps.link(cp(GH[:, at, m, :], GF[:, m % 3, :]))
                tt(GL[:, at, m, :], GF[:, m % 3, :], GH[:, at, m, :].bitcast(F32),
                   ALU.subtract).then_inc(hid_ready, 1)

        def accumulate(base, slot):
            for t in range(TG):
                dve.wait_ge(down_ps, base + t + 1)
                w = comb[:, t, slot - 1:slot]
                steps.link(stt(ACC[:, t, :], PS[0:TB, 4 + t, 0:D], w, ACC[:, t, :], ALU.mult, ALU.add))
                last = stt(ACC[:, t, :], PS[0:TB, 4 + t, D:2 * D], w, ACC[:, t, :], ALU.mult, ALU.add)
                last.then_inc(down_read, 1)
                if slot == NF - 1 and t == TG - 1:
                    dve.wait_ge(down_read, base + TG + 4)
                    cp(den[:, 0:1], den[:, 1:2]).then_inc(out_ready, 1)

        def mlp_out(base):
            for t in range(TG):
                dve.wait_ge(down_ps, base + t + 1)
            steps.link(tt(X2[:, :, :], PS[0:TB, 4:8, 0:D], X[:, :, :], ALU.add))
            steps.link(tt(X2[:, :, :], PS[0:TB, 4:8, D:2 * D], X2[:, :, :], ALU.add))
            cp(den[:, 0:1], X2[:, 0, 0:1]).then_inc(down_read, 4)
            for t in range(TG):
                last = nc.vector.bn_stats(st2[:, t, :], X2[:, t, :])
            steps.link_aggregate(last, pad[:, 0:1])
            for t in range(TG):
                last = nc.vector.bn_aggr(mv2[:, t, :], st2[:, t, :])
            steps.link(last)
            ts(ve2[:, :], mv2[:, :, 1], EPS, None, ALU.add).then_inc(var2_ready, 1)

        def x2_normed(n):
            dve.wait_ge(rstd2_ready, n + 1)
            for t in range(TG):
                last = ts(Z2[:, t, :], X2[:, t, :], mv2[:, t, 0:1], rs2[:, t:t + 1], ALU.subtract, ALU.mult)
            last.then_inc(z2_ready, 1)

        def gate_logits(n):
            dve.wait_ge(gate_ps, n + 1)
            steps.link(tt(lg[:, :, :], PS[0:TB, 0, GT:GT + TG * NE].rearrange("p (t e) -> p t e", t=TG),
                          gbb[0:TB, :].unsqueeze(1).to_broadcast([TB, TG, NE]), ALU.add))
            nc.vector.tensor_reduce(top[:, :], lg[:, :, :], AX_X, ALU.max)
            for t in range(TG):
                lj = lg[:, t, :].unsqueeze(1).to_broadcast([TB, NE, NE])
                le = lg[:, t, :].unsqueeze(2).to_broadcast([TB, NE, NE])
                tt(gtm[:, t, :, :], lj, le, ALU.is_gt)
                last = tt(eqm[:, t, :, :], lj, le, ALU.is_equal)
            steps.link(last)
            tt(ldf[:, :, :], lg[:, :, :], top[:, :].unsqueeze(2).to_broadcast([TB, TG, NE]), ALU.subtract).then_inc(ldiff_ready, 1)

        def gate_weights(n):
            steps.link(tt(eqm[:, :, :, :], eqm[:, :, :, :],
                          tri[0:TB, :, :].unsqueeze(1).to_broadcast([TB, TG, NE, NE]), ALU.mult))
            steps.link(tt(gtm[:, :, :, :], gtm[:, :, :, :], eqm[:, :, :, :], ALU.add))
            steps.link(nc.vector.tensor_reduce(rank[:, :, :], gtm[:, :, :, :], AX_X, ALU.add))
            dve.wait_ge(lexp_ready, n + 1)
            steps.link(stt(gex[:, :, :], rank[:, :, :], 2.0, lex[:, :, :], ALU.is_lt, ALU.mult))
            steps.link(nc.vector.tensor_reduce(den[:, :], gex[:, :, :], AX_X, ALU.add))
            steps.link(nc.vector.reciprocal(den[:, :], den[:, :]))
            steps.link(tt(comb[:, :, :], gex[:, :, :], den[:, :].unsqueeze(2).to_broadcast([TB, TG, NE]), ALU.mult))

        def group(n, more):
            up = lambda slot: n * UPS + KH + order(more).index(slot) * KH
            down = lambda slot: n * DOWNS + TG + order(more).index(slot) * TG
            gate_logits(n)
            hidden(up(1), 1, place(1, more), HALF[0])
            if more:
                split_low(n + 1, 0)
            hidden(up(1), 1, place(1, more), HALF[1])
            gate_weights(n)
            if more:
                hidden(up(0), 0, place(0, more))
            else:
                hidden(up(2), 2, place(2, more))
            dve.wait_ge(acc_init, n + 1)
            accumulate(down(1), 1)
            if more:
                hidden(up(2), 2, place(2, more))
                mlp_out(down(0))
            hidden(up(3), 3, place(3, more))
            if more:
                x2_normed(n + 1)
            accumulate(down(2), 2)
            hidden(up(4), 4, place(4, more))
            if more:
                split_low(n + 1, 1)
            accumulate(down(3), 3)
            accumulate(down(4), 4)

        split_low(0, 0)
        hidden(0, 0, 0)
        mlp_out(0)
        x2_normed(0)
        split_low(0, 1)
        first = steps.base + steps.k
        first_highs = highs[0]
        n_highs = sum(high_by_act(slot, m) for slot in range(NF) for m in range(KH))
        N2 = 59 - n_highs
        with dve.Fori(0, GROUPS - 1) as n:
            steps.at(first + n * N2)
            highs_before[0], highs[0] = first_highs + n * n_highs, 0
            group(n, True)
            assert steps.k == N2, steps.k
        steps.at(first + (GROUPS - 1) * N2)
        highs_before[0], highs[0] = first_highs + (GROUPS - 1) * n_highs, 0
        group(GROUPS - 1, False)

    @block.tensor
    def _(pe):
        def mm(o, l, r, start=True, stop=True):
            return nc.tensor.matmul(o, l, r, start=start, stop=stop)

        def tr(o, x, rows=P):
            return nc.tensor.transpose(o, x, ident[0:rows, 0:rows])

        pe.wait_ge(const_in, NCONST * 16)
        pe.wait_ge(ident_ready, 2)
        for m in range(2):
            for k in range(2):
                last = mm(PS[0:KA[m], 0, m * DA:(m + 1) * DA], wka[0:KD[k], k, P * m:P * m + KA[m]], wqa[0:KD[k], k, :], k == 0, k == 1)
        last.then_inc(setup_ps, 1)
        pe.wait_ge(setup_dve, 1)
        for k in range(KP):
            last = mm(PS[:, 2, 0:D], lnp_rep[:, k, :], wlin[:, k, :], k == 0, k == KP - 1)
        last.then_inc(setup_ps, 1)
        for m in range(6):
            for k in range(2):
                mm(PS[:, 3, m:m + 1], wqk[0:KD[k], k, m, :, :], fb[0:KD[k], k:k + 1], k == 0, k == 1)
        for k in range(2):
            last = mm(PS[:, 4, 0:D], fb_rep[0:KD[k], k, :], wv[0:KD[k], k, :], k == 0, k == 1)
        last.then_inc(setup_ps, 1)
        pe.wait_ge(setup_dve, 2)
        tr(PS[:, 5, 0:P], vb[:, 0:P])
        tr(PS[0:64, 5, P:2 * P], vb[:, P:D]).then_inc(setup_ps, 1)
        pe.wait_ge(setup_act, 2)
        for k in range(2):
            last = mm(PS[:, 6, 0:D], vbT[0:KD[k], k, :], ow[0:KD[k], k, :], k == 0, k == 1)
        last.then_inc(setup_ps, 1)
        pe.wait_ge(attn_const_ready, 1)

        def transpose_set(x, bank, rows, ps):
            for k in range(2):
                w = rows[k]
                o = PS[0:w, bank + k, 0:2 * D].rearrange("p (b c) -> p b c", b=2)
                for b in range(2):
                    tr(o[:, b, 0:P], x[:, b, P * k:P * k + w])
                last = tr(o[:, :, P:D], x[:, 2, P * k:P * k + w])
            last.then_inc(ps, 1)

        def scores(i, u):
            t = TILE_OF[u // 2]
            if u == 0:
                pe.wait_ge(qk_ready, i * 6 + 6)
            if u == 1:
                pe.wait_ge(max_ready, i * 6 + 1)
            for c in range(3):
                for half in range(2):
                    rows = slice(64 * half, 64 * half + 64)
                    bank, col = 2 * (u % 2) + half, c * S
                    q, k = Q[rows, c, u % 2, :], K[rows, c, :]
                    for at, key, n in ((0, 0, S),) if half == 0 else ((0, P, NIMG), (NIMG, 0, NTXT)):
                        if t < 2:
                            last = mm(PS[:, bank, col + at:col + at + n], q[:, D * t:D * t + P], k[:, D * t + key:D * t + key + n])
                        else:
                            for b in range(2):
                                last = mm(PS[64 * b:64 * b + 64, bank, col + at:col + at + n], q[:, D * b + P:D * b + D],
                                          k[:, D * b + key:D * b + key + n])
            last.then_inc(score_ps, 1)

        def transpose_probs(i, u, cs=range(3)):
            for c in cs:
                g = 3 * u + c
                if c == 0:
                    pe.wait_ge(prob_ready, i * 6 + u + 1)
                if g >= 2:
                    if g % 2:
                        pe.wait_ge(probT_act_ready, i * 9 + g // 2)
                    else:
                        pe.wait_ge(probT_dve_ready, i * 9 + g // 2)
                for slot, col in enumerate((0, PXW - NTXT, NTXT)):
                    last = tr(PS[:, 4 + g % 2, P * slot:P * slot + P], PX[:, u % 2, c, col:col + P])
                last.then_inc(probT_ps, 1)

        def patches_T(j, core):
            pe.wait_ge(xn_ready, j + 1)
            if core:
                pe.wait_ge(v_ready, j)
            for k in range(KP):
                last = tr(PS[:, 6 + k // 4, P * (k % 4):P * (k % 4) + P], XN[:, P * k:P * k + P])
            last.then_inc(xnT_ps, 1)

        def patch_tokens(j):
            pe.wait_ge(xnT_ready, j + 1)
            for k in range(KP):
                last = mm(PS[:, 6, 0:D], XNT[:, k, :], wlin[:, k, :], k == 0, k == KP - 1)
            last.then_inc(tok_ps, 1)

        def tokens_T(j):
            pe.wait_ge(xa_ready, j + 1)
            transpose_set(XA, 6, KA, xaT_ps)

        def lin_gram(j):
            pe.wait_ge(xaT_ready, j + 1)
            for b in range(2):
                for m in range(2):
                    o = PS[0:KA[m], 6 + b, m * DA:(m + 1) * DA]
                    mm(o, XA[:, b, P * m:P * m + KA[m]], XA[:, b, :], True, False)
                    last = mm(o, XA[64 * b:64 * b + NIMG, 2, P * m:P * m + KA[m]], XA[64 * b:64 * b + NIMG, 2, :], False, True)
                last.then_inc(lin_mat_ps, 1)

        def lin_product(j, step):
            for b in range(2):
                pe.wait_ge(lin_mat_ready, j * 6 + 2 * step + b + 1)
                for m in range(2):
                    for k in range(2):
                        l = (GS[0:KA[k], b, k, P * m:P * m + KA[m]], AT[0:KA[k], k, P * m:P * m + KA[m]])[step]
                        r = (wva[0:KA[k], k, :], T1[0:KA[k], b, k, :])[step]
                        last = mm(PS[0:KA[m], 6 + b, m * D:(m + 1) * D], l, r, k == 0, k == 1)
                last.then_inc(lin_mat_ps, 1)

        def lin_tokens(j):
            for b in range(2):
                pe.wait_ge(lin_mat_ready, j * 6 + 5 + b)
                for k in range(2):
                    mm(PS[:, 6, b * D:(b + 1) * D], XAT[0:KA[k], k, b, 0:P], PM[0:KA[k], b, k, :], k == 0, k == 1)
            for b in range(2):
                for k in range(2):
                    last = mm(PS[64 * b:64 * b + 64, 7, 0:D], XAT[0:KA[k], k, b, P:D], PM[0:KA[k], b, k, :], k == 0, k == 1)
            last.then_inc(lin_ps, 1)

        def z_T(j):
            pe.wait_ge(z_ready, j + 1)
            transpose_set(Z, 6, KD, zT_ps)

        def split_product(o, ws, zs, weights_stay, first_of=None):
            parts = ((ws[:, 0], ZH[:, zs]), (ws[:, 1], ZH[:, zs]), (ws[:, 0], ZL[:, zs]), (ws[:, 2], ZS[:, zs]),
                     (ws[0:64, 3], ZS[0:64, zs]))
            for n, (w, z) in enumerate(parts):
                if n == 2 and first_of is not None:
                    pe.wait_ge(zT_ready, first_of + 1)
                last = mm(o, *((w, z) if weights_stay else (z, w)), n == 0, n == 4)
            return last

        def queries_keys(j, ms):
            for m in ms:
                if m == 0:
                    pe.wait_ge(zT_high, j + 1)
                if m >= 3:
                    pe.wait_ge(qk_ready, j * 6 + m - 1)
                split_product(PS[:, qk_bank(m), 0:2 * D], wqkr[:, :, m, :], slice(0, 2 * D), True, j if m == 0 else None).then_inc(qk_ps, 1)

        def values(j):
            pe.wait_ge(qk_ready, j * 6 + 6)
            for b in range(2):
                split_product(PS[:, 6, b * D:(b + 1) * D], wvr, slice(D * b, D * b + P), False)
                last = split_product(PS[0:64, 7, b * D:(b + 1) * D], wvr, slice(D * b + P, D * b + D), False)
            last.then_inc(v_ps, 1)

        def contexts_T(i, b):
            if b == 0:
                pe.wait_ge(v_ready, i + 1)
                pe.wait_ge(probT_act_ready, i * 9 + 6)
                pe.wait_ge(probT_dve_ready, i * 9 + 6)
            for c in range(3):
                if b == 1 and c < 2:
                    pe.wait_ge(probT_dve_ready, i * 9 + (7, 9)[c])
                if b == 1 and c != 1:
                    pe.wait_ge(probT_act_ready, i * 9 + (8, 0, 9)[c])
                bank, col = (2 * b, c * D) if c < 2 else (1, b * D)
                for k in range(2):
                    for j in range(4):
                        half, r = j // 2, j % 2
                        rows = slice(0, P) if k == 0 else slice(64 * half, 64 * half + NIMG)
                        last = mm(PS[32 * j:32 * j + 32, bank, col:col + D], VX[rows, k, b, 4 * c + j, :],
                                  PT[rows, 3 * r + c, half if k == 0 else 2, D * b:D * b + D], k == 0, k == 1)
            last.then_inc(ctxT_ps, 1)

        def contexts(i):
            pe.wait_ge(ctxT_ready, i * 2 + 2)
            pe.wait_ge(ctxT2_ready, i + 1)
            for t in range(3):
                for c in range(3):
                    last = tr(PS[:, 3 + t, P * c:P * c + P], CT[:, c, P * t:P * t + P])
                last.then_inc(ctx_ps, 1)

        def normed_T(i):
            for t in range(3):
                pe.wait_ge(ctx_ready, i * 3 + t + 1)
                for k in range(2):
                    last = tr(PS[0:KD[k], k, P * t:P * t + P], CN[:, t, P * k:P * k + KD[k]])
            last.then_inc(cnT_ps, 1)

        def project(i):
            pe.wait_ge(cnT_ready, i + 1)
            for t in range(3):
                o = PS[:, 2, t * D:(t + 1) * D] if t < 2 else PS[:, 3, 0:D]
                for k in range(2):
                    last = mm(o, CNT[0:KD[k], k, P * t:P * t + P], ow[0:KD[k], k, :], k == 0, k == 1)
            last.then_inc(proj_ps, 1)

        def body(i, j):
            core, pre = i is not None, j is not None
            core and scores(i, 0)
            core and values(i)
            core and scores(i, 1)
            pre and patches_T(j, core)
            core and transpose_probs(i, 0, (0, 1))
            core and scores(i, 2)
            core and transpose_probs(i, 0, (2,))
            pre and patch_tokens(j)
            core and transpose_probs(i, 1, (0, 1))
            core and scores(i, 3)
            core and transpose_probs(i, 1, (2,))
            core and transpose_probs(i, 2, (0, 1))
            core and scores(i, 4)
            core and transpose_probs(i, 2, (2,))
            pre and tokens_T(j)
            core and transpose_probs(i, 3, (0, 1))
            core and transpose_probs(i, 3, (2,))
            pre and lin_gram(j)
            pre and lin_product(j, 0)
            pre and lin_product(j, 1)
            pre and lin_tokens(j)
            core and scores(i, 5)
            core and transpose_probs(i, 4)
            core and contexts_T(i, 0)
            core and transpose_probs(i, 5)
            core and contexts_T(i, 1)
            pre and z_T(j)
            core and contexts(i)
            pre and queries_keys(j, (0, 1))
            core and normed_T(i)
            pre and queries_keys(j, (2, 3, 4, 5))
            core and project(i)

        body(None, 0)
        with pe.Fori(0, PAIRS - 1) as i:
            body(i, i + 1)
        body(PAIRS - 1, None)

        def transpose_group(x, ps):
            for t in range(TG):
                for k in range(2):
                    last = tr(PS[0:KD[k], k, TB * t:TB * t + TB], x[:, t, P * k:P * k + KD[k]], TB)
            last.then_inc(ps, 1)

        def up(base, slot, ms=range(KH)):
            which = int(slot > 0)
            xh, xl, xs = XH[:, which, :], XL[:, which, :], XS[:, which, :]
            for m in ms:
                o = PS[:, 2 + m % 2, 0:GT]
                w = w1r[:, slot, :, P * m:P * m + P]
                pe.wait_ge(gelu_ready, base + m + 1)
                mm(o, w[:, 0, :], xh, True, False)
                mm(o, w[:, 0, :], xl, False, False)
                mm(o, w[:, 1, :], xh, False, False)
                mm(o, w[:, 2, :], xs, False, False)
                mm(o, w[0:64, 3, :], xs[0:64, :], False, True).then_inc(up_ps, 1)

        def down(base, up_base, slot, at):
            for t in range(TG):
                bank = PS[0:TB, 4 + t, :]
                if t == 0:
                    pe.wait_ge(hid_ready, up_base + KH + 3)
                pe.wait_ge(down_read, base + t + 1)
                for k in range(KH):
                    mm(bank[:, 0:2 * D], GH[:, at, k, TB * t:TB * t + TB], w2r[:, slot, k, :], k == 0, False)
                    mm(bank[:, 0:D], GL[:, at, k, TB * t:TB * t + TB], w2r[:, slot, k, 0:D], False, False)
                mm(bank[:, 0:D], ones33[:, :], b2r[:, slot, :], False, True).then_inc(down_ps, 1)

        def gate(n):
            pe.wait_ge(actT_ready, n * 2 + 2)
            for t in range(TG):
                o = PS[0:TB, 0, GT + NE * t:GT + NE * t + NE]
                cols = slice(TB * t, TB * t + TB)
                mm(o, XH[:, 1, cols], gwr[:, 0, :], True, False)
                mm(o, XL[:, 1, cols], gwr[:, 0, :], False, False)
                mm(o, XH[:, 1, cols], gwr[:, 1, :], False, False)
                mm(o, XS[:, 1, cols], gwr[:, 2, :], False, False)
                last = mm(o, XS[0:64, 1, cols], gwr[0:64, 3, :], False, True)
            last.then_inc(gate_ps, 1)

        def group(n, more):
            seq = order(more)
            up_base = lambda slot: n * UPS + KH + seq.index(slot) * KH
            down_base = lambda slot: n * DOWNS + TG + seq.index(slot) * TG
            gate(n)
            up(up_base(1), 1, HALF[0])
            if more:
                pe.wait_ge(x_in, n * 16 + 32)
                pe.wait_ge(ldiff_ready, n + 1)
                transpose_group(X, actT_ps)
            up(up_base(1), 1, HALF[1])
            for before, slot in zip(seq, seq[1:]):
                if more and slot == 0:
                    pe.wait_ge(actT_ready, n * 2 + 3)
                up(up_base(slot), slot)
                if more and slot == NF - 1:
                    pe.wait_ge(z2_ready, n + 2)
                    transpose_group(Z2, actT_ps)
                down(down_base(before), up_base(before), before, place(before, more))
            down(down_base(NF - 1), up_base(NF - 1), NF - 1, place(NF - 1, more))

        pe.wait_ge(phase_done, 3)
        pe.wait_ge(x_in, 16)
        transpose_group(X, actT_ps)
        pe.wait_ge(w1lo_ready, NF)
        pe.wait_ge(w2lo_ready, NF)
        pe.wait_ge(out_stored, 1)
        pe.wait_ge(actT_ready, 1)
        up(0, 0)
        down(0, 0, 0, 0)
        pe.wait_ge(z2_ready, 1)
        transpose_group(Z2, actT_ps)
        with pe.Fori(0, GROUPS - 1) as n:
            group(n, True)
        group(GROUPS - 1, False)

    ctx.close()


_RENAMED = {
    "txt": "txt", "lnp_g": "L0_tok_ln1_g", "lnp_b": "L0_tok_ln1_b", "W_lin": "L0_tok_W_lin", "b_lin": "L0_tok_b_lin",
    "ln2_g": "L0_tok_ln2_g", "ln2_b": "L0_tok_ln2_b", "pos": "L0_tok_pos_embedding", "cls": "L0_tok_cls_token",
    "Wq": "L0_attn_Wq", "bq": "L0_attn_bq", "Wk": "L0_attn_Wk", "bk": "L0_attn_bk", "bv": "L0_attn_bv",
    "f1_g": "L0_ffn_ln1_g", "f1_b": "L0_ffn_ln1_b", "in_b": "L0_ffn_in_b", "out_b": "L0_ffn_out_b",
    "mlp_w1": "L0_ffn_mlp_w1", "mlp_b1": "L0_ffn_mlp_b1", "mlp_w2": "L0_ffn_mlp_w2", "mlp_b2": "L0_ffn_mlp_b2",
    "f2_g": "L0_ffn_ln2_g", "f2_b": "L0_ffn_ln2_b", "gate_b": "L0_ffn_gate_b",
    "exp_w1": "L0_ffn_exp_w1", "exp_b1": "L0_ffn_exp_b1", "exp_w2": "L0_ffn_exp_w2", "exp_b2": "L0_ffn_exp_b2",
}
_TRANSPOSED = {"WvT": "L0_attn_Wv", "in_wT": "L0_ffn_in_w", "out_wT": "L0_ffn_out_w", "gate_wT": "L0_ffn_gate_w"}


def attention_constants(np_, v):
    f = np_.zeros
    c = {name: f((128,) + shape, np_.float32) for name, shape in SETUP_COLS + CONST_COLS}
    c["wlin"][:] = v["W_lin"].reshape(KP, 128, D).transpose(1, 0, 2)
    c["lnp_g"][:], c["lnp_b"][:] = v["lnp_g"], v["lnp_b"]
    for name, source in (("lin_bias", v["b_lin"]), ("vb", v["in_b"][2 * D:3 * D]), ("ob", v["out_b"])):
        c[name][:] = source
    for b in range(2):
        c["g2m"][64 * b + 1:64 * b + NIMG] = v["ln2_g"]
        c["b2m"][64 * b:64 * b + NIMG] = v["pos"][0, 0:NIMG]
        c["clsb"][64 * b + 1:64 * b + NIMG] = v["ln2_b"]
        c["clsb"][64 * b] = v["cls"].reshape(-1)
    for k in range(2):
        rows, n = slice(128 * k, 128 * k + KD[k]), KD[k]
        for name, w, bias in (("wqa", "Wq", "bq"), ("wka", "Wk", "bk")):
            c[name][0:n, k, 0:D], c[name][0:n, k, D] = v[w][rows], v[bias][rows]
        c["wva"][0:n, k] = v["WvT"][rows]
        for at in range(0, 128, n):
            to = slice(at, at + n)
            c["wv"][to, k] = v["in_wT"][rows, 2 * D:3 * D]
            c["fg"][to, k], c["fb"][to, k] = v["f1_g"][rows], v["f1_b"][rows]
            for which in range(2):
                c["wqk"][to, k, which::2, :, 0:HD] = v["in_wT"][rows, which * D:(which + 1) * D].reshape(n, 3, 4, HD)
    c["wva"][64, 1] = v["bv"]
    for j in range(4):
        c["qkb"][32 * j:32 * j + HD] = v["qk_b"][j]
    return [np_.ascontiguousarray(np_.concatenate([c[name].reshape(128, -1) for name, _ in cols], axis=1))
            for cols in (SETUP_COLS, CONST_COLS)]


def kernel(**inputs):
    import numpy as _np
    import concourse.bacc as _bacc
    from concourse import mybir as _mybir
    from concourse.bass_utils import run_bass_kernel_spmd as _run

    nc = _bacc.Bacc("TRN2", target_bir_lowering=False, num_devices=1)
    laid = {name: _np.ascontiguousarray(inputs[source]) for name, source in _RENAMED.items()}
    laid |= {name: _np.ascontiguousarray(_np.asarray(inputs[source]).T) for name, source in _TRANSPOSED.items()}
    for name in ("lnp_g", "lnp_b", "mlp_b1"):
        laid[name] = _np.ascontiguousarray(laid[name].reshape(-1, 128).T)
    laid["exp_b1"] = _np.ascontiguousarray(laid["exp_b1"].reshape(4, -1, 128).transpose(2, 0, 1))
    laid["qk_b"] = _np.ascontiguousarray(laid["in_b"][0:384].reshape(2, 3, 4, 16).transpose(2, 3, 1, 0)).reshape(4, 16, 6)
    x = _np.asarray(inputs["x"]).reshape(32, 3, 6, 16, 6, 16)
    laid["patches"] = _np.ascontiguousarray(x.transpose(0, 2, 4, 3, 5, 1)).reshape(32, 36, 768)
    laid["setup_const"], laid["attn_const"] = attention_constants(_np, laid)
    for name in ("lnp_g", "lnp_b", "W_lin", "b_lin", "ln2_g", "ln2_b", "pos", "cls", "Wq", "bq", "Wk", "bk", "bv", "f1_g", "f1_b",
                 "in_b", "out_b", "WvT", "in_wT", "qk_b"):
        del laid[name]
    arrays, args = {}, {}
    for name, v in laid.items():
        arrays[f"in_{name}"] = v
        args[name] = nc.dram_tensor(f"in_{name}", v.shape, _mybir.dt.from_np(v.dtype), kind="ExternalInput").ap()
    out = nc.dram_tensor("out", (32, 165, 192), _mybir.dt.from_np(_np.dtype("float32")), kind="ExternalOutput").ap()
    build_program(nc, args, out)
    r = _run(nc, [arrays], core_ids=[0])
    return r.results[0]["out"]
```
